# Optimizing a Trainium2 kernel written in Bass

```python
import numpy as np
import jax
import jax.numpy as jnp

def _softmax(x, axis=-1):
    return jax.nn.softmax(x, axis=axis)

def _gelu(x):
    return jax.nn.gelu(x, approximate=True)

def _silu(x):
    return jax.nn.silu(x)

def _sigmoid(x):
    return jax.nn.sigmoid(x)

def _layernorm(x, axis=-1, eps=1e-05):
    m = jnp.mean(x, axis=axis, keepdims=True)
    v = jnp.var(x, axis=axis, keepdims=True)
    return (x - m) / jnp.sqrt(v + eps)

def _scatter_add(tgt, idx, src, axis=0):
    return tgt.at[idx].add(src)

def _segment_sum(src, seg, n):
    return jax.ops.segment_sum(src, seg, n)
kernel_name = 'mk_gnn_resnorm_d4_gnn_r16_048ff0'

def setup_inputs(seed: int=0):
    np.random.seed(seed)
    _w = jnp.asarray

    def _rec_inputs():
        import jax
        import jax.numpy as jnp
        _gk = jax.random.key(seed)
        x = -0.0002117 + 1 * jax.random.normal(jax.random.fold_in(_gk, 1), (6250, 256), jnp.float32)
        _s = jax.random.randint(jax.random.fold_in(_gk, 2), (50000,), 0, 6250, jnp.int32)
        _d = jax.random.randint(jax.random.fold_in(_gk, 3), (50000,), 0, 6250, jnp.int32)
        _loop = jnp.arange(6250, dtype=jnp.int32)
        src = jnp.concatenate([_s, _d, _loop])
        dst = jnp.concatenate([_d, _s, _loop])
        _o = jnp.argsort(dst, stable=True)
        src = src[_o]
        dst = dst[_o]
        edge_weight = jax.random.uniform(jax.random.fold_in(_gk, 14), (106250,), jnp.float32, 0.0, 1)
        edge_weight1 = jax.random.uniform(jax.random.fold_in(_gk, 15), (106250, 1), jnp.float32, 0.0, 1)
        return (x, src, dst, edge_weight, edge_weight1)
    x, src, dst, edge_weight, edge_weight1 = _rec_inputs()

    def _L0_gnn_setup():
        import jax, jax.numpy as jnp
        import numpy as np
        BN_EPS = 1e-05
        IDX = np.array([[0, 1, 2, 3, 4, 5, 6, 7], [1, 0, 3, 2, 5, 4, 7, 6], [2, 3, 0, 1, 6, 7, 4, 5], [3, 2, 1, 0, 7, 6, 5, 4], [4, 5, 6, 7, 0, 1, 2, 3], [5, 4, 7, 6, 1, 0, 3, 2], [6, 7, 4, 5, 2, 3, 0, 1], [7, 6, 5, 4, 3, 2, 1, 0]], dtype=np.int32)
        SIGN = np.array([[1, 1, 1, 1, 1, 1, 1, 1], [1, -1, 1, -1, 1, -1, -1, 1], [1, -1, -1, 1, 1, 1, -1, -1], [1, 1, -1, -1, 1, -1, 1, -1], [1, -1, -1, -1, -1, 1, 1, 1], [1, 1, -1, 1, -1, -1, -1, 1], [1, 1, 1, -1, -1, 1, -1, -1], [1, -1, 1, 1, -1, -1, 1, -1]], dtype=np.float32)

        def make_octonion_mul(kernel):
            in8, out = kernel.shape
            out8 = out // 8
            a = kernel.reshape(in8, 8, out8).transpose(1, 0, 2)
            blocks = jnp.asarray(SIGN)[:, :, None, None] * a[jnp.asarray(IDX)]
            return jnp.transpose(blocks, (1, 2, 0, 3)).reshape(8 * in8, out)
        key = jax.random.key(seed)
        ks = jax.random.split(key, 5)
        N, E, D_IN, D_OUT = (6250, 200000, 256, 256)
        stdv = float(np.sqrt(6.0 / (D_IN // 8 + D_OUT)))
        return {'x': jax.random.normal(ks[0], (N, D_IN), dtype=jnp.float32), 'weight': jax.random.uniform(ks[1], (D_IN // 8, D_OUT), dtype=jnp.float32, minval=-stdv, maxval=stdv), 'gamma': jnp.ones((D_OUT,), dtype=jnp.float32), 'beta': jnp.zeros((D_OUT,), dtype=jnp.float32), 'edge_weight': jax.random.uniform(ks[2], (E,), dtype=jnp.float32), 'edge_src': jax.random.randint(ks[3], (E,), 0, N, dtype=jnp.int32), 'edge_dst': jax.random.randint(ks[4], (E,), 0, N, dtype=jnp.int32)}
    _L0_gnn_all = _L0_gnn_setup()
    _L0_gnn_in = {k: v for k, v in _L0_gnn_all.items() if k in ('weight', 'gamma', 'beta')}
    del _L0_gnn_all

    def _L1_gnn_setup():
        import jax, jax.numpy as jnp
        import numpy as np
        BS = 512
        EMBED = 256
        NHEAD = 8
        HDIM = EMBED // NHEAD
        E = BS * BS

        def _xavier(key, shape):
            lim = float(np.sqrt(6.0 / (shape[0] + shape[1])))
            return jax.random.uniform(key, shape, jnp.float32, -lim, lim)
        key = jax.random.key(seed)
        ks = jax.random.split(key, 6)
        feats = jax.random.normal(ks[0], (BS, EMBED), jnp.float32)
        dst = jnp.repeat(jnp.arange(BS), BS)
        src = jnp.tile(jnp.arange(BS), BS)
        edge_index = jnp.stack([src, dst], axis=1).astype(jnp.int32)
        edge_attr = jnp.zeros((E, 1), jnp.float32)
        return {'feats': feats, 'edge_index': edge_index, 'edge_attr': edge_attr, 'Wq': _xavier(ks[1], (EMBED, EMBED)), 'bq': jnp.zeros((EMBED,), jnp.float32), 'Wk': _xavier(ks[2], (EMBED, EMBED)), 'bk': jnp.zeros((EMBED,), jnp.float32), 'Wv': _xavier(ks[3], (EMBED, EMBED)), 'bv': jnp.zeros((EMBED,), jnp.float32), 'Wo': _xavier(ks[4], (EMBED, EMBED)), 'bo': jnp.zeros((EMBED,), jnp.float32)}
    _L1_gnn_all = _L1_gnn_setup()
    _L1_gnn_in = {k: v for k, v in _L1_gnn_all.items() if k in ('Wq', 'bq', 'Wk', 'bk', 'Wv', 'bv', 'Wo', 'bo')}
    del _L1_gnn_all

    def _L2_gnn_setup():
        import jax, jax.numpy as jnp
        import numpy as np
        N = 1250
        E = 20000
        D_IN = 256
        HID = 64
        HEADS = 4
        D_OUT = 256
        EPS = 1e-05
        SLOPE = 0.2

        def _gat(x, src, dst, W, a_src, a_dst, b, heads, ch, concat):
            n = x.shape[0]
            h = (x @ W).reshape(n, heads, ch)
            es = (h * a_src).sum(-1)
            ed = (h * a_dst).sum(-1)
            e = jax.nn.leaky_relu(es[src] + ed[dst], SLOPE)
            m = jax.ops.segment_max(e, dst, num_segments=n)
            w = jnp.exp(e - m[dst])
            den = jax.ops.segment_sum(w, dst, num_segments=n)
            alpha = w / den[dst]
            msg = h[src] * alpha[:, :, None]
            out = jax.ops.segment_sum(msg, dst, num_segments=n)
            out = out.reshape(n, heads * ch) if concat else out.mean(axis=1)
            return out + b

        def _layernorm(x, g, b):
            mu = x.mean(-1, keepdims=True)
            v = ((x - mu) ** 2).mean(-1, keepdims=True)
            return (x - mu) * jax.lax.rsqrt(v + EPS) * g + b
        key = jax.random.key(seed)
        ks = jax.random.split(key, 10)

        def glorot(k, shape):
            fan_in, fan_out = (shape[0], int(np.prod(shape[1:])))
            s = np.sqrt(2.0 / (fan_in + fan_out)).astype(np.float32)
            return jax.random.normal(k, shape, dtype=jnp.float32) * s
        x = jax.random.normal(ks[0], (N, D_IN), dtype=jnp.float32)
        edge_index = jax.random.randint(ks[1], (2, E), 0, N, dtype=jnp.int64)
        return {'x': x, 'edge_index': edge_index, 'W1': glorot(ks[2], (D_IN, HEADS * HID)), 'a1_src': glorot(ks[3], (HEADS, HID)), 'a1_dst': glorot(ks[4], (HEADS, HID)), 'b1': jnp.zeros((HEADS * HID,), jnp.float32), 'ln_g': jnp.ones((HEADS * HID,), jnp.float32), 'ln_b': jnp.zeros((HEADS * HID,), jnp.float32), 'W2': glorot(ks[5], (HEADS * HID, D_OUT)), 'a2_src': glorot(ks[6], (1, D_OUT)), 'a2_dst': glorot(ks[7], (1, D_OUT)), 'b2': jnp.zeros((D_OUT,), jnp.float32)}
    _L2_gnn_all = _L2_gnn_setup()
    _L2_gnn_in = {k: v for k, v in _L2_gnn_all.items() if k in ('W1', 'a1_src', 'a1_dst', 'b1', 'ln_g', 'ln_b', 'W2', 'a2_src', 'a2_dst', 'b2')}
    del _L2_gnn_all

    def _L3_gnn_setup():
        import jax, jax.numpy as jnp
        import numpy as np
        N_NODES = 6250
        N_EDGES = 18750
        D = 256
        BN_EPS = 1e-05
        key = jax.random.key(seed)
        k1, k2, k3, k4 = jax.random.split(key, 4)
        x = jax.random.normal(k1, (N_NODES, D), dtype=jnp.float32)
        edge_index = jax.random.randint(k2, (2, N_EDGES), 0, N_NODES, dtype=jnp.int64)
        W = jax.random.normal(k3, (D, D), dtype=jnp.float32) / np.sqrt(D)
        b = jax.random.normal(k4, (D,), dtype=jnp.float32) * 0.01
        gamma = jnp.ones((D,), dtype=jnp.float32)
        beta = jnp.zeros((D,), dtype=jnp.float32)
        return {'x': x, 'edge_index': edge_index, 'W': W, 'b': b, 'gamma': gamma, 'beta': beta}
    _L3_gnn_all = _L3_gnn_setup()
    _L3_gnn_in = {k: v for k, v in _L3_gnn_all.items() if k in ('W', 'b', 'gamma', 'beta')}
    del _L3_gnn_all
    return {'x': x, 'src': src, 'dst': dst, 'edge_weight': edge_weight, 'edge_weight1': edge_weight1, 'L0_gnn_weight': _L0_gnn_in['weight'], 'L0_gnn_gamma': _L0_gnn_in['gamma'], 'L0_gnn_beta': _L0_gnn_in['beta'], 'L1_gnn_Wq': _L1_gnn_in['Wq'], 'L1_gnn_bq': _L1_gnn_in['bq'], 'L1_gnn_Wk': _L1_gnn_in['Wk'], 'L1_gnn_bk': _L1_gnn_in['bk'], 'L1_gnn_Wv': _L1_gnn_in['Wv'], 'L1_gnn_bv': _L1_gnn_in['bv'], 'L1_gnn_Wo': _L1_gnn_in['Wo'], 'L1_gnn_bo': _L1_gnn_in['bo'], 'L2_gnn_W1': _L2_gnn_in['W1'], 'L2_gnn_a1_src': _L2_gnn_in['a1_src'], 'L2_gnn_a1_dst': _L2_gnn_in['a1_dst'], 'L2_gnn_b1': _L2_gnn_in['b1'], 'L2_gnn_ln_g': _L2_gnn_in['ln_g'], 'L2_gnn_ln_b': _L2_gnn_in['ln_b'], 'L2_gnn_W2': _L2_gnn_in['W2'], 'L2_gnn_a2_src': _L2_gnn_in['a2_src'], 'L2_gnn_a2_dst': _L2_gnn_in['a2_dst'], 'L2_gnn_b2': _L2_gnn_in['b2'], 'L3_gnn_W': _L3_gnn_in['W'], 'L3_gnn_b': _L3_gnn_in['b'], 'L3_gnn_gamma': _L3_gnn_in['gamma'], 'L3_gnn_beta': _L3_gnn_in['beta']}

def reference(x, src, dst, edge_weight, edge_weight1, L0_gnn_weight, L0_gnn_gamma, L0_gnn_beta, L1_gnn_Wq, L1_gnn_bq, L1_gnn_Wk, L1_gnn_bk, L1_gnn_Wv, L1_gnn_bv, L1_gnn_Wo, L1_gnn_bo, L2_gnn_W1, L2_gnn_a1_src, L2_gnn_a1_dst, L2_gnn_b1, L2_gnn_ln_g, L2_gnn_ln_b, L2_gnn_W2, L2_gnn_a2_src, L2_gnn_a2_dst, L2_gnn_b2, L3_gnn_W, L3_gnn_b, L3_gnn_gamma, L3_gnn_beta):
    import jax
    import jax.numpy as jnp

    def _L0_gnn_ref(x, weight, gamma, beta, edge_weight, edge_src, edge_dst):
        import jax, jax.numpy as jnp
        import numpy as np
        BN_EPS = 1e-05
        IDX = np.array([[0, 1, 2, 3, 4, 5, 6, 7], [1, 0, 3, 2, 5, 4, 7, 6], [2, 3, 0, 1, 6, 7, 4, 5], [3, 2, 1, 0, 7, 6, 5, 4], [4, 5, 6, 7, 0, 1, 2, 3], [5, 4, 7, 6, 1, 0, 3, 2], [6, 7, 4, 5, 2, 3, 0, 1], [7, 6, 5, 4, 3, 2, 1, 0]], dtype=np.int32)
        SIGN = np.array([[1, 1, 1, 1, 1, 1, 1, 1], [1, -1, 1, -1, 1, -1, -1, 1], [1, -1, -1, 1, 1, 1, -1, -1], [1, 1, -1, -1, 1, -1, 1, -1], [1, -1, -1, -1, -1, 1, 1, 1], [1, 1, -1, 1, -1, -1, -1, 1], [1, 1, 1, -1, -1, 1, -1, -1], [1, -1, 1, 1, -1, -1, 1, -1]], dtype=np.float32)

        def make_octonion_mul(kernel):
            in8, out = kernel.shape
            out8 = out // 8
            a = kernel.reshape(in8, 8, out8).transpose(1, 0, 2)
            blocks = jnp.asarray(SIGN)[:, :, None, None] * a[jnp.asarray(IDX)]
            return jnp.transpose(blocks, (1, 2, 0, 3)).reshape(8 * in8, out)
        N = x.shape[0]
        hamilton = make_octonion_mul(weight)
        support = x @ hamilton
        msgs = edge_weight[:, None] * support[edge_src]
        out = jax.ops.segment_sum(msgs, edge_dst, num_segments=N)
        mean = jnp.mean(out, axis=0)
        var = jnp.var(out, axis=0)
        out = (out - mean) * jax.lax.rsqrt(var + BN_EPS) * gamma + beta
        return jnp.tanh(out)

    def _L1_gnn_ref(feats, edge_index, edge_attr, Wq, bq, Wk, bk, Wv, bv, Wo, bo):
        import jax, jax.numpy as jnp
        import numpy as np
        BS = 512
        EMBED = 256
        NHEAD = 8
        HDIM = EMBED // NHEAD
        E = BS * BS

        def _xavier(key, shape):
            lim = float(np.sqrt(6.0 / (shape[0] + shape[1])))
            return jax.random.uniform(key, shape, jnp.float32, -lim, lim)
        bs = feats.shape[0]
        scale = 1.0 / np.sqrt(HDIM)
        q = (feats @ Wq.T + bq).reshape(bs, NHEAD, HDIM).transpose(1, 0, 2)
        k = (feats @ Wk.T + bk).reshape(bs, NHEAD, HDIM).transpose(1, 0, 2)
        v = (feats @ Wv.T + bv).reshape(bs, NHEAD, HDIM).transpose(1, 0, 2)
        r, c = (edge_index[:, 0], edge_index[:, 1])
        qe = q[:, c, :]
        ke = k[:, r, :]
        ve = v[:, r, :]
        sim = jnp.einsum('hed,hed->eh', qe, ke) * scale
        m = jax.ops.segment_max(sim, c, num_segments=bs)
        p = jnp.exp(sim - m[c])
        s = jax.ops.segment_sum(p, c, num_segments=bs)
        attn = p / s[c]
        out_e = attn.T[..., None] * ve
        out_e = out_e.transpose(1, 0, 2).reshape(-1, NHEAD * HDIM)
        agg = jax.ops.segment_sum(out_e, c, num_segments=bs)
        return agg @ Wo.T + bo

    def _L2_gnn_ref(x, edge_index, W1, a1_src, a1_dst, b1, ln_g, ln_b, W2, a2_src, a2_dst, b2):
        import jax, jax.numpy as jnp
        import numpy as np
        N = 1250
        E = 20000
        D_IN = 256
        HID = 64
        HEADS = 4
        D_OUT = 256
        EPS = 1e-05
        SLOPE = 0.2

        def _gat(x, src, dst, W, a_src, a_dst, b, heads, ch, concat):
            n = x.shape[0]
            h = (x @ W).reshape(n, heads, ch)
            es = (h * a_src).sum(-1)
            ed = (h * a_dst).sum(-1)
            e = jax.nn.leaky_relu(es[src] + ed[dst], SLOPE)
            m = jax.ops.segment_max(e, dst, num_segments=n)
            w = jnp.exp(e - m[dst])
            den = jax.ops.segment_sum(w, dst, num_segments=n)
            alpha = w / den[dst]
            msg = h[src] * alpha[:, :, None]
            out = jax.ops.segment_sum(msg, dst, num_segments=n)
            out = out.reshape(n, heads * ch) if concat else out.mean(axis=1)
            return out + b

        def _layernorm(x, g, b):
            mu = x.mean(-1, keepdims=True)
            v = ((x - mu) ** 2).mean(-1, keepdims=True)
            return (x - mu) * jax.lax.rsqrt(v + EPS) * g + b
        loops = jnp.arange(N, dtype=edge_index.dtype)
        src = jnp.concatenate([edge_index[0], loops])
        dst = jnp.concatenate([edge_index[1], loops])
        h = _gat(x, src, dst, W1, a1_src, a1_dst, b1, HEADS, HID, True)
        h = jax.nn.relu(_layernorm(h, ln_g, ln_b))
        out = _gat(h, src, dst, W2, a2_src, a2_dst, b2, 1, D_OUT, False)
        return out

    def _L3_gnn_ref(x, edge_index, W, b, gamma, beta):
        import jax, jax.numpy as jnp
        import numpy as np
        N_NODES = 6250
        N_EDGES = 18750
        D = 256
        BN_EPS = 1e-05
        N = x.shape[0]
        xw = x @ W.T
        loops = jnp.arange(N, dtype=edge_index.dtype)
        src = jnp.concatenate([edge_index[0], loops])
        dst = jnp.concatenate([edge_index[1], loops])
        ones = jnp.ones(src.shape[0], dtype=xw.dtype)
        deg = jax.ops.segment_sum(ones, dst, num_segments=N)
        dinv = jnp.where(deg > 0, jax.lax.rsqrt(deg), 0.0)
        norm = dinv[src] * dinv[dst]
        msg = xw[src] * norm[:, None]
        out = jax.ops.segment_sum(msg, dst, num_segments=N) + b
        mean = jnp.mean(out, axis=0)
        var = jnp.var(out, axis=0)
        out = (out - mean) * jax.lax.rsqrt(var + BN_EPS) * gamma + beta
        out = jax.nn.relu(out)
        return out + x
    edge_index = jnp.stack([src, dst])
    edge_index_t = jnp.stack([src, dst], axis=1)
    x = _layernorm(x + _L0_gnn_ref(x, L0_gnn_weight, L0_gnn_gamma, L0_gnn_beta, edge_weight, src, dst), axis=-1)
    x = _layernorm(x + _L1_gnn_ref(x, edge_index_t, edge_weight1, L1_gnn_Wq, L1_gnn_bq, L1_gnn_Wk, L1_gnn_bk, L1_gnn_Wv, L1_gnn_bv, L1_gnn_Wo, L1_gnn_bo), axis=-1)
    x = _layernorm(x + _L2_gnn_ref(x, edge_index, L2_gnn_W1, L2_gnn_a1_src, L2_gnn_a1_dst, L2_gnn_b1, L2_gnn_ln_g, L2_gnn_ln_b, L2_gnn_W2, L2_gnn_a2_src, L2_gnn_a2_dst, L2_gnn_b2), axis=-1)
    x = _layernorm(x + _L3_gnn_ref(x, edge_index, L3_gnn_W, L3_gnn_b, L3_gnn_gamma, L3_gnn_beta), axis=-1)
    return x

_drawn_inputs = setup_inputs


def setup_inputs(seed=0):
    import zlib

    import numpy as np

    out = dict(_drawn_inputs(seed))
    spreads = {'L0_gnn_gamma': (1.0, 0.2),
     'L0_gnn_beta': (0.0, 0.1),
     'L1_gnn_bq': (0.0, 0.314),
     'L1_gnn_bk': (0.0, 0.8),
     'L1_gnn_bv': (0.0, 0.1),
     'L1_gnn_bo': (0.0, 0.1),
     'L2_gnn_b1': (0.0, 0.1),
     'L2_gnn_ln_g': (1.0, 0.2),
     'L2_gnn_ln_b': (0.0, 0.1),
     'L2_gnn_b2': (0.0, 0.1),
     'L3_gnn_gamma': (1.0, 0.2),
     'L3_gnn_beta': (0.0, 0.1)}
    factors = {'L3_gnn_b': 8.0}
    for name, (base, spread) in spreads.items():
        noise = np.random.default_rng([zlib.crc32(name.encode()), seed]).standard_normal(out[name].shape)
        drawn = base * np.exp(spread * noise) if base else spread * noise
        out[name] = jnp.asarray(drawn.astype(out[name].dtype))
    for name, factor in factors.items():
        out[name] = (out[name] * factor).astype(out[name].dtype)
    return out
```

```python
import concourse.bass as bass
from concourse import mybir
from contextlib import ExitStack

F32 = mybir.dt.float32
I32 = mybir.dt.int32
ALU = mybir.AluOpType
ACT = mybir.ActivationFunctionType
AX = mybir.AxisListType

N, E, D = 6250, 106250, 256
G = 16
T = 832
NB = T // G
FULL, REST = divmod(E, 128)
NT = 50
NP = NT * 128
CH, NCH = 250, 25
RING_USES = 64 * (NB // 2)
BIG = 1.0e30
EPS = 1e-5
H1, H2 = 8, 4
MKW = 513
LOOPS2 = 1250
LN2 = 0.6931471805599453
OCT_IDX = [[i ^ j for j in range(8)] for i in range(8)]
OCT_SIGN = [[1, 1, 1, 1, 1, 1, 1, 1], [1, -1, 1, -1, 1, -1, -1, 1], [1, -1, -1, 1, 1, 1, -1, -1],
            [1, 1, -1, -1, 1, -1, 1, -1], [1, -1, -1, -1, -1, 1, 1, 1], [1, 1, -1, 1, -1, -1, -1, 1],
            [1, 1, 1, -1, -1, 1, -1, -1], [1, -1, 1, 1, -1, -1, 1, -1]]
WIDTH = [256, 512, 260, 257, 256]
HEADS = [0, H1, H2, 1, 0]
PLANES = [2, 3, 3, 3, 2]
ds = bass.ds


def past(L):
    return NB * (L - 1)


def wait(eng, sem, value):
    if isinstance(value, int) and value <= 0:
        return
    eng.wait_ge(sem, value)


def gate(eng, sem, value):
    wait(eng, sem, value)
    eng.nop(nofuse=True)


def gnn_kernel(nc, a, out):
    ctx = ExitStack()
    with ctx:
        def sb(name, shape, dt=F32):
            return ctx.enter_context(nc.sbuf_tensor(name, shape, dt))

        def sem(name):
            return ctx.enter_context(nc.semaphore(name))

        def dram(name, shape, dt=F32):
            return nc.dram_tensor(name, shape, dt).ap()

        x0 = dram("x0", (NP, D))
        x1 = dram("x1", (NP, D))
        x2 = dram("x2", (NP, D))
        x3 = dram("x3", (NP, D))
        kv_t = dram("kv_t", (NP, 512))
        q_t = dram("q_t", (NP, D))
        g1_t = dram("g1_t", (NP, 260))
        ed1_t = dram("ed1_t", (NP, 4))
        g2_t = dram("g2_t", (NP, 257))
        ed2_t = dram("ed2_t", (NP, 1))
        xs_t = dram("xs_t", (NP, D))
        deg_d = dram("deg_d", (NP,))
        dinv_d = dram("dinv_d", (NP,))
        mk1 = dram("mk1", (T, MKW))
        mk4 = dram("mk4", (NB, 4, G, MKW))
        mk8 = dram("mk8", (NB, 8, G, MKW))
        table = [a["x"], kv_t, g1_t, g2_t, xs_t]

        acc = sb("acc", [128, 3, NP])
        ring = sb("ring", [128, 32, 512])
        rflat = ring[:, :, :].rearrange("p s w -> p (s w)")
        oh = sb("oh", [128, 2, G, 128])
        oht = sb("oht", [128, 2, 4, 128])
        qw = sb("qw", [128, 4, 256])
        prod = sb("prod", [128, 2, 2, 256])
        src_c = sb("src_c", [128, T + G], I32)
        rel_c = sb("rel_c", [128, T + G])
        ew_c = sb("ew_c", [128, T + G])
        base_r = sb("base_r", [1, T], I32)
        cneg_r = sb("cneg_r", [1, T])
        sneg_r = sb("sneg_r", [1, T])
        stage = sb("stage", [128, 4, G], I32)
        mk = sb("mk", [128, 2, MKW])
        sc = sb("sc", [128, 2, 128])
        fw = sb("fw", [128, 128])
        mx = sb("mx", [128, 128])
        m2 = sb("m2", [128, 128])
        dd = sb("dd", [128, 128])
        px = sb("px", [128, 128])
        w8 = sb("w8", [128, 2, G, 8])
        edw = sb("edw", [128, 2, G, 4])
        corr = sb("corr", [128, 2, 4])
        cl = sb("cl", [128, 4])
        ident = sb("ident", [128, 128])
        iota = sb("iota", [128, 128])
        ones = sb("ones", [128, 128])
        zeros = sb("zeros", [128, 128])
        selc8 = sb("selc8", [128, 384])
        selc4 = sb("selc4", [128, 384])
        seld8 = sb("seld8", [128, 256])
        seld4 = sb("seld4", [128, 256])
        degm = sb("degm", [1, 128])
        rows = sb("rows", [1, 7, 132])
        fprev = sb("fprev", [1, 8])
        bn = sb("bn", [128, 2, 4])
        lnst = sb("lnst", [128, 2, 12])
        cols = sb("cols", [128, 2, 4])
        dcol = sb("dcol", [128, NT])
        banks = [ctx.enter_context(nc.psum_tensor(f"bank{k}", [128, 512], F32)) for k in range(8)]
        ag, ot, qe, m0, m1 = banks[0:2], banks[2:4], banks[4:6], banks[6], banks[7]
        selc = {H1: selc8, H2: selc4}
        seld = {H1: seld8, H2: seld4}

        at = [0]

        def view(*shape, dt=F32):
            size = 1
            for s in shape:
                size *= s
            v = rflat[:, at[0]:at[0] + size]
            at[0] += size
            assert at[0] <= 32 * 512
            if dt is not F32:
                v = v.bitcast(dt)
            if len(shape) == 2:
                v = v.rearrange("p (u v) -> p u v", u=shape[0])
            if len(shape) == 3:
                v = v.rearrange("p (u v w) -> p u v w", u=shape[0], v=shape[1])
            return v

        raw_i = view(7, 128, dt=I32)
        raw_f = view(7, 128)
        relr = view(7, 128)
        ewr = view(7, 128)
        mkr = view(7, MKW)
        last_r = view(T, dt=I32)
        raw_d = view(7, 128, dt=I32)
        zrow = view(256)
        raw_n = view(7, 128, dt=I32)
        lt = view(7, 128)
        at[0] = 0
        wraw = view(8, 256)
        wout = view(2, 256)
        pre = view(2, 256)
        xr = view(2, 256)
        xn = view(2, 256)
        rr = view(2, 256)
        stats = view(2, NCH * 6)
        shared = at[0]
        dinv_b = view(NP)
        at[0] = shared
        wproj = view(2, 768)
        xt = view(2, 256)
        po = view(2, 768)
        brow = view(768)
        bo_b = view(256)
        lg_b = view(256)
        lb_b = view(256)
        as_b = view(256)
        ad_b = view(256)
        wtmp = view(256)
        dvt = view(2, 256)
        xs = view(2, 256)

        bar = sem("bar")
        s_ring = [sem(f"ring_ready{k}") for k in range(8)]
        s_const = sem("const_ready")
        s_prep_dma = sem("prep_loaded")
        s_base = sem("base_loaded")
        s_rowsdma = sem("lasts_loaded")
        s_prep = sem("prep_rows")
        s_prep_t = sem("prep_transposed")
        s_prep_c = sem("prep_copied")
        s_mkst = sem("masks_stored")
        s_x0 = sem("x0_stored")
        PASS = []
        for L in range(5):
            p = {k: sem(f"{k}{L}") for k in ("staged", "agg", "added", "wready")}
            if L == 1:
                p.update({k: sem(f"{k}{L}") for k in (
                    "oh", "oht", "ohtc", "s", "st", "ch1", "row", "ch2", "col", "ch3", "px", "pb", "w",
                    "mk0", "mk1", "qe", "prod", "red", "qw0", "qw1", "qw2", "qw3")})
            if L == 2:
                p.update({k: sem(f"{k}{L}") for k in ("qeg", "z", "ed0", "ed1")})
            if L in (2, 3):
                p = {**PASS[L - 1], **p}
            PASS.append(p)
        NODE = []
        for P in range(5):
            names = ["wl", "w", "pre", "y", "var", "std", "xn"]
            names += ["wt", "wc"] if P in (0, 1, 4) else []
            names += ["xt", "xtc", "pj", "po", "ps0", "ps1"] if P < 3 else []
            names += ["xt", "xtc", "ps0", "ps1"] if P == 3 else []
            names += ["xr0", "xr1", "st0", "st1"] if P != 2 else []
            names += ["den", "clr"] if P in (1, 2) else []
            names += ["ch", "chd"] if P in (0, 4) else []
            NODE.append({k: sem(f"n_{k}{P}") for k in names})
        s_deg = sem("deg_moved")
        s_sq = sem("to_square_root")
        s_sqd = sem("square_root_taken")

        block = ctx.enter_context(nc.Block())
        nbar = {}

        def barrier(eng):
            k = nbar.get(id(eng), 0) + 1
            nbar[id(eng)] = k
            eng.drain()
            eng.sem_inc(bar, 1)
            eng.wait_ge(bar, 5 * k)
            eng.nop(nofuse=True)

        def softmax_batches(eng, body):
            body(0, 0, True, False)
            with eng.Fori(0, (NB - 2) // 2) as i:
                body(i * 2 + 1, 1, True, True)
                body(i * 2 + 2, 0, True, True)
            body(NB - 1, 1, True, True)
            body(NB, 0, False, True)

        def pipeline(eng, body):
            for m in range(6):
                body(0, m)
            with eng.Fori(3, NT // 2 - 2) as i:
                body(i, 0)
                body(i, 1)
            for m in range(NT - 4, NT + 4):
                body(0, m)

        def tile_of(i, off, skew):
            o = off - skew
            if isinstance(i, int):
                n = 2 * i + o
                return (0 <= n < NT), n, n % 2, n // 2
            return True, i * 2 + o, o % 2, i + o // 2

        @block.sync
        def _(sp):
            sp.wait_ge(s_const, 1)
            sp.nop(nofuse=True)
            C6 = 6 * 128
            for dst_v, name in ((raw_i, "src"), (raw_d, "dst"), (ewr, "edge_weight")):
                v = a[name]
                sp.dma_start(dst_v[:, 0:6, :], v[0:C6 * 128].rearrange("(c p e) -> p c e", p=128, e=128))\
                    .then_inc(s_prep_dma, 16)
                sp.dma_start(dst_v[0:FULL - C6, 6, :], v[C6 * 128:FULL * 128].rearrange("(p e) -> p e", e=128))\
                    .then_inc(s_prep_dma, 16)
                sp.dma_start(dst_v[FULL - C6:FULL - C6 + 1, 6, 0:REST],
                             v[FULL * 128:E].rearrange("(p e) -> p e", p=1)).then_inc(s_prep_dma, 16)
            dn = a["dst"]
            sp.dma_start(raw_n[:, 0:6, :], dn[1:C6 * 128 + 1].rearrange("(c p e) -> p c e", p=128, e=128))\
                .then_inc(s_prep_dma, 16)
            sp.dma_start(raw_n[0:FULL - C6, 6, :], dn[C6 * 128 + 1:FULL * 128 + 1].rearrange("(p e) -> p e", e=128))\
                .then_inc(s_prep_dma, 16)
            sp.dma_start(raw_n[FULL - C6:FULL - C6 + 1, 6, 0:REST - 1],
                         dn[FULL * 128 + 1:E].rearrange("(p e) -> p e", p=1)).then_inc(s_prep_dma, 16)
            with nc.allow_non_contiguous_dma("one number of each tile"):
                dv = a["dst"][0:FULL * 128].rearrange("(o t e) -> o t e", o=1, e=128)
                sp.dma_start(base_r[0:1, 0:FULL].unsqueeze(2), dv[:, :, 0:1]).then_inc(s_base, 16)
                sp.dma_start(base_r[0:1, FULL:FULL + 1], a["dst"][FULL * 128:FULL * 128 + 1].unsqueeze(0))\
                    .then_inc(s_base, 16)
                sp.dma_start(last_r[0:1, 0:FULL].unsqueeze(2), dv[:, :, 127:128]).then_inc(s_rowsdma, 16)
            sp.dma_start(x0[0:N, :], a["x"][:, :]).then_inc(s_x0, 16)
            sp.dma_start(x0[N:N + 128, :], zrow[:, :]).then_inc(s_x0, 16)
            sp.dma_start(x0[N + 128:NP, :], zrow[0:NP - N - 128, :]).then_inc(s_x0, 16)
            sp.wait_ge(s_prep, 1)
            sp.nop(nofuse=True)
            sp.dma_start(mk1[0:C6, :].rearrange("(c p) w -> p c w", p=128), mkr[:, 0:6, :]).then_inc(s_mkst, 16)
            sp.dma_start(mk1[C6:T, :], mkr[0:T - C6, 6, :]).then_inc(s_mkst, 16)
            sp.wait_ge(s_mkst, 32)
            mkb = mk1.rearrange("(b t) w -> b (t w)", t=G)
            for dstm, H in ((mk4, H2), (mk8, H1)):
                for h in range(H):
                    sp.dma_start(dstm[:, h, :, :].rearrange("b t w -> b (t w)"), mkb).then_inc(s_mkst, 16)
            sp.wait_ge(s_mkst, 16 * (2 + H1 + H2))
            sp.wait_ge(s_x0, 48)
            barrier(sp)
            mk_of = {1: mk8, 2: mk4, 3: mk1}
            for L in range(5):
                p, H = PASS[L], HEADS[L]
                if H:
                    mrows = mk_of[L].rearrange("b h t w -> (b h t) w") if L < 3 else mk1

                    def windows(b, par, scores, sums):
                        if not scores:
                            return
                        wait(sp, p["w"], b + (past(L) + 1))
                        sp.nop(nofuse=True)
                        sp.dma_start(mk[0:G * H, par, :], mrows[ds(b * (G * H), G * H), :])\
                            .then_inc(p[f"mk{par}"], 16)
                        for k in range(G):
                            base = sp.value_load(base_r[0:1, ds(b * G + k, 1)], min_val=0, max_val=N)
                            if L == 1:
                                if k % 2 == 0:
                                    wait(sp, p["qe"], b * 8 + k // 2 + 1)
                                    sp.nop(nofuse=True)
                                sp.dma_start(qw[:, k % 4, :], q_t[ds(base, 128), :]).then_inc(p[f"qw{k % 4}"], 16)
                            else:
                                edt = ed1_t if L == 2 else ed2_t
                                sp.dma_start(edw[:, par, k, 0:H], edt[ds(base, 128), :])\
                                    .then_inc(p[f"ed{par}"], 16)
                    softmax_batches(sp, windows)
                barrier(sp)
                q = NODE[L]
                col = lambda v: v.rearrange("(k p) -> p k", p=128)
                bc = lambda v, w: v.rearrange("(o w) -> o w", o=1).to_broadcast([128, w])

                def load(dst_v, src_v):
                    sp.dma_start(dst_v, src_v).then_inc(q["wl"], 16)

                def rowsof(v):
                    return v.rearrange("(k p) w -> p k w", p=128)
                with nc.allow_non_contiguous_dma("vectors as columns"):
                    if L == 0:
                        for j in range(8):
                            load(wraw[32 * (j % 4):32 * (j % 4) + 32, 6 + j // 4, :], a["L0_gnn_weight"][:, :])
                        load(cols[:, :, 0], col(a["L0_gnn_gamma"]))
                        load(cols[:, :, 1], col(a["L0_gnn_beta"]))
                        load(wraw[:, 0:2, :], rowsof(a["L1_gnn_Wk"]))
                        load(wraw[:, 2:4, :], rowsof(a["L1_gnn_Wv"]))
                        load(wraw[:, 4:6, :], rowsof(a["L1_gnn_Wq"]))
                        load(brow[0:1, 0:256], a["L1_gnn_bk"].unsqueeze(0))
                        load(brow[0:1, 256:512], a["L1_gnn_bv"].unsqueeze(0))
                        load(brow[0:1, 512:768], a["L1_gnn_bq"].unsqueeze(0))
                    if L == 1:
                        load(wraw[:, 0:2, :], rowsof(a["L1_gnn_Wo"]))
                        load(wproj[:, :, 0:256], rowsof(a["L2_gnn_W1"]))
                        load(bo_b[:, :], bc(a["L1_gnn_bo"], 256))
                        load(as_b[:, :], a["L2_gnn_a1_src"].rearrange("(o h) w -> o (h w)", o=1).to_broadcast([128, 256]))
                        load(ad_b[:, :], a["L2_gnn_a1_dst"].rearrange("(o h) w -> o (h w)", o=1).to_broadcast([128, 256]))
                    if L == 2:
                        load(wproj[:, :, 0:256], rowsof(a["L2_gnn_W2"]))
                        load(bo_b[:, :], bc(a["L2_gnn_b1"], 256))
                        load(lg_b[:, :], bc(a["L2_gnn_ln_g"], 256))
                        load(lb_b[:, :], bc(a["L2_gnn_ln_b"], 256))
                        load(as_b[:, :], a["L2_gnn_a2_src"].to_broadcast([128, 256]))
                        load(ad_b[:, :], a["L2_gnn_a2_dst"].to_broadcast([128, 256]))
                        sp.dma_start(deg_d.unsqueeze(0), acc[4:5, 2, :]).then_inc(s_deg, 16)
                        sp.wait_ge(s_deg, 16)
                    if L == 3:
                        load(bo_b[:, :], bc(a["L2_gnn_b2"], 256))
                        load(dcol[:, :], deg_d.rearrange("(n p) -> p n", p=128))
                    if L == 4:
                        load(wraw[:, 0:2, :], rowsof(a["L3_gnn_W"]))
                        load(cols[:, :, 0], col(a["L3_gnn_gamma"]))
                        load(cols[:, :, 1], col(a["L3_gnn_beta"]))
                        load(cols[:, :, 2], col(a["L3_gnn_b"]))
                        load(dinv_b[:, :], bc(dinv_d, NP))
                    if L == 3:
                        sp.wait_ge(q["w"], 1)
                        sp.dma_start(dinv_d.rearrange("(n p) -> p n", p=128), dcol[:, :]).then_inc(s_deg, 16)
                        sp.wait_ge(s_deg, 32)
                resid = [x0, x1, None, x2, x3][L]
                keep = [x1, x2, None, x3, None][L]

                def moves(i, off):
                    ok, n, par, use = tile_of(i, off, 0)
                    if ok and resid is not None:
                        wait(sp, q["var"], n - 1)
                        sp.nop(nofuse=True)
                        sp.dma_start(xr[:, par, :], resid[ds(n * 128, 128), :]).then_inc(q[f"xr{par}"], 16)
                    ok, n, par, use = tile_of(i, off, 2)
                    if ok and L != 2:
                        wait(sp, q["xn"], n + 1)
                        sp.nop(nofuse=True)
                        if keep is not None:
                            sp.dma_start(keep[ds(n * 128, 128), :], xn[:, par, :]).then_inc(q[f"st{par}"], 16)
                            if L == 3:
                                sp.dma_start(xs_t[ds(n * 128, 128), :], xs[:, par, :]).then_inc(q[f"ps{par}"], 16)
                        elif not isinstance(n, int) or 128 * (n + 1) <= N:
                            sp.dma_start(out[ds(n * 128, 128), :], xn[:, par, :]).then_inc(q[f"st{par}"], 16)
                        elif 128 * n < N:
                            sp.dma_start(out[128 * n:N, :], xn[0:N - 128 * n, par, :]).then_inc(q[f"st{par}"], 16)
                        else:
                            sp.nop().then_inc(q[f"st{par}"], 16)
                    ok, n, par, use = tile_of(i, off, 4)
                    if ok and L < 3:
                        wait(sp, q["po"], n + 1)
                        sp.nop(nofuse=True)
                        rws = ds(n * 128, 128)
                        if L == 0:
                            sp.dma_start(kv_t[rws, :], po[:, par, 0:512]).then_inc(q[f"ps{par}"], 16)
                            sp.dma_start(q_t[rws, :], po[:, par, 512:768]).then_inc(q[f"ps{par}"], 16)
                        if L == 1:
                            sp.dma_start(g1_t[rws, :], po[:, par, 0:260]).then_inc(q[f"ps{par}"], 16)
                            sp.dma_start(ed1_t[rws, :], po[:, par, 260:264]).then_inc(q[f"ps{par}"], 16)
                        if L == 2:
                            sp.dma_start(g2_t[rws, :], po[:, par, 0:257]).then_inc(q[f"ps{par}"], 16)
                            sp.dma_start(ed2_t[rws, :], po[:, par, 257:258]).then_inc(q[f"ps{par}"], 16)
                pipeline(sp, moves)
                for par in range(2):
                    if L != 2:
                        sp.wait_ge(q[f"st{par}"], 16 * (NT // 2))
                    if L < 4:
                        sp.wait_ge(q[f"ps{par}"], 16 * (NT // 2) * (2 if L < 3 else 1))
                barrier(sp)

        @block.gpsimd
        def _(pool):
            nc.gpsimd.memset(raw_i[:, :, :], 0)
            nc.gpsimd.memset(raw_d[:, :, :], N)
            nc.gpsimd.memset(raw_n[:, :, :], N)
            nc.gpsimd.memset(ewr[:, :, :], 0.0)
            nc.gpsimd.memset(base_r[:, :], N)
            nc.gpsimd.memset(last_r[0:1, :], N)
            nc.gpsimd.memset(zrow[:, :], 0.0)
            pool.drain()
            pool.sem_inc(s_const, 1)
            nc.gpsimd.memset(src_c[:, T:T + G], 0)
            nc.gpsimd.memset(rel_c[:, T:T + G], 0.0)
            nc.gpsimd.memset(ew_c[:, T:T + G], 0.0)
            nc.gpsimd.memset(ident[:, :], 0.0)
            nc.gpsimd.memset(ones[:, :], 1.0)
            nc.gpsimd.memset(zeros[:, :], 0.0)
            nc.gpsimd.memset(selc8[:, :], 0.0)
            nc.gpsimd.memset(selc4[:, :], 0.0)
            nc.gpsimd.memset(seld8[:, :], 0.0)
            nc.gpsimd.memset(seld4[:, :], 0.0)
            nc.gpsimd.memset(degm[:, :], 1.0)
            nc.gpsimd.memset(w8[:, :, :, :], 1.0)
            nc.gpsimd.iota(iota[:, :], pattern=[[1, 128]], base=0, channel_multiplier=0,
                           allow_small_or_imprecise_dtypes=True)
            pool.drain()

            def ones_where(view_, pattern):
                nc.gpsimd.affine_select(out=view_, in_=view_, compare_op=ALU.not_equal, fill=1.0, base=0,
                                        pattern=pattern, channel_multiplier=1)
            ones_where(ident[:, :], [[-1, 128]])
            ones_where(selc8[:, 0:256].rearrange("p (g f) -> p g f", g=8), [[-G, 8], [0, 32]])
            ones_where(selc8[:, 256:384], [[-G, 128]])
            ones_where(selc4[:, 0:256].rearrange("p (g f) -> p g f", g=4), [[-G, 4], [0, 64]])
            ones_where(selc4[:, 256:384], [[-G, 128]])
            ones_where(seld8[:, :].rearrange("p (g f) -> p g f", g=8), [[-1, 8], [0, 32]])
            ones_where(seld4[:, :].rearrange("p (g f) -> p g f", g=4), [[-1, 4], [0, 64]])
            nc.gpsimd.memset(degm[:, 0:4], 0.0)
            nc.gpsimd.memset(acc[:, :, :], 0.0)
            pool.drain()
            pool.sem_inc(s_const, 1)
            barrier(pool)
            for L in range(5):
                p, W = PASS[L], WIDTH[L]
                nc.gpsimd.tensor_copy(stage[:, 0, :], src_c[:, 0:G]).then_inc(p["staged"], 1)
                with pool.Fori(0, NB // 4) as i:
                    for s in range(4):
                        nc.gpsimd.tensor_copy(stage[:, (s + 1) % 4, :], src_c[:, ds(i * (4 * G) + (s + 1) * G, G)])\
                            .then_inc(p["staged"], 1)
                        for g in range(4):
                            pool.wait_ge(p["agg"], i * (4 * G) + (s * G + 4 * g + 4))
                            if g == 0:
                                pool.wait_ge(p["staged"], i * 4 + (s + 1))
                            pool.nop(nofuse=True)
                            for j in range(4):
                                slot = (s % 2) * G + 4 * g + j
                                nc.gpsimd.indirect_dma_start(
                                    out=ring[:, slot, 0:W], out_offset=None, in_=table[L][:, :],
                                    in_offset=bass.IndirectOffsetOnAxis(
                                        ap=stage[:, s, 4 * g + j:4 * g + j + 1], axis=0))\
                                    .then_inc(s_ring[slot // 4], 16)
                barrier(pool)
                q = NODE[L]
                if L < 3:
                    def clear(i, off):
                        ok, n, par, use = tile_of(i, off, 1)
                        if ok:
                            wait(pool, q["pre"], n + 1)
                            nc.gpsimd.tensor_copy(acc[:, :, ds(n * 128, 128)],
                                                  zeros[:, :].unsqueeze(1).to_broadcast([128, 3, 128]))
                    if L == 2:
                        pool.wait_ge(s_deg, 16)
                    pipeline(pool, clear)
                barrier(pool)

        @block.scalar
        def _(act):
            barrier(act)
            for L in range(5):
                p, H = PASS[L], HEADS[L]
                R = G * H
                if H:
                    if L == 1:
                        act.sem_inc(p["ohtc"], 2)
                        act.sem_inc(p["w"], 2)

                    def chain(b, par, scores, sums):
                        if not scores:
                            return
                        for g in range(4):
                            wait(act, p["oht"], b * 4 + (4 * past(L) + g + 1))
                            if L == 1:
                                wait(act, p["qe"], b * 8 + 2 * g)
                            else:
                                wait(act, p["qeg"], b * 4 + (4 * past(L - 1) + g + 1))
                            act.activation(oht[:, g % 2, :, :], ot[g % 2][:, :].rearrange("p (k j) -> p k j", k=4),
                                           ACT.Copy).then_inc(p["ohtc"], 1)
                        wait(act, p["ch3"], b + (past(L) + 1))
                        act.activation(px[0:R, :], dd[0:R, :], ACT.Exp)
                        act.activation(cl[0:R, 3:4], cl[0:R, 2:3], ACT.Exp).then_inc(p["px"], 1)
                        wait(act, p["pb"], b + (past(L) + 1))
                        act.activation(w8[:, par, :, 0:H],
                                       m0[:, 128:128 + R].rearrange("p (h t) -> p t h", h=H), ACT.Copy)
                        act.activation(corr[:, par, 0:3], m1[:, 264:267], ACT.Copy).then_inc(p["w"], 1)
                    softmax_batches(act, chain)
                barrier(act)
                q = NODE[L]
                if L in (0, 4):
                    act.sem_inc(q["ch"], 2)
                if L < 4:
                    act.sem_inc(q["xtc"], 2)
                if L in (0, 1, 4):
                    for m in range({0: 3, 1: 1, 4: 1}[L]):
                        act.wait_ge(q["wt"], m + 1)
                        dst_v = {0: wproj[:, :, 256 * m:256 * m + 256], 1: wout, 4: wout}[L]
                        scale = float(1.0 / (32.0 ** 0.5)) if (L == 0 and m == 2) else 1.0
                        act.activation(dst_v, ot[m % 2][:, :].rearrange("p (k f) -> p k f", k=2), ACT.Copy,
                                       scale=scale).then_inc(q["wc"], 1)
                    if L == 0:
                        act.wait_ge(q["wl"], 16 * 16)
                        act.activation(brow[0:1, 512:768], brow[0:1, 512:768], ACT.Copy,
                                       scale=float(1.0 / (32.0 ** 0.5))).then_inc(q["wc"], 1)
                if L in (0, 4):
                    if L == 0:
                        def keep_chunk(c, par):
                            act.wait_ge(q["chd"], c + 1)
                            act.activation(acc[:, 0:2, ds(c * CH, CH)],
                                           qe[par][:, 0:2 * CH].rearrange("p (k n) -> p k n", k=2), ACT.Copy)\
                                .then_inc(q["ch"], 1)
                        with act.Fori(0, NCH // 2) as i:
                            keep_chunk(i * 2, 0)
                            keep_chunk(i * 2 + 1, 1)
                        keep_chunk(NCH - 1, 0)
                    for m in {0: (1,), 4: (3,)}[L]:
                        act.wait_ge(s_sq, m)
                        act.activation(bn[:, :, 1], bn[:, :, 1], ACT.Sqrt).then_inc(s_sqd, 1)
                    act.wait_ge(q["w"], 1 if L == 4 else 2)
                if L == 0:
                    act.drain()
                    for k in range(2):
                        act.activation(acc[:, k, 0:N], acc[:, k, 0:N], ACT.Tanh,
                                       bias=bn[:, k, 3:4], scale=bn[:, k, 2:3])
                if L == 3:
                    act.wait_ge(s_sq, 2)
                    act.activation(rr[:, 0, 0:NT], rr[:, 0, 0:NT], ACT.Sqrt).then_inc(s_sqd, 1)
                act.drain()

                def stages(i, off):
                    ok, n, par, use = tile_of(i, off, 0)
                    if ok and L in (0, 4):
                        wait(act, q["y"], n + 1)
                        for k in range(2):
                            if L == 0:
                                ins = act.activation(pre[:, par, 128 * k:128 * k + 128],
                                                     acc[:, k, ds(n * 128, 128)], ACT.Copy)
                            else:
                                ins = act.activation(pre[:, par, 128 * k:128 * k + 128],
                                                     acc[:, k, ds(n * 128, 128)], ACT.Relu,
                                                     bias=bn[:, k, 3:4], scale=bn[:, k, 2:3])
                        ins.then_inc(q["pre"], 1)
                    ok, n, par, use = tile_of(i, off, 1)
                    if ok:
                        act.wait_ge(q["var"], n + 1)
                        act.activation(lnst[:, par, 9:10], lnst[:, par, 8:9], ACT.Sqrt).then_inc(q["std"], 1)
                    ok, n, par, use = tile_of(i, off, 3)
                    if ok and L == 3:
                        wait(act, q["xt"], n + 1)
                        act.activation(acc[:, 0:2, ds(n * 128, 128)],
                                       (m0, m1)[par][:, 0:256].rearrange("p (k j) -> p k j", k=2), ACT.Copy)\
                            .then_inc(q["xtc"], 1)
                    if ok and L < 3:
                        wait(act, q["xt"], n + 1)
                        wait(act, q["pj"], n + 1)
                        act.activation(xt[:, par, :], (m0, m1)[par][:, 0:256], ACT.Copy)\
                            .then_inc(q["xtc"], 1)
                    ok, n, par, use = tile_of(i, off, 4)
                    if ok and L < 3:
                        wait(act, q["pj"], n + 3)
                        wait(act, q[f"ps{par}"], use * 32)
                        w1 = [512, 264, 258][L]
                        ins = act.activation(po[:, par, 0:w1], qe[par][:, 0:w1], ACT.Copy)
                        if L == 0:
                            ins = act.activation(po[:, par, 512:768], ag[par][:, 0:256], ACT.Copy)
                        ins.then_inc(q["po"], 1)
                pipeline(act, stages)
                barrier(act)

        @block.tensor
        def _(pe):
            mm = nc.tensor.matmul
            tr = nc.tensor.transpose
            pe.wait_ge(s_const, 2)
            for c in range(21):
                which, c7 = divmod(c, 7)
                n = 128 if c7 < 6 else T - 6 * 128
                rows_v = (raw_f, relr, ewr)[which]
                if c7 == 0:
                    pe.wait_ge(s_prep, (2, 3, 3)[which])
                if c >= 2:
                    pe.wait_ge(s_prep_c, c - 1)
                tr(ot[c % 2][:, 0:n], rows_v[0:n, c7, :], ident[0:n, 0:n]).then_inc(s_prep_t, 1)
            barrier(pe)
            for L in range(5):
                p, H, PL = PASS[L], HEADS[L], PLANES[L]
                R = G * H
                pe.sem_inc(p["agg"], 32)
                if L in (1, 2):
                    pe.sem_inc(p["qe" if L == 1 else "qeg"], 2)
                vo = 256 if L == 1 else 0

                def add_tile(b, par, k, use):
                    if k % 4 == 0:
                        pe.wait_ge(p["wready"], b * 4 + k // 4 + 1)
                    slot = par * G + k
                    if not H and k % 4 == 0:
                        pe.wait_ge(s_ring[slot // 4], use * 64 + (64 + RING_USES * L))
                    pe.wait_ge(p["added"], b * G + k + 1)
                    for c in range(2):
                        ins = mm(ag[k % 2][:, 128 * c:128 * c + 128], ring[:, slot, vo + 128 * c:vo + 128 * c + 128],
                                 oh[:, par, k, :], start=True, stop=True)
                    if H > 1:
                        ins = mm(ag[k % 2][0:8, 256:384], w8[:, par, k, :], oh[:, par, k, :], start=True, stop=True)
                    elif H == 1:
                        ins = mm(ag[k % 2][:, 256:384], ones[:, :], oh[:, par, k, :], start=True, stop=True)
                    ins.then_inc(p["agg"], 1)

                if not H:
                    with pe.Fori(0, NB // 2) as i:
                        for par in range(2):
                            for k in range(G):
                                add_tile(i * 2 + par, par, k, i)
                else:
                    def batch(b, par, scores, sums):
                        if scores:
                            for g in range(5):
                                if g < 4:
                                    pe.wait_ge(p["oh"], b * 4 + (4 * past(L) + g + 1))
                                    pe.wait_ge(p["ohtc"], b * 4 + (4 * past(L) + g + 1))
                                    for j in range(4):
                                        ins = tr(ot[g % 2][:, 128 * j:128 * j + 128], oh[:, par, 4 * g + j, :],
                                                 ident[:, :])
                                    ins.then_inc(p["oht"], 1)
                                if g > 0:
                                    f = g - 1
                                    gate(pe, p["ohtc"], b * 4 + (4 * past(L) + f + 3))
                                    if L == 1:
                                        for r in (2 * f, 2 * f + 1):
                                            pe.wait_ge(p["prod"], b * 8 + r + 1)
                                            for j in range(2):
                                                k = 2 * r + j
                                                pe.wait_ge(p[f"qw{k % 4}"], b * 64 + 16 * (k // 4) + 16)
                                                ins = mm(qe[r % 2][:, 256 * j:256 * j + 256],
                                                         oht[:, f % 2, k % 4, :], qw[:, k % 4, :],
                                                         start=True, stop=True)
                                            ins.then_inc(p["qe"], 1)
                                    else:
                                        if f == 0:
                                            if isinstance(b, int):
                                                pe.wait_ge(p[f"ed{par}"], 256 * (b // 2 + 1) + 128 * past(L - 1))
                                            else:
                                                pe.wait_ge(p[f"ed{par}"],
                                                           b * 128 + (128 * past(L - 1) + (256 if par == 0 else 128)))
                                            gate(pe, p["z"], b + (past(L - 1) + 1))
                                        for j in range(4):
                                            k = 4 * f + j
                                            ins = mm(qe[par][:, k * H:k * H + H], oht[:, f % 2, j, :],
                                                     edw[:, par, k, 0:H], start=True, stop=True)
                                        ins.then_inc(p["qeg"], 1)
                            gate(pe, p["w"], b + (past(L) + 2))
                            gate(pe, p["s"], b + (past(L) + 1))
                            tr(m0[0:R, 0:128], sc[:, par, 0:R], ident[:, :]).then_inc(p["st"], 1)
                        for k in range(G):
                            if sums:
                                add_tile(b - 1, 1 - par, k, None)
                            if scores and k == 5:
                                gate(pe, p["ch1"], b + (past(L) + 1))
                                mm(m1[0:1, 0:R], mx[0:R, 0:1], ident[0:R, 0:R], start=True, stop=True)
                                mm(m1[0:1, 128:128 + R], mx[0:R, 127:128], ident[0:R, 0:R], start=True, stop=True)\
                                    .then_inc(p["row"], 1)
                            if scores and k == 9:
                                gate(pe, p["ch2"], b + (past(L) + 1))
                                mm(m1[0:R, 256:257], rows[0:1, 5, 0:R], ones[0:1, 0:1], start=True, stop=True)
                                mm(m1[0:R, 257:258], rows[0:1, 4, 0:R], ones[0:1, 0:1], start=True, stop=True)\
                                    .then_inc(p["col"], 1)
                            if scores and k == 13:
                                gate(pe, p["px"], b + (past(L) + 1))
                                tr(m0[:, 128:128 + R], px[0:R, :], ident[0:R, 0:R])
                                for c in range(3):
                                    if H == 1:
                                        ins = mm(m1[:, 264 + c:265 + c], ones[0:1, :], cl[0:1, 3:4],
                                                 start=True, stop=True)
                                    else:
                                        add = H == H2 and c == 2
                                        ins = mm(m1[:, 264 + c:265 + c], selc[H][0:R, 128 * c:128 * c + 128],
                                                 cl[0:R, 3:4], start=True, stop=not add)
                                        if add:
                                            ins = mm(m1[:, 264 + c:265 + c], degm[0:1, :], ones[0:1, 0:1],
                                                     start=False, stop=True)
                                ins.then_inc(p["pb"], 1)
                    softmax_batches(pe, batch)
                barrier(pe)
                q = NODE[L]
                if L in (0, 1, 4):
                    pe.wait_ge(q["wl"], 16 * {0: 16, 1: 5, 4: 5}[L])
                    for m in range({0: 3, 1: 1, 4: 1}[L]):
                        if m >= 2:
                            pe.wait_ge(q["wc"], m - 1)
                        for kc in range(2):
                            for oc in range(2):
                                ins = tr(ot[m % 2][:, 256 * kc + 128 * oc:256 * kc + 128 * oc + 128],
                                         wraw[:, 2 * m + oc, 128 * kc:128 * kc + 128], ident[:, :])
                        ins.then_inc(q["wt"], 1)
                    pe.wait_ge(q["wc"], {0: 4, 1: 1, 4: 1}[L])
                if L in (0, 4):
                    if L == 0:
                        pe.wait_ge(q["w"], 1)

                    def project(c, par):
                        pe.wait_ge(q["ch"], c + 1)
                        for oc in range(2):
                            for kc in range(2):
                                ins = mm(qe[par][:, CH * oc:CH * oc + CH], wout[:, kc, 128 * oc:128 * oc + 128],
                                         acc[:, kc, ds(c * CH, CH)], start=kc == 0, stop=kc == 1)
                        ins.then_inc(q["chd"], 1)
                    with pe.Fori(0, NCH // 2) as i:
                        project(i * 2, 0)
                        project(i * 2 + 1, 1)
                    project(NCH - 1, 0)
                pe.sem_inc(q["y"], 2)
                if L < 3:
                    pe.sem_inc(q["pj"], 2)

                def stages(i, off):
                    ok, n, par, use = tile_of(i, off, 0)
                    if ok and L in (1, 2):
                        gate(pe, q["clr"], n + 1)
                        for c in range(2):
                            ins = mm(ag[par][:, 128 * c:128 * c + 128], seld[H][0:H, 128 * c:128 * c + 128],
                                     acc[0:H, 2, ds(n * 128, 128)], start=True, stop=True)
                        ins.then_inc(q["den"], 1)
                    ok, n, par, use = tile_of(i, off, 3)
                    if ok and L < 4:
                        pe.wait_ge(q["xn"], n + 1)
                        pe.wait_ge(q["xtc"], n + 1)
                        for c in range(2):
                            ins = tr((m0, m1)[par][:, 128 * c:128 * c + 128],
                                     (xs if L == 3 else xn)[:, par, 128 * c:128 * c + 128], ident[:, :])
                        ins.then_inc(q["xt"], 1)
                    ok, n, par, use = tile_of(i, off, 1)
                    if ok:
                        pe.wait_ge(q["pre"], n + 1)
                        wait(pe, q["var"], n - 1)
                        if L == 1:
                            for c in range(2):
                                ins = mm(ot[par][:, 0:256], pre[:, par, 128 * c:128 * c + 128], wout[:, c, :],
                                         start=c == 0, stop=c == 1)
                        else:
                            for c in range(2):
                                ins = tr(ot[par][:, 128 * c:128 * c + 128], pre[:, par, 128 * c:128 * c + 128],
                                         ident[:, :])
                        ins.then_inc(q["y"], 1)
                    ok, n, par, use = tile_of(i, off, 3)
                    if ok and L < 3:
                        pe.wait_ge(q["xtc"], n + 3)
                        wait(pe, q["po"], n - 1)
                        if L:
                            pe.wait_ge(q["w"], 1)
                        w1 = [512, 264, 258][L]
                        xv = xt[:, par, :]
                        for c in range(2):
                            ins = mm(qe[par][:, 0:w1], xv[:, 128 * c:128 * c + 128], wproj[:, c, 0:w1],
                                     start=c == 0, stop=(c == 1 and L > 0))
                        if L == 0:
                            mm(qe[par][:, 0:512], ones[0:1, :], brow[0:1, 0:512], start=False, stop=True)
                            for c in range(2):
                                mm(ag[par][:, 0:256], xv[:, 128 * c:128 * c + 128],
                                   wproj[:, c, 512:768], start=c == 0, stop=False)
                            ins = mm(ag[par][:, 0:256], ones[0:1, :], brow[0:1, 512:768],
                                     start=False, stop=True)
                        ins.then_inc(q["pj"], 1)
                pipeline(pe, stages)
                barrier(pe)

        @block.vector
        def _(dve):
            v = nc.vector
            tt = v.tensor_tensor
            dve.wait_ge(s_prep_dma, 12 * 16)
            v.tensor_copy(raw_f[:, :, :], raw_i[:, :, :])
            v.tensor_copy(relr[:, :, :], raw_d[:, :, :])
            dve.drain()
            tt(relr[:, :, :], relr[:, :, :], raw_d[:, :, 0:1].to_broadcast([128, 7, 128]), ALU.subtract)
            v.memset(mkr[:, :, 0:1], 0.0)
            v.memset(mkr[:, :, 128:129], 0.0)
            dve.drain()
            tt(mkr[:, :, 1:128], relr[:, :, 1:128], relr[:, :, 0:127], ALU.not_equal)
            v.tensor_scalar(mkr[:, :, 129:257], relr[:, :, :], 0.0, -BIG, ALU.not_equal, ALU.mult)
            tt(mkr[:, :, 257:385], relr[:, :, :], relr[:, :, 127:128].to_broadcast([128, 7, 128]), ALU.not_equal)
            tt(mkr[:, :, 385:513], raw_d[:, :, :], raw_n[:, :, :], ALU.not_equal)
            v.tensor_scalar(lt[:, :, :], raw_d[:, :, :], float(LOOPS2), LN2, ALU.is_lt, ALU.mult)
            dve.drain()
            tt(mkr[:, :, 385:513], mkr[:, :, 385:513], lt[:, :, :], ALU.mult)
            v.tensor_scalar(mkr[:, :, 1:128], mkr[:, :, 1:128], -BIG, None, ALU.mult)
            v.tensor_scalar(mkr[:, :, 257:385], mkr[:, :, 257:385], -BIG, None, ALU.mult)
            dve.drain()
            dve.sem_inc(s_prep, 3)
            for c in range(21):
                which, c7 = divmod(c, 7)
                n = 128 if c7 < 6 else T - 6 * 128
                dst_v = (src_c, rel_c, ew_c)[which]
                dve.wait_ge(s_prep_t, c + 1)
                v.tensor_copy(dst_v[:, 128 * c7:128 * c7 + n], ot[c % 2][:, 0:n]).then_inc(s_prep_c, 1)
            dve.wait_ge(s_base, 32)
            dve.wait_ge(s_rowsdma, 16)
            tt(cneg_r[:, 1:T], base_r[:, 1:T], last_r[0:1, 0:T - 1], ALU.not_equal)
            tt(sneg_r[:, :], base_r[:, :], last_r[0:1, :], ALU.not_equal)
            v.memset(cneg_r[:, 0:1], 1.0)
            for k in range(2):
                v.memset(ag[k][:, :], 0.0)
            dve.drain()
            tt(sneg_r[:, :], sneg_r[:, :], cneg_r[:, :], ALU.add)
            dve.drain()
            v.tensor_scalar(cneg_r[:, :], cneg_r[:, :], -BIG, None, ALU.mult)
            v.tensor_scalar(sneg_r[:, :], sneg_r[:, :], -BIG, None, ALU.mult)
            barrier(dve)
            for L in range(5):
                p, H, PL = PASS[L], HEADS[L], PLANES[L]
                R = G * H
                dve.sem_inc(p["added"], 2)

                def add_window(b, par, k):
                    base = dve.value_load(base_r[0:1, ds(b * G + k, 1)], min_val=0, max_val=N)
                    win = acc[:, 0:PL, ds(base, 128)]
                    dve.wait_ge(p["agg"], b * G + (k + 33))
                    dve.wait_ge(p["added"], b * G + (k + 2))
                    tt(win, win, ag[k % 2][:, 0:128 * PL].rearrange("p (c j) -> p c j", c=PL), ALU.add)\
                        .then_inc(p["added"], 1)

                def one_hots(b, par, g, weight):
                    for k in range(4 * g, 4 * g + 4):
                        if weight is None:
                            ins = v.tensor_scalar(oh[:, par, k, :], iota[:, :], rel_c[:, ds(b * G + k, 1)], None,
                                                  ALU.is_equal)
                        else:
                            ins = v.tensor_scalar(oh[:, par, k, :], iota[:, :], rel_c[:, ds(b * G + k, 1)],
                                                  weight(k), ALU.is_equal, ALU.mult)
                    return ins

                if not H:
                    def hots(b, par, g):
                        wt = (lambda k: ew_c[:, ds(b * G + k, 1)]) if L == 0 else None
                        one_hots(b, par, g, wt).then_inc(p["wready"], 1)
                    hots(0, 0, 0)
                    with dve.Fori(0, NB // 2) as i:
                        for par in range(2):
                            b = i * 2 + par
                            for g in range(4):
                                if g < 3:
                                    hots(b, par, g + 1)
                                else:
                                    hots(b + 1, 1 - par, 0)
                                for k in range(4 * g, 4 * g + 4):
                                    add_window(b, par, k)
                else:
                    if L == 2:
                        dve.sem_inc(p["z"], 2)
                    if L == 1:
                        dve.sem_inc(p["prod"], 2)
                        dve.sem_inc(p["red"], 2)
                    if L == 2:
                        v.memset(w8[:, :, :, :], 1.0)
                    v.memset(fprev[:, :], -BIG)
                    v.memset(rows[:, :, :], -2.0 * BIG)

                    def scores_of(b, par):
                        for g in range(4):
                            one_hots(b, par, g, None).then_inc(p["oh"], 1)
                        sv = sc[:, par, 0:R].rearrange("p (h t) -> p t h", h=H)

                        def ready(k):
                            if isinstance(b, int):
                                dve.wait_ge(s_ring[par * 4 + k // 4], 64 * (b // 2 + 1) + RING_USES * L)
                            else:
                                dve.wait_ge(s_ring[par * 4 + k // 4],
                                            b * 32 + ((64 if par == 0 else 32) + RING_USES * L))
                        if L == 1:
                            def reduce(r):
                                dve.wait_ge(p["prod"], b * 8 + (r + 3))
                                ins = v.tensor_reduce(
                                    sv[:, 2 * r:2 * r + 2, :],
                                    prod[:, r % 2, :, :].rearrange("p t (h d) -> p t h d", h=H), AX.X, ALU.add)
                                ins.then_inc(p["red"], 1)
                            for r in range(8):
                                if r % 2 == 0:
                                    ready(2 * r)
                                dve.wait_ge(p["qe"], b * 8 + (r + 3))
                                dve.wait_ge(p["red"], b * 8 + (r + 1))
                                tt(prod[:, r % 2, :, :], qe[r % 2][:, :].rearrange("p (t w) -> p t w", t=2),
                                   ring[:, par * G + 2 * r:par * G + 2 * r + 2, 0:256], ALU.mult)\
                                    .then_inc(p["prod"], 1)
                                if r:
                                    reduce(r - 1)
                            reduce(7)
                        else:
                            for k in range(0, G, 4):
                                ready(k)
                            dve.wait_ge(p["qeg"], b * 4 + (4 * past(L - 1) + 6))
                            tt(sv, qe[par][:, 0:R].rearrange("p (t h) -> p t h", h=H),
                               ring[:, par * G:par * G + G, 256:256 + H], ALU.add).then_inc(p["z"], 1)
                            dve.drain()
                            v.scalar_tensor_tensor(sc[:, par, 0:R], sc[:, par, 0:R], 0.2, sc[:, par, 0:R],
                                                   ALU.mult, ALU.max)
                        dve.drain()
                        dve.sem_inc(p["s"], 1)

                    def ch1(b, par):
                        if isinstance(b, int):
                            dve.wait_ge(p[f"mk{par}"], 16 * (b // 2 + 1) + 8 * past(L))
                        else:
                            dve.wait_ge(p[f"mk{par}"], b * 8 + (8 * past(L) + (16 if par == 0 else 8)))
                        dve.wait_ge(p["st"], b + (past(L) + 1))
                        v.tensor_tensor_scan(out=fw[0:R, :], data0=mk[0:R, par, 0:128], data1=m0[0:R, 0:128],
                                             initial=-BIG, op0=ALU.add, op1=ALU.max)
                        dve.drain()
                        v.tensor_tensor_scan(out=mx[0:R, ::-1], data0=mk[0:R, par, 1:129][:, ::-1],
                                             data1=fw[0:R, ::-1], initial=-BIG, op0=ALU.add, op1=ALU.max)\
                            .then_inc(p["ch1"], 1)

                    def ch2(b, par):
                        hv = lambda k: rows[0:1, k, 0:R].rearrange("p (h t) -> p h t", h=H)
                        nb = lambda r_, o, n: r_[0:1, ds(b * G + o, n)].unsqueeze(1).to_broadcast([1, H, n])
                        head = m1[0:1, 0:R].rearrange("p (h t) -> p h t", h=H)
                        tail = m1[0:1, 128:128 + R].rearrange("p (h t) -> p h t", h=H)
                        fp = fprev[0:1, 0:H].unsqueeze(2)
                        v.tensor_copy(hv(0)[:, :, 1:G], nb(sneg_r, 1, G - 1))
                        tt(hv(6)[:, :, 0:1], fp, nb(sneg_r, 0, 1), ALU.add)
                        dve.wait_ge(p["row"], b + (past(L) + 1))
                        v.tensor_copy(hv(1), tail)
                        tt(hv(2)[:, :, 0:G - 1], head[:, :, 1:G], nb(cneg_r, 1, G - 1), ALU.add)
                        tt(hv(5)[:, :, 0:1], fp, nb(cneg_r, 0, 1), ALU.add)
                        dve.drain()
                        tt(hv(1)[:, :, 0:1], hv(1)[:, :, 0:1], hv(6)[:, :, 0:1], ALU.max)
                        v.tensor_tensor_scan(out=rows[0:1, 3, 0:R][:, ::-1], data0=rows[0:1, 0, 1:R + 1][:, ::-1],
                                             data1=rows[0:1, 2, 0:R][:, ::-1], initial=-BIG,
                                             op0=ALU.add, op1=ALU.max)
                        dve.drain()
                        v.tensor_tensor_scan(out=rows[0:1, 4, 0:R], data0=rows[0:1, 0, 0:R],
                                             data1=rows[0:1, 1, 0:R], initial=-BIG, op0=ALU.add, op1=ALU.max)
                        dve.drain()
                        tt(rows[0:1, 4, 0:R], rows[0:1, 4, 0:R], rows[0:1, 3, 0:R], ALU.max)
                        dve.drain()
                        tt(hv(5)[:, :, 1:G], hv(4)[:, :, 0:G - 1], nb(cneg_r, 1, G - 1), ALU.add)
                        v.tensor_copy(fp, hv(4)[:, :, G - 1:G])
                        dve.drain()
                        dve.sem_inc(p["ch2"], 1)

                    def ch3(b, par):
                        dve.wait_ge(p["col"], b + (past(L) + 1))
                        v.tensor_copy(cl[0:R, 0:2], m1[0:R, 256:258])
                        dve.drain()
                        v.scalar_tensor_tensor(m2[0:R, :], mk[0:R, par, 129:257], cl[0:R, 0:1], mx[0:R, :],
                                               ALU.add, ALU.max)
                        dve.drain()
                        v.scalar_tensor_tensor(m2[0:R, :], mk[0:R, par, 257:385], cl[0:R, 1:2], m2[0:R, :],
                                               ALU.add, ALU.max)
                        dve.drain()
                        tt(dd[0:R, :], m0[0:R, 0:128], m2[0:R, :], ALU.subtract)
                        tt(cl[0:R, 2:3], cl[0:R, 0:1], m2[0:R, 0:1], ALU.subtract)
                        dve.drain()
                        if L > 1:
                            tt(dd[0:R, :], dd[0:R, :], mk[0:R, par, 385:513], ALU.add)
                            dve.drain()
                        dve.sem_inc(p["ch3"], 1)

                    def weigh(b, par, g):
                        if H == 1:
                            for k in range(4 * g, 4 * g + 4):
                                ins = v.tensor_scalar(oh[:, par, k, :], oh[:, par, k, :], w8[:, par, k, 0:1], None,
                                                      ALU.mult)
                        else:
                            o = 256 if L == 1 else 0
                            for k in range(4 * g, 4 * g + 4, 1):
                                vv = ring[:, par * G + k, o:o + 256].rearrange("p (h d) -> p h d", h=H)
                                wv = w8[:, par, k, 0:H].unsqueeze(2).to_broadcast([128, H, 256 // H])
                                ins = tt(vv, vv, wv, ALU.mult)
                        ins.then_inc(p["wready"], 1)

                    def batch(b, par, scores, sums):
                        if scores:
                            scores_of(b, par)
                        if sums:
                            c, cp = b - 1, 1 - par
                            dve.wait_ge(p["w"], c + (past(L) + 3))
                            base = dve.value_load(base_r[0:1, ds(c * G, 1)], min_val=0, max_val=N)
                            colv = acc[:, 0:3, ds(base, 1)]
                            dve.wait_ge(p["added"], c * G + 2)
                            tt(colv, colv, corr[:, cp, 0:3].unsqueeze(2), ALU.mult)
                            weigh(c, cp, 0)
                            dve.drain()
                        for g in range(4):
                            if sums:
                                if g < 3:
                                    weigh(c, cp, g + 1)
                                for k in range(4 * g, 4 * g + 4):
                                    add_window(c, cp, k)
                            if scores:
                                (ch1, ch2, ch3, lambda b_, p_: None)[g](b, par)
                    softmax_batches(dve, batch)
                barrier(dve)
                q = NODE[L]
                if L == 0:
                    dve.wait_ge(q["wl"], 16 * 16)
                    for j in range(8):
                        kc, pp = j // 4, 32 * (j % 4)
                        for i8 in range(8):
                            c = OCT_IDX[i8][j]
                            v.tensor_scalar(wout[pp:pp + 32, kc, 32 * i8:32 * i8 + 32],
                                            wraw[pp:pp + 32, 6 + kc, 32 * c:32 * c + 32],
                                            float(OCT_SIGN[i8][j]), None, ALU.mult)
                    dve.drain()
                    dve.sem_inc(q["w"], 1)
                if L in (1, 2):
                    dve.wait_ge(q["wl"], 16 * {1: 5, 2: 6}[L])
                    Hn = HEADS[L + 1]
                    for kc in range(2):
                        for s_, av in ((0, as_b), (1, ad_b)):
                            tt(wtmp[:, :], wproj[:, kc, 0:256], av[:, :], ALU.mult)
                            dve.drain()
                            v.tensor_reduce(wproj[:, kc, 256 + Hn * s_:256 + Hn * s_ + Hn],
                                            wtmp[:, :].rearrange("p (h d) -> p h d", h=Hn), AX.X, ALU.add)
                            dve.drain()
                    dve.sem_inc(q["w"], 1)
                if L == 3:
                    dve.wait_ge(q["wl"], 32)
                    v.tensor_scalar(dcol[:, :], dcol[:, :], 1.0, None, ALU.add)
                    dve.drain()
                    v.tensor_scalar(rr[:, 0, 0:NT], dcol[:, :], 1.0, None, ALU.max).then_inc(s_sq, 1)
                    v.tensor_scalar(dcol[:, :], dcol[:, :], 0.0, None, ALU.is_gt)
                    dve.wait_ge(s_sqd, 2)
                    v.reciprocal(rr[:, 1, 0:NT], rr[:, 0, 0:NT])
                    dve.drain()
                    tt(dcol[:, :], dcol[:, :], rr[:, 1, 0:NT], ALU.mult)
                    dve.drain()
                    dve.sem_inc(q["w"], 1)
                if L in (0, 4):
                    if L == 4:
                        dve.wait_ge(q["wl"], 16 * 5)

                    def measure(c, par):
                        if L == 4:
                            dve.wait_ge(q["chd"], c + 1)
                        else:
                            dve.wait_ge(q["ch"], c + 3)
                        zv = qe[par][:, 0:2 * CH].rearrange("p (k n) -> p k n", k=2)
                        if L == 4:
                            dst_v = acc[:, 0:2, ds(c * CH, CH)]
                            tt(dst_v, zv, dinv_b[:, ds(c * CH, CH)].unsqueeze(1).to_broadcast([128, 2, CH]), ALU.mult)
                            dve.drain()
                            dve.sem_inc(q["ch"], 1)
                            for k in range(2):
                                v.tensor_scalar(acc[:, k, ds(c * CH, CH)], acc[:, k, ds(c * CH, CH)],
                                                cols[:, k, 2:3], None, ALU.add)
                            dve.drain()
                            for k in range(2):
                                v.bn_stats(stats[:, k, ds(c * 6, 6)], acc[:, k, ds(c * CH, CH)])
                        else:
                            for k in range(2):
                                v.bn_stats(stats[:, k, ds(c * 6, 6)], acc[:, k, ds(c * CH, CH)])
                    with dve.Fori(0, NCH // 2) as i:
                        measure(i * 2, 0)
                        measure(i * 2 + 1, 1)
                    measure(NCH - 1, 0)
                    dve.drain()
                    for k in range(2):
                        v.bn_aggr(bn[:, k, 0:2], stats[:, k, :])
                    dve.drain()
                    v.tensor_scalar(bn[:, :, 1], bn[:, :, 1], EPS, None, ALU.add).then_inc(s_sq, 1)
                    dve.wait_ge(s_sqd, 1 if L == 0 else 3)
                    v.reciprocal(bn[:, :, 1], bn[:, :, 1])
                    dve.drain()
                    for k in range(2):
                        tt(bn[:, k, 2:3], bn[:, k, 1:2], cols[:, k, 0:1], ALU.mult)
                    dve.drain()
                    for k in range(2):
                        tt(bn[:, k, 0:1], bn[:, k, 0:1], bn[:, k, 2:3], ALU.mult)
                    dve.drain()
                    for k in range(2):
                        tt(bn[:, k, 3:4], cols[:, k, 1:2], bn[:, k, 0:1], ALU.subtract)
                    dve.drain()
                    dve.sem_inc(q["w"], 1)
                if L in (1, 2):
                    dve.sem_inc(q["clr"], 2)

                def stages(i, off):
                    ok, n, par, use = tile_of(i, off, 0)
                    if ok and L in (1, 2, 3):
                        if L < 3:
                            dve.wait_ge(q["den"], n + 1)
                            v.tensor_scalar(dvt[:, par, :], ag[par][:, 0:256], 0.5, None, ALU.max)\
                                .then_inc(q["clr"], 1)
                        else:
                            v.tensor_scalar(dvt[:, par, 0:128], acc[:, 2, ds(n * 128, 128)], 0.5, None, ALU.max)
                        dve.drain()
                        wd = 256 if L < 3 else 128
                        v.reciprocal(dvt[:, par, 0:wd], dvt[:, par, 0:wd])
                        dve.drain()
                        dve.wait_ge(q["y"], n + 1)
                        dn = dvt[:, par, :].rearrange("p (k j) -> p k j", k=2) if L < 3 else \
                            dvt[:, par, 0:128].unsqueeze(1).to_broadcast([128, 2, 128])
                        tt(pre[:, par, :].rearrange("p (k j) -> p k j", k=2), acc[:, 0:2, ds(n * 128, 128)], dn,
                           ALU.mult).then_inc(q["pre"], 1)
                    ok, n, par, use = tile_of(i, off, 1)
                    if ok:
                        dve.wait_ge(q["y"], n + 3)
                        wait(dve, q["xn"], n - 1)
                        if L in (1, 2, 3):
                            tt(rr[:, par, :], ot[par][:, 0:256], bo_b[:, :], ALU.add)
                            dve.drain()
                        if L != 2:
                            dve.wait_ge(q[f"xr{par}"], use * 16 + 16)
                            v.scalar_tensor_tensor(rr[:, par, :], xr[:, par, :], 2.0 if L == 4 else 1.0,
                                                   rr[:, par, :] if L in (1, 3) else ot[par][:, 0:256],
                                                   ALU.mult, ALU.add)
                            dve.drain()
                        v.bn_stats(lnst[:, par, 0:6], rr[:, par, :])
                        dve.drain()
                        v.bn_aggr(lnst[:, par, 6:8], lnst[:, par, 0:6])
                        dve.drain()
                        v.tensor_scalar(lnst[:, par, 8:9], lnst[:, par, 7:8], EPS, None, ALU.add)\
                            .then_inc(q["var"], 1)
                    ok, n, par, use = tile_of(i, off, 2)
                    if ok:
                        dve.wait_ge(q["std"], n + 1)
                        v.reciprocal(lnst[:, par, 10:11], lnst[:, par, 9:10])
                        if L != 2:
                            wait(dve, q[f"st{par}"], use * 16)
                        if L < 4:
                            wait(dve, q["xt"], n - 1)
                        dve.nop(nofuse=True)
                        dve.drain()
                        ins = v.tensor_scalar(xn[:, par, :], rr[:, par, :], lnst[:, par, 6:7], lnst[:, par, 10:11],
                                              ALU.subtract, ALU.mult)
                        if L == 2:
                            dve.drain()
                            tt(xn[:, par, :], xn[:, par, :], lg_b[:, :], ALU.mult)
                            dve.drain()
                            tt(xn[:, par, :], xn[:, par, :], lb_b[:, :], ALU.add)
                            dve.drain()
                            ins = v.tensor_scalar(xn[:, par, :], xn[:, par, :], 0.0, None, ALU.max)
                        if L == 3:
                            dve.drain()
                            wait(dve, q[f"ps{par}"], use * 16)
                            ins = v.tensor_scalar(xs[:, par, :], xn[:, par, :], dcol[:, ds(n, 1)], None, ALU.mult)
                        ins.then_inc(q["xn"], 1)
                if L == 3:
                    dve.wait_ge(s_deg, 32)
                dve.drain()
                pipeline(dve, stages)
                barrier(dve)


_INS = ["x", "src", "dst", "edge_weight", "L0_gnn_weight", "L0_gnn_gamma", "L0_gnn_beta",
        "L1_gnn_Wq", "L1_gnn_bq", "L1_gnn_Wk", "L1_gnn_bk", "L1_gnn_Wv", "L1_gnn_bv", "L1_gnn_Wo", "L1_gnn_bo",
        "L2_gnn_W1", "L2_gnn_a1_src", "L2_gnn_a1_dst", "L2_gnn_b1", "L2_gnn_ln_g", "L2_gnn_ln_b", "L2_gnn_W2",
        "L2_gnn_a2_src", "L2_gnn_a2_dst", "L2_gnn_b2", "L3_gnn_W", "L3_gnn_b", "L3_gnn_gamma", "L3_gnn_beta"]


def kernel(**inputs):
    import numpy as _np
    import concourse.bacc as _bacc
    from concourse.bass_utils import run_bass_kernel_spmd as _run

    nc = _bacc.Bacc("TRN2", target_bir_lowering=False, num_devices=1)
    arrays, args = {}, {}
    for name in _INS:
        arr = _np.ascontiguousarray(inputs[name])
        arrays[f"in_{name}"] = arr
        args[name] = nc.dram_tensor(f"in_{name}", arr.shape, mybir.dt.from_np(arr.dtype), kind="ExternalInput").ap()
    out = nc.dram_tensor("out_0", (N, D), F32, kind="ExternalOutput").ap()
    gnn_kernel(nc, args, out)
    r = _run(nc, [arrays], core_ids=[0])
    return r.results[0]["out_0"]
```

```python
import concourse.bass as bass
from concourse import mybir
from contextlib import ExitStack

F32 = mybir.dt.float32
I32 = mybir.dt.int32
BF16 = mybir.dt.bfloat16
ALU = mybir.AluOpType
ACT = mybir.ActivationFunctionType
AX = mybir.AxisListType

N, E, D = 6250, 106250, 256
G = 16
T = 832
NB = T // G
FULL, REST = divmod(E, 128)
NT = 50
NP = NT * 128
CH, NCH = 250, 25
SETS = [4, 2, 4, 4, 4]
AHEAD = [2, 2, 4, 4, 4]
SLOT = [260, 512, 260, 260, 260]
BIG = 1.0e30
EPS = 1e-5
H1, H2 = 8, 4
MKW = 513
LOOPS2 = 1250
LN2 = 0.6931471805599453
OCT_IDX = [[i ^ j for j in range(8)] for i in range(8)]
OCT_SIGN = [[1, 1, 1, 1, 1, 1, 1, 1], [1, -1, 1, -1, 1, -1, -1, 1], [1, -1, -1, 1, 1, 1, -1, -1],
            [1, 1, -1, -1, 1, -1, 1, -1], [1, -1, -1, -1, -1, 1, 1, 1], [1, 1, -1, 1, -1, -1, -1, 1],
            [1, 1, 1, -1, -1, 1, -1, -1], [1, -1, 1, 1, -1, -1, 1, -1]]
WIDTH = [256, 512, 260, 257, 256]
HEADS = [0, H1, H2, 1, 0]
PLANES = [2, 3, 3, 3, 2]
ds = bass.ds


def ring_base(L, k):
    return sum(64 * (NB // SETS[m]) for m in range(L) if k < 4 * SETS[m])


def groups_before(L):
    return sum(4 * NB + (HEADS[m] == 0) for m in range(L))


def past(L):
    return NB * (L - 1)


def wait(eng, sem, value):
    if isinstance(value, int) and value <= 0:
        return
    eng.wait_ge(sem, value)


def gate(eng, sem, value):
    wait(eng, sem, value)
    eng.nop(nofuse=True)


def gnn_kernel(nc, a, out):
    ctx = ExitStack()
    with ctx:
        def sb(name, shape, dt=F32):
            return ctx.enter_context(nc.sbuf_tensor(name, shape, dt))

        def sem(name):
            return ctx.enter_context(nc.semaphore(name))

        def dram(name, shape, dt=F32):
            return nc.dram_tensor(name, shape, dt).ap()

        x0 = dram("x0", (NP, D))
        x1 = dram("x1", (NP, D))
        x2 = dram("x2", (NP, D))
        x3 = dram("x3", (NP, D))
        kv_t = dram("kv_t", (NP, 512))
        q_t = dram("q_t", (NP, D))
        g1_t = dram("g1_t", (NP, 260))
        ed1_t = dram("ed1_t", (NP, 4))
        g2_t = dram("g2_t", (NP, 257))
        ed2_t = dram("ed2_t", (NP, 1))
        xs_t = dram("xs_t", (NP, D))
        deg_d = dram("deg_d", (NP,))
        dinv_d = dram("dinv_d", (NP,))
        mk1 = dram("mk1", (T, MKW))
        mk4 = dram("mk4", (NB, 4, G, MKW))
        mk8 = dram("mk8", (NB, 8, G, MKW))
        table = [a["x"], kv_t, g1_t, g2_t, xs_t]

        acc = sb("acc", [128, 3, NP])
        ring = sb("ring", [128, 64 * 260])
        rflat = ring[:, :]
        rings = [ring[:, 0:4 * SETS[L] * 4 * SLOT[L]].rearrange("p (s w) -> p s w", w=SLOT[L]) for L in range(5)]
        ohc = sb("ohc", [128, 2, 4, 128])
        ohb = sb("ohb", [128, 2, 4, 128], BF16)
        oht = sb("oht", [128, 4, 4, 128])
        qw = sb("qw", [128, 8, 256])
        prod = sb("prod", [128, 2, 2, 256])
        src_c = sb("src_c", [128, T + G], I32)
        rel_c = sb("rel_c", [128, T + G])
        ew_c = sb("ew_c", [128, T + G])
        rel_s = sb("rel_s", [128, 4, G])
        base_r = sb("base_r", [1, T], I32)
        cneg_r = sb("cneg_r", [1, T])
        sneg_r = sb("sneg_r", [1, T])
        stage = sb("stage", [128, 4, G], I32)
        mk = sb("mk", [128, 2, MKW])
        sc = sb("sc", [128, 2, 128])
        fw = sb("fw", [128, 128])
        mx = sb("mx", [128, 128])
        m2 = sb("m2", [128, 128])
        dd = sb("dd", [128, 128])
        px = sb("px", [128, 128])
        w8 = sb("w8", [128, 2, G, 8])
        edw = sb("edw", [128, 2, G, 4])
        corr = sb("corr", [128, 2, 4])
        cl = sb("cl", [128, 4])
        ident = sb("ident", [128, 128])
        iota = sb("iota", [128, 128])
        ident_b = sb("ident_b", [128, 128], BF16)
        iota_b = sb("iota_b", [128, 128], BF16)
        ones = sb("ones", [128, 128])
        zeros = sb("zeros", [128, 128])
        selc8 = sb("selc8", [128, 384])
        selc4 = sb("selc4", [128, 384])
        seld8 = sb("seld8", [128, 256])
        seld4 = sb("seld4", [128, 256])
        degm = sb("degm", [1, 128])
        rows = sb("rows", [1, 7, 132])
        fprev = sb("fprev", [1, 8])
        bn = sb("bn", [128, 2, 4])
        lnst = sb("lnst", [128, 2, 12])
        cols = sb("cols", [128, 2, 4])
        dcol = sb("dcol", [128, NT])
        banks = [ctx.enter_context(nc.psum_tensor(f"bank{k}", [128, 512], F32)) for k in range(8)]
        ag, ot, qe, m0, m1 = banks[0:2], banks[2:4], banks[4:6], banks[6], banks[7]
        selc = {H1: selc8, H2: selc4}
        seld = {H1: seld8, H2: seld4}

        at = [0]

        def view(*shape, dt=F32):
            size = 1
            for s in shape:
                size *= s
            v = rflat[:, at[0]:at[0] + size]
            at[0] += size
            assert at[0] <= 64 * 260
            if dt is not F32:
                v = v.bitcast(dt)
            if len(shape) == 2:
                v = v.rearrange("p (u v) -> p u v", u=shape[0])
            if len(shape) == 3:
                v = v.rearrange("p (u v w) -> p u v w", u=shape[0], v=shape[1])
            return v

        raw_i = view(7, 128, dt=I32)
        raw_f = view(7, 128)
        relr = view(7, 128)
        ewr = view(7, 128)
        mkr = view(7, MKW)
        last_r = view(T, dt=I32)
        raw_d = view(7, 128, dt=I32)
        zrow = view(256)
        raw_n = view(7, 128, dt=I32)
        lt = view(7, 128)
        at[0] = 0
        wraw = view(8, 256)
        wout = view(2, 256)
        pre = view(2, 256)
        xr = view(2, 256)
        xn = view(2, 256)
        rr = view(2, 256)
        stats = view(2, NCH * 6)
        shared = at[0]
        dinv_b = view(NP)
        at[0] = shared
        wproj = view(2, 768)
        xt = view(2, 256)
        po = view(2, 768)
        brow = view(768)
        bo_b = view(256)
        lg_b = view(256)
        lb_b = view(256)
        as_b = view(256)
        ad_b = view(256)
        wtmp = view(256)
        xs = view(2, 256)

        bar = sem("bar")
        s_ring = [sem(f"ring_ready{k}") for k in range(16)]
        s_const = sem("const_ready")
        s_prep_dma = sem("prep_loaded")
        s_base = sem("base_loaded")
        s_rowsdma = sem("lasts_loaded")
        s_prep = sem("prep_rows")
        s_prep_t = sem("prep_transposed")
        s_prep_c = sem("prep_copied")
        s_mkst = sem("masks_stored")
        s_x0 = sem("x0_stored")
        shared_sems = {k: sem(k) for k in ("staged", "added", "wready")}
        PASS = []
        for L in range(5):
            p = {"agg": sem(f"agg{L}"), **shared_sems}
            if L == 1:
                p.update({k: sem(f"{k}{L}") for k in (
                    "oh", "oht", "ohtc", "s", "st", "ch1", "row", "ch2", "col", "ch3", "px", "pb", "w",
                    "mk0", "mk1", "qe", "prod", "red", "qw0", "qw1", "qw2", "qw3")})
            if L == 2:
                p.update({k: sem(f"{k}{L}") for k in ("qeg", "z", "ed0", "ed1")})
            if L in (2, 3):
                p = {**PASS[L - 1], **p}
            PASS.append(p)
        NODE = []
        for P in range(5):
            names = ["wl", "w", "pre", "y", "var", "std", "xn"]
            names += ["wt", "wc"] if P in (0, 1, 4) else []
            names += ["xt", "xtc", "pj", "po", "ps0", "ps1"] if P < 3 else []
            names += ["xt", "xtc", "ps0", "ps1"] if P == 3 else []
            names += ["xr0", "xr1", "st0", "st1"] if P != 2 else []
            names += ["den", "clr"] if P in (1, 2, 3) else []
            names += ["ch", "chd"] if P in (0, 4) else []
            NODE.append({k: sem(f"n_{k}{P}") for k in names})
        s_deg = sem("deg_moved")
        s_sq = sem("to_square_root")
        s_sqd = sem("square_root_taken")

        block = ctx.enter_context(nc.Block())
        nbar = {}

        def barrier(eng):
            k = nbar.get(id(eng), 0) + 1
            nbar[id(eng)] = k
            eng.drain()
            eng.sem_inc(bar, 1)
            eng.wait_ge(bar, 5 * k)
            eng.nop(nofuse=True)

        def softmax_batches(eng, L, body):
            U = SETS[L]
            loops = (NB - 2) // U
            body(0, 0, True, False)
            with eng.Fori(0, loops) as i:
                for o in range(1, U + 1):
                    body(i, o, True, True)
            for b in range(loops * U + 1, NB):
                body(0, b, True, True)
            body(0, NB, False, True)

        def batch_at(L, i, o):
            U = SETS[L]
            return i * U + o, o % U, i + o // U, o % 2, i * (U // 2) + o // 2

        def pipeline(eng, body):
            for m in range(6):
                body(0, m)
            with eng.Fori(3, NT // 2 - 2) as i:
                body(i, 0)
                body(i, 1)
            for m in range(NT - 4, NT + 4):
                body(0, m)

        def tile_of(i, off, skew):
            o = off - skew
            if isinstance(i, int):
                n = 2 * i + o
                return (0 <= n < NT), n, n % 2, n // 2
            return True, i * 2 + o, o % 2, i + o // 2

        @block.sync
        def _(sp):
            sp.wait_ge(s_const, 1)
            sp.nop(nofuse=True)
            C6 = 6 * 128
            for dst_v, name in ((raw_i, "src"), (raw_d, "dst"), (ewr, "edge_weight")):
                v = a[name]
                sp.dma_start(dst_v[:, 0:6, :], v[0:C6 * 128].rearrange("(c p e) -> p c e", p=128, e=128))\
                    .then_inc(s_prep_dma, 16)
                sp.dma_start(dst_v[0:FULL - C6, 6, :], v[C6 * 128:FULL * 128].rearrange("(p e) -> p e", e=128))\
                    .then_inc(s_prep_dma, 16)
                sp.dma_start(dst_v[FULL - C6:FULL - C6 + 1, 6, 0:REST],
                             v[FULL * 128:E].rearrange("(p e) -> p e", p=1)).then_inc(s_prep_dma, 16)
            dn = a["dst"]
            sp.dma_start(raw_n[:, 0:6, :], dn[1:C6 * 128 + 1].rearrange("(c p e) -> p c e", p=128, e=128))\
                .then_inc(s_prep_dma, 16)
            sp.dma_start(raw_n[0:FULL - C6, 6, :], dn[C6 * 128 + 1:FULL * 128 + 1].rearrange("(p e) -> p e", e=128))\
                .then_inc(s_prep_dma, 16)
            sp.dma_start(raw_n[FULL - C6:FULL - C6 + 1, 6, 0:REST - 1],
                         dn[FULL * 128 + 1:E].rearrange("(p e) -> p e", p=1)).then_inc(s_prep_dma, 16)
            with nc.allow_non_contiguous_dma("one number of each tile"):
                dv = a["dst"][0:FULL * 128].rearrange("(o t e) -> o t e", o=1, e=128)
                sp.dma_start(base_r[0:1, 0:FULL].unsqueeze(2), dv[:, :, 0:1]).then_inc(s_base, 16)
                sp.dma_start(base_r[0:1, FULL:FULL + 1], a["dst"][FULL * 128:FULL * 128 + 1].unsqueeze(0))\
                    .then_inc(s_base, 16)
                sp.dma_start(last_r[0:1, 0:FULL].unsqueeze(2), dv[:, :, 127:128]).then_inc(s_rowsdma, 16)
            sp.dma_start(x0[0:N, :], a["x"][:, :]).then_inc(s_x0, 16)
            sp.dma_start(x0[N:N + 128, :], zrow[:, :]).then_inc(s_x0, 16)
            sp.dma_start(x0[N + 128:NP, :], zrow[0:NP - N - 128, :]).then_inc(s_x0, 16)
            sp.wait_ge(s_prep, 1)
            sp.nop(nofuse=True)
            sp.dma_start(mk1[0:C6, :].rearrange("(c p) w -> p c w", p=128), mkr[:, 0:6, :]).then_inc(s_mkst, 16)
            sp.dma_start(mk1[C6:T, :], mkr[0:T - C6, 6, :]).then_inc(s_mkst, 16)
            sp.wait_ge(s_mkst, 32)
            mkb = mk1.rearrange("(b t) w -> b (t w)", t=G)
            for dstm, H in ((mk4, H2), (mk8, H1)):
                for h in range(H):
                    sp.dma_start(dstm[:, h, :, :].rearrange("b t w -> b (t w)"), mkb).then_inc(s_mkst, 16)
            sp.wait_ge(s_mkst, 16 * (2 + H1 + H2))
            sp.wait_ge(s_x0, 48)
            barrier(sp)
            mk_of = {1: mk8, 2: mk4, 3: mk1}
            for L in range(5):
                p, H = PASS[L], HEADS[L]
                if H:
                    mrows = mk_of[L].rearrange("b h t w -> (b h t) w") if L < 3 else mk1

                    def windows(i, o, scores, sums):
                        if not scores:
                            return
                        b, _, _, par, _ = batch_at(L, i, o)
                        wait(sp, p["w"], b + (past(L) + 1))
                        sp.nop(nofuse=True)
                        sp.dma_start(mk[0:G * H, par, :], mrows[ds(b * (G * H), G * H), :])\
                            .then_inc(p[f"mk{par}"], 16)
                        for k in range(G):
                            base = sp.value_load(base_r[0:1, ds(b * G + k, 1)], min_val=0, max_val=N)
                            if L == 1:
                                if k % 2 == 0:
                                    wait(sp, p["qe"], b * 8 + (k // 2 - 1))
                                    sp.nop(nofuse=True)
                                sp.dma_start(qw[:, k % 8, :], q_t[ds(base, 128), :])\
                                    .then_inc(p[f"qw{k // 2 % 4}"], 16)
                            else:
                                edt = ed1_t if L == 2 else ed2_t
                                sp.dma_start(edw[:, par, k, 0:H], edt[ds(base, 128), :])\
                                    .then_inc(p[f"ed{par}"], 16)
                    softmax_batches(sp, L, windows)
                barrier(sp)
                q = NODE[L]
                col = lambda v: v.rearrange("(k p) -> p k", p=128)
                bc = lambda v, w: v.rearrange("(o w) -> o w", o=1).to_broadcast([128, w])

                def load(dst_v, src_v):
                    sp.dma_start(dst_v, src_v).then_inc(q["wl"], 16)

                def rowsof(v):
                    return v.rearrange("(k p) w -> p k w", p=128)
                with nc.allow_non_contiguous_dma("vectors as columns"):
                    if L == 0:
                        for j in range(8):
                            load(wraw[32 * (j % 4):32 * (j % 4) + 32, 6 + j // 4, :], a["L0_gnn_weight"][:, :])
                        load(cols[:, :, 0], col(a["L0_gnn_gamma"]))
                        load(cols[:, :, 1], col(a["L0_gnn_beta"]))
                        load(wraw[:, 0:2, :], rowsof(a["L1_gnn_Wk"]))
                        load(wraw[:, 2:4, :], rowsof(a["L1_gnn_Wv"]))
                        load(wraw[:, 4:6, :], rowsof(a["L1_gnn_Wq"]))
                        load(brow[0:1, 0:256], a["L1_gnn_bk"].unsqueeze(0))
                        load(brow[0:1, 256:512], a["L1_gnn_bv"].unsqueeze(0))
                        load(brow[0:1, 512:768], a["L1_gnn_bq"].unsqueeze(0))
                    if L == 1:
                        load(wraw[:, 0:2, :], rowsof(a["L1_gnn_Wo"]))
                        load(wproj[:, :, 0:256], rowsof(a["L2_gnn_W1"]))
                        load(bo_b[:, :], bc(a["L1_gnn_bo"], 256))
                        load(as_b[:, :], a["L2_gnn_a1_src"].rearrange("(o h) w -> o (h w)", o=1).to_broadcast([128, 256]))
                        load(ad_b[:, :], a["L2_gnn_a1_dst"].rearrange("(o h) w -> o (h w)", o=1).to_broadcast([128, 256]))
                    if L == 2:
                        load(wproj[:, :, 0:256], rowsof(a["L2_gnn_W2"]))
                        load(bo_b[:, :], bc(a["L2_gnn_b1"], 256))
                        load(lg_b[:, :], bc(a["L2_gnn_ln_g"], 256))
                        load(lb_b[:, :], bc(a["L2_gnn_ln_b"], 256))
                        load(as_b[:, :], a["L2_gnn_a2_src"].to_broadcast([128, 256]))
                        load(ad_b[:, :], a["L2_gnn_a2_dst"].to_broadcast([128, 256]))
                        sp.dma_start(deg_d.unsqueeze(0), acc[4:5, 2, :]).then_inc(s_deg, 16)
                        sp.wait_ge(s_deg, 16)
                    if L == 3:
                        load(bo_b[:, :], bc(a["L2_gnn_b2"], 256))
                        load(dcol[:, :], deg_d.rearrange("(n p) -> p n", p=128))
                    if L == 4:
                        load(wraw[:, 0:2, :], rowsof(a["L3_gnn_W"]))
                        load(cols[:, :, 0], col(a["L3_gnn_gamma"]))
                        load(cols[:, :, 1], col(a["L3_gnn_beta"]))
                        load(cols[:, :, 2], col(a["L3_gnn_b"]))
                        load(dinv_b[:, :], bc(dinv_d, NP))
                    if L == 3:
                        sp.wait_ge(q["w"], 1)
                        sp.dma_start(dinv_d.rearrange("(n p) -> p n", p=128), dcol[:, :]).then_inc(s_deg, 16)
                        sp.wait_ge(s_deg, 32)
                resid = [x0, x1, None, x2, x3][L]
                keep = [x1, x2, None, x3, None][L]

                def moves(i, off):
                    ok, n, par, use = tile_of(i, off, 0)
                    if ok and resid is not None:
                        wait(sp, q["var"], n - 1)
                        sp.nop(nofuse=True)
                        sp.dma_start(xr[:, par, :], resid[ds(n * 128, 128), :]).then_inc(q[f"xr{par}"], 16)
                    ok, n, par, use = tile_of(i, off, 2)
                    if ok and L != 2:
                        wait(sp, q["xn"], n + 1)
                        sp.nop(nofuse=True)
                        if keep is not None:
                            sp.dma_start(keep[ds(n * 128, 128), :], xn[:, par, :]).then_inc(q[f"st{par}"], 16)
                            if L == 3:
                                sp.dma_start(xs_t[ds(n * 128, 128), :], xs[:, par, :]).then_inc(q[f"ps{par}"], 16)
                        elif not isinstance(n, int) or 128 * (n + 1) <= N:
                            sp.dma_start(out[ds(n * 128, 128), :], xn[:, par, :]).then_inc(q[f"st{par}"], 16)
                        elif 128 * n < N:
                            sp.dma_start(out[128 * n:N, :], xn[0:N - 128 * n, par, :]).then_inc(q[f"st{par}"], 16)
                        else:
                            sp.nop().then_inc(q[f"st{par}"], 16)
                    ok, n, par, use = tile_of(i, off, 4)
                    if ok and L < 3:
                        wait(sp, q["po"], n + 1)
                        sp.nop(nofuse=True)
                        rws = ds(n * 128, 128)
                        if L == 0:
                            sp.dma_start(kv_t[rws, :], po[:, par, 0:512]).then_inc(q[f"ps{par}"], 16)
                            sp.dma_start(q_t[rws, :], po[:, par, 512:768]).then_inc(q[f"ps{par}"], 16)
                        if L == 1:
                            sp.dma_start(g1_t[rws, :], po[:, par, 0:260]).then_inc(q[f"ps{par}"], 16)
                            sp.dma_start(ed1_t[rws, :], po[:, par, 260:264]).then_inc(q[f"ps{par}"], 16)
                        if L == 2:
                            sp.dma_start(g2_t[rws, :], po[:, par, 0:257]).then_inc(q[f"ps{par}"], 16)
                            sp.dma_start(ed2_t[rws, :], po[:, par, 257:258]).then_inc(q[f"ps{par}"], 16)
                pipeline(sp, moves)
                for par in range(2):
                    if L != 2:
                        sp.wait_ge(q[f"st{par}"], 16 * (NT // 2))
                    if L < 4:
                        sp.wait_ge(q[f"ps{par}"], 16 * (NT // 2) * (2 if L < 3 else 1))
                barrier(sp)

        @block.gpsimd
        def _(pool):
            nc.gpsimd.memset(raw_i[:, :, :], 0)
            nc.gpsimd.memset(raw_d[:, :, :], N)
            nc.gpsimd.memset(raw_n[:, :, :], N)
            nc.gpsimd.memset(ewr[:, :, :], 0.0)
            nc.gpsimd.memset(base_r[:, :], N)
            nc.gpsimd.memset(last_r[0:1, :], N)
            nc.gpsimd.memset(zrow[:, :], 0.0)
            pool.drain()
            pool.sem_inc(s_const, 1)
            nc.gpsimd.memset(src_c[:, T:T + G], 0)
            nc.gpsimd.memset(rel_c[:, T:T + G], 0.0)
            nc.gpsimd.memset(ew_c[:, T:T + G], 0.0)
            nc.gpsimd.memset(ident[:, :], 0.0)
            nc.gpsimd.memset(ones[:, :], 1.0)
            nc.gpsimd.memset(zeros[:, :], 0.0)
            nc.gpsimd.memset(selc8[:, :], 0.0)
            nc.gpsimd.memset(selc4[:, :], 0.0)
            nc.gpsimd.memset(seld8[:, :], 0.0)
            nc.gpsimd.memset(seld4[:, :], 0.0)
            nc.gpsimd.memset(degm[:, :], 1.0)
            nc.gpsimd.memset(w8[:, :, :, :], 1.0)
            nc.gpsimd.iota(iota[:, :], pattern=[[1, 128]], base=0, channel_multiplier=0,
                           allow_small_or_imprecise_dtypes=True)
            pool.drain()

            def ones_where(view_, pattern):
                nc.gpsimd.affine_select(out=view_, in_=view_, compare_op=ALU.not_equal, fill=1.0, base=0,
                                        pattern=pattern, channel_multiplier=1)
            ones_where(ident[:, :], [[-1, 128]])
            ones_where(selc8[:, 0:256].rearrange("p (g f) -> p g f", g=8), [[-G, 8], [0, 32]])
            ones_where(selc8[:, 256:384], [[-G, 128]])
            ones_where(selc4[:, 0:256].rearrange("p (g f) -> p g f", g=4), [[-G, 4], [0, 64]])
            ones_where(selc4[:, 256:384], [[-G, 128]])
            ones_where(seld8[:, :].rearrange("p (g f) -> p g f", g=8), [[-1, 8], [0, 32]])
            ones_where(seld4[:, :].rearrange("p (g f) -> p g f", g=4), [[-1, 4], [0, 64]])
            nc.gpsimd.memset(degm[:, 0:4], 0.0)
            pool.drain()
            nc.gpsimd.tensor_copy(ident_b[:, :], ident[:, :])
            nc.gpsimd.tensor_copy(iota_b[:, :], iota[:, :])
            nc.gpsimd.memset(acc[:, :, :], 0.0)
            pool.drain()
            pool.sem_inc(s_const, 1)
            barrier(pool)
            for L in range(5):
                p, W = PASS[L], WIDTH[L]
                nc.gpsimd.tensor_copy(stage[:, 0, :], src_c[:, 0:G]).then_inc(p["staged"], 1)
                with pool.Fori(0, NB // 4) as i:
                    for s in range(4):
                        if AHEAD[L] > 2:
                            for f in range(4):
                                f += (s + 1) % 4 * 4
                                pool.wait_ge(s_ring[f], i * 64 + ((s + 1) // 4 * 64 + ring_base(L, f)))
                            pool.nop(nofuse=True)
                        nc.gpsimd.tensor_copy(stage[:, (s + 1) % 4, :], src_c[:, ds(i * (4 * G) + (s + 1) * G, G)])\
                            .then_inc(p["staged"], 1)
                        for g in range(4):
                            pool.wait_ge(p["agg"], i * (4 * G) + (s * G + 4 * g + 4))
                            if g == 0:
                                pool.wait_ge(p["staged"], i * 4 + (s + 1 + (NB + 1) * L))
                            pool.nop(nofuse=True)
                            for j in range(4):
                                slot = (s % SETS[L]) * G + 4 * g + j
                                nc.gpsimd.indirect_dma_start(
                                    out=rings[L][:, slot, 0:W], out_offset=None, in_=table[L][:, :],
                                    in_offset=bass.IndirectOffsetOnAxis(
                                        ap=stage[:, s, 4 * g + j:4 * g + j + 1], axis=0))\
                                    .then_inc(s_ring[slot // 4], 16)
                barrier(pool)
                q = NODE[L]
                if L < 3:
                    def clear(i, off):
                        ok, n, par, use = tile_of(i, off, 1)
                        if ok:
                            wait(pool, q["pre"], n + 1)
                            nc.gpsimd.tensor_copy(acc[:, :, ds(n * 128, 128)],
                                                  zeros[:, :].unsqueeze(1).to_broadcast([128, 3, 128]))
                    if L == 2:
                        pool.wait_ge(s_deg, 16)
                    pipeline(pool, clear)
                barrier(pool)

        @block.scalar
        def _(act):
            barrier(act)
            for L in range(5):
                p, H = PASS[L], HEADS[L]
                R = G * H
                if H:
                    if L == 1:
                        act.sem_inc(p["ohtc"], 2)
                        act.sem_inc(p["w"], 2)

                    def turned(b):
                        for g in range(4):
                            wait(act, p["oht"], b * 4 + (4 * past(L) + g + 1))
                            if L == 1:
                                wait(act, p["qe"], b * 8 + (2 * g - 4))
                            elif g == 0:
                                wait(act, p["qeg"], b + NB * (L - 2))
                            act.activation(oht[:, g, :, :],
                                           ot[g % 2][:, 0:256].bitcast(BF16).rearrange("p (k j) -> p k j", k=4),
                                           ACT.Copy).then_inc(p["ohtc"], 1)
                    if L > 1:
                        turned(0)

                    def chain(i, o, scores, sums):
                        if not scores:
                            return
                        b, _, _, par, _ = batch_at(L, i, o)
                        if L == 1:
                            turned(b)
                        elif not isinstance(b, int) or b + 1 < NB:
                            turned(b + 1)
                        wait(act, p["ch3"], b + (past(L) + 1))
                        act.activation(px[0:R, :], dd[0:R, :], ACT.Exp)
                        act.activation(cl[0:R, 3:4], cl[0:R, 2:3], ACT.Exp).then_inc(p["px"], 1)
                        wait(act, p["pb"], b + (past(L) + 1))
                        act.activation(w8[:, par, :, 0:H],
                                       m0[:, 128:128 + R].rearrange("p (h t) -> p t h", h=H), ACT.Copy)
                        act.activation(corr[:, par, 0:3], m1[:, 264:267], ACT.Copy).then_inc(p["w"], 1)
                    softmax_batches(act, L, chain)
                barrier(act)
                q = NODE[L]
                if L in (0, 4):
                    act.sem_inc(q["ch"], 2)
                if L < 4:
                    act.sem_inc(q["xtc"], 2)
                if L in (0, 1, 4):
                    for m in range({0: 3, 1: 1, 4: 1}[L]):
                        act.wait_ge(q["wt"], m + 1)
                        dst_v = {0: wproj[:, :, 256 * m:256 * m + 256], 1: wout, 4: wout}[L]
                        scale = float(1.0 / (32.0 ** 0.5)) if (L == 0 and m == 2) else 1.0
                        act.activation(dst_v, ot[m % 2][:, :].rearrange("p (k f) -> p k f", k=2), ACT.Copy,
                                       scale=scale).then_inc(q["wc"], 1)
                    if L == 0:
                        act.wait_ge(q["wl"], 16 * 16)
                        act.activation(brow[0:1, 512:768], brow[0:1, 512:768], ACT.Copy,
                                       scale=float(1.0 / (32.0 ** 0.5))).then_inc(q["wc"], 1)
                if L in (0, 4):
                    if L == 0:
                        def keep_chunk(c, par):
                            act.wait_ge(q["chd"], c + 1)
                            act.activation(acc[:, 0:2, ds(c * CH, CH)],
                                           qe[par][:, 0:2 * CH].rearrange("p (k n) -> p k n", k=2), ACT.Copy)\
                                .then_inc(q["ch"], 1)
                        with act.Fori(0, NCH // 2) as i:
                            keep_chunk(i * 2, 0)
                            keep_chunk(i * 2 + 1, 1)
                        keep_chunk(NCH - 1, 0)
                    for m in {0: (1,), 4: (3,)}[L]:
                        act.wait_ge(s_sq, m)
                        act.activation(bn[:, :, 1], bn[:, :, 1], ACT.Sqrt).then_inc(s_sqd, 1)
                    act.wait_ge(q["w"], 1 if L == 4 else 2)
                if L == 0:
                    act.drain()
                    for k in range(2):
                        act.activation(acc[:, k, 0:N], acc[:, k, 0:N], ACT.Tanh,
                                       bias=bn[:, k, 3:4], scale=bn[:, k, 2:3])
                if L == 3:
                    act.wait_ge(s_sq, 2)
                    act.activation(rr[:, 0, 0:NT], rr[:, 0, 0:NT], ACT.Sqrt).then_inc(s_sqd, 1)
                act.drain()

                def stages(i, off):
                    ok, n, par, use = tile_of(i, off, 3)
                    if ok and L == 3:
                        wait(act, q["xt"], n + 1)
                        act.activation(acc[:, 0:2, ds(n * 128, 128)],
                                       (m0, m1)[par][:, 0:256].rearrange("p (k j) -> p k j", k=2), ACT.Copy)\
                            .then_inc(q["xtc"], 1)
                    if ok and L < 3:
                        wait(act, q["xt"], n + 1)
                        wait(act, q["pj"], n + 1)
                        act.activation(xt[:, par, :], (m0, m1)[par][:, 0:256], ACT.Copy)\
                            .then_inc(q["xtc"], 1)
                    ok, n, par, use = tile_of(i, off, 0)
                    if ok and L in (0, 4):
                        wait(act, q["y"], n + 1)
                        for k in range(2):
                            if L == 0:
                                ins = act.activation(pre[:, par, 128 * k:128 * k + 128],
                                                     acc[:, k, ds(n * 128, 128)], ACT.Copy)
                            else:
                                ins = act.activation(pre[:, par, 128 * k:128 * k + 128],
                                                     acc[:, k, ds(n * 128, 128)], ACT.Relu,
                                                     bias=bn[:, k, 3:4], scale=bn[:, k, 2:3])
                        ins.then_inc(q["pre"], 1)
                    ok, n, par, use = tile_of(i, off, 4)
                    if ok and L < 3:
                        wait(act, q["pj"], n + 3)
                        wait(act, q[f"ps{par}"], use * 32)
                        w1 = [512, 264, 258][L]
                        ins = act.activation(po[:, par, 0:w1], qe[par][:, 0:w1], ACT.Copy)
                        if L == 0:
                            ins = act.activation(po[:, par, 512:768], ag[par][:, 0:256], ACT.Copy)
                        ins.then_inc(q["po"], 1)
                    ok, n, par, use = tile_of(i, off, 1)
                    if ok:
                        act.wait_ge(q["var"], n + 1)
                        act.activation(lnst[:, par, 9:10], lnst[:, par, 8:9], ACT.Sqrt).then_inc(q["std"], 1)
                pipeline(act, stages)
                barrier(act)

        @block.tensor
        def _(pe):
            mm = nc.tensor.matmul
            tr = nc.tensor.transpose
            pe.wait_ge(s_const, 2)
            for c in range(21):
                which, c7 = divmod(c, 7)
                n = 128 if c7 < 6 else T - 6 * 128
                rows_v = (raw_f, relr, ewr)[which]
                if c7 == 0:
                    pe.wait_ge(s_prep, (2, 3, 3)[which])
                if c >= 2:
                    pe.wait_ge(s_prep_c, c - 1)
                tr(ot[c % 2][:, 0:n], rows_v[0:n, c7, :], ident[0:n, 0:n]).then_inc(s_prep_t, 1)
            barrier(pe)
            for L in range(5):
                p, H, PL = PASS[L], HEADS[L], PLANES[L]
                R = G * H
                pe.sem_inc(p["agg"], G * AHEAD[L])
                if L == 1:
                    pe.sem_inc(p["qe"], 2)
                rg = rings[L]
                vo = 256 if L == 1 else 0

                def add_tile(b, rset, k, use):
                    if k % 4 == 0:
                        pe.wait_ge(p["wready"], b * 4 + (k // 4 + 1 + groups_before(L)))
                    slot = rset * G + k
                    one_hot = ohc[:, k // 4 % 2, k % 4, :]
                    if not H and k % 4 == 0:
                        pe.wait_ge(s_ring[slot // 4], use * 64 + (64 + ring_base(L, slot // 4)))
                    pe.wait_ge(p["added"], b * G + (k + 1 + T * L))
                    for c in range(2):
                        ins = mm(ag[k % 2][:, 128 * c:128 * c + 128], rg[:, slot, vo + 128 * c:vo + 128 * c + 128],
                                 one_hot, start=True, stop=True)
                    if H > 1:
                        ins = mm(ag[k % 2][0:8, 256:384], w8[:, rset % 2, k, :], one_hot, start=True, stop=True)
                    elif H == 1:
                        ins = mm(ag[k % 2][:, 256:384], ones[:, :], one_hot, start=True, stop=True)
                    ins.then_inc(p["agg"], 1)

                if not H:
                    with pe.Fori(0, NB // 4) as i:
                        for rset in range(4):
                            for k in range(G):
                                add_tile(i * 4 + rset, rset, k, i)
                else:
                    def turn(b, g):
                        pe.wait_ge(p["oh"], b * 4 + (4 * past(L) + g + 1))
                        pe.wait_ge(p["ohtc"], b * 4 + (4 * past(L) + g + 1))
                        for j in range(4):
                            ins = tr(ot[g % 2][:, 64 * j:64 * j + 64].bitcast(BF16), ohb[:, g % 2, j, :],
                                     ident_b[:, :])
                        ins.then_inc(p["oht"], 1)

                    def dest_scores(b, par, ub):
                        gate(pe, p["ohtc"], b * 4 + (4 * past(L) + 6))
                        pe.wait_ge(p[f"ed{par}"], ub * 256 + (256 + 128 * past(L - 1)))
                        gate(pe, p["z"], b + (past(L - 1) + 1))
                        for k in range(G):
                            ins = mm(qe[par][:, k * H:k * H + H], oht[:, k // 4, k % 4, :],
                                     edw[:, par, k, 0:H], start=True, stop=True)
                        ins.then_inc(p["qeg"], 1)
                    if L > 1:
                        for g in range(4):
                            turn(0, g)
                        dest_scores(0, 0, 0)

                    def batch(i, o, scores, sums):
                        b, _, _, par, _ = batch_at(L, i, o)
                        c, cset, cu, _, _ = batch_at(L, i, o - 1)
                        nb, _, _, npar, nub = batch_at(L, i, o + 1)
                        feed = L > 1 and scores and (not isinstance(b, int) or b + 1 < NB)
                        if scores:
                            if L == 1:
                                for g in range(5):
                                    if g < 4:
                                        turn(b, g)
                                    if g > 0:
                                        f = g - 1
                                        gate(pe, p["ohtc"], b * 4 + (4 * past(L) + f + 3))
                                        for r in (2 * f, 2 * f + 1):
                                            pe.wait_ge(p["prod"], b * 8 + r + 1)
                                            pe.wait_ge(p[f"qw{r % 4}"], b * 64 + 32 * (r // 4) + 32)
                                            for j in range(2):
                                                k = 2 * r + j
                                                ins = mm(qe[r % 2][:, 256 * j:256 * j + 256],
                                                         oht[:, f, k % 4, :], qw[:, k % 8, :],
                                                         start=True, stop=True)
                                            ins.then_inc(p["qe"], 1)
                            gate(pe, p["w"], b + (past(L) + 2))
                            gate(pe, p["s"], b + (past(L) + 1))
                            tr(m0[0:R, 0:128], sc[:, par, 0:R], ident[:, :]).then_inc(p["st"], 1)
                        for k in range(G):
                            if sums:
                                add_tile(c, cset, k, None)
                            if feed and k in (2, 4, 8, 11):
                                turn(nb, (2, 4, 8, 11).index(k))
                            if scores and k == 5:
                                gate(pe, p["ch1"], b + (past(L) + 1))
                                mm(m1[0:1, 0:R], mx[0:R, 0:1], ident[0:R, 0:R], start=True, stop=True)
                                mm(m1[0:1, 128:128 + R], mx[0:R, 127:128], ident[0:R, 0:R], start=True, stop=True)\
                                    .then_inc(p["row"], 1)
                            if scores and k == 9:
                                gate(pe, p["ch2"], b + (past(L) + 1))
                                mm(m1[0:R, 256:257], rows[0:1, 5, 0:R], ones[0:1, 0:1], start=True, stop=True)
                                mm(m1[0:R, 257:258], rows[0:1, 4, 0:R], ones[0:1, 0:1], start=True, stop=True)\
                                    .then_inc(p["col"], 1)
                            if scores and k == 13:
                                gate(pe, p["px"], b + (past(L) + 1))
                                tr(m0[:, 128:128 + R], px[0:R, :], ident[0:R, 0:R])
                                for f in range(3):
                                    if H == 1:
                                        ins = mm(m1[:, 264 + f:265 + f], ones[0:1, :], cl[0:1, 3:4],
                                                 start=True, stop=True)
                                    else:
                                        add = H == H2 and f == 2
                                        ins = mm(m1[:, 264 + f:265 + f], selc[H][0:R, 128 * f:128 * f + 128],
                                                 cl[0:R, 3:4], start=True, stop=not add)
                                        if add:
                                            ins = mm(m1[:, 264 + f:265 + f], degm[0:1, :], ones[0:1, 0:1],
                                                     start=False, stop=True)
                                ins.then_inc(p["pb"], 1)
                        if feed:
                            dest_scores(nb, npar, nub)
                    softmax_batches(pe, L, batch)
                barrier(pe)
                q = NODE[L]
                if L in (0, 1, 4):
                    pe.wait_ge(q["wl"], 16 * {0: 16, 1: 5, 4: 5}[L])
                    for m in range({0: 3, 1: 1, 4: 1}[L]):
                        if m >= 2:
                            pe.wait_ge(q["wc"], m - 1)
                        for kc in range(2):
                            for oc in range(2):
                                ins = tr(ot[m % 2][:, 256 * kc + 128 * oc:256 * kc + 128 * oc + 128],
                                         wraw[:, 2 * m + oc, 128 * kc:128 * kc + 128], ident[:, :])
                        ins.then_inc(q["wt"], 1)
                    pe.wait_ge(q["wc"], {0: 4, 1: 1, 4: 1}[L])
                if L in (0, 4):
                    if L == 0:
                        pe.wait_ge(q["w"], 1)

                    def project(c, par):
                        pe.wait_ge(q["ch"], c + 1)
                        for oc in range(2):
                            for kc in range(2):
                                ins = mm(qe[par][:, CH * oc:CH * oc + CH], wout[:, kc, 128 * oc:128 * oc + 128],
                                         acc[:, kc, ds(c * CH, CH)], start=kc == 0, stop=kc == 1)
                        ins.then_inc(q["chd"], 1)
                    with pe.Fori(0, NCH // 2) as i:
                        project(i * 2, 0)
                        project(i * 2 + 1, 1)
                    project(NCH - 1, 0)
                pe.sem_inc(q["y"], 2)
                if L < 3:
                    pe.sem_inc(q["pj"], 2)

                def stages(i, off):
                    ok, n, par, use = tile_of(i, off, 0)
                    if ok and L in (1, 2):
                        if isinstance(n, int) and n == 0:
                            pe.wait_ge(q["clr"], 1)
                        wait(pe, q["pre"], n - 1)
                        pe.nop(nofuse=True)
                        for c in range(2):
                            ins = mm(ag[par][:, 128 * c:128 * c + 128], seld[H][0:H, 128 * c:128 * c + 128],
                                     acc[0:H, 2, ds(n * 128, 128)], start=True, stop=True)
                        ins.then_inc(q["den"], 1)
                    ok, n, par, use = tile_of(i, off, 3)
                    if ok and L < 4:
                        pe.wait_ge(q["xn"], n + 1)
                        pe.wait_ge(q["xtc"], n + 1)
                        for c in range(2):
                            ins = tr((m0, m1)[par][:, 128 * c:128 * c + 128],
                                     (xs if L == 3 else xn)[:, par, 128 * c:128 * c + 128], ident[:, :])
                        ins.then_inc(q["xt"], 1)
                    ok, n, par, use = tile_of(i, off, 1)
                    if ok:
                        pe.wait_ge(q["pre"], n + 1)
                        wait(pe, q["var"], n - 1)
                        if L == 1:
                            for c in range(2):
                                ins = mm(ot[par][:, 0:256], pre[:, par, 128 * c:128 * c + 128], wout[:, c, :],
                                         start=c == 0, stop=c == 1)
                        else:
                            for c in range(2):
                                ins = tr(ot[par][:, 128 * c:128 * c + 128], pre[:, par, 128 * c:128 * c + 128],
                                         ident[:, :])
                        ins.then_inc(q["y"], 1)
                    ok, n, par, use = tile_of(i, off, 3)
                    if ok and L < 3:
                        pe.wait_ge(q["xtc"], n + 3)
                        wait(pe, q["po"], n - 1)
                        if L:
                            pe.wait_ge(q["w"], 1)
                        w1 = [512, 264, 258][L]
                        xv = xt[:, par, :]
                        for c in range(2):
                            ins = mm(qe[par][:, 0:w1], xv[:, 128 * c:128 * c + 128], wproj[:, c, 0:w1],
                                     start=c == 0, stop=(c == 1 and L > 0))
                        if L == 0:
                            mm(qe[par][:, 0:512], ones[0:1, :], brow[0:1, 0:512], start=False, stop=True)
                            for c in range(2):
                                mm(ag[par][:, 0:256], xv[:, 128 * c:128 * c + 128],
                                   wproj[:, c, 512:768], start=c == 0, stop=False)
                            ins = mm(ag[par][:, 0:256], ones[0:1, :], brow[0:1, 512:768],
                                     start=False, stop=True)
                        ins.then_inc(q["pj"], 1)
                pipeline(pe, stages)
                barrier(pe)

        @block.vector
        def _(dve):
            v = nc.vector
            tt = v.tensor_tensor
            dve.wait_ge(s_prep_dma, 12 * 16)
            v.tensor_copy(raw_f[:, :, :], raw_i[:, :, :])
            v.tensor_copy(relr[:, :, :], raw_d[:, :, :])
            dve.drain()
            tt(relr[:, :, :], relr[:, :, :], raw_d[:, :, 0:1].to_broadcast([128, 7, 128]), ALU.subtract)
            v.memset(mkr[:, :, 0:1], 0.0)
            v.memset(mkr[:, :, 128:129], 0.0)
            dve.drain()
            tt(mkr[:, :, 1:128], relr[:, :, 1:128], relr[:, :, 0:127], ALU.not_equal)
            v.tensor_scalar(mkr[:, :, 129:257], relr[:, :, :], 0.0, -BIG, ALU.not_equal, ALU.mult)
            tt(mkr[:, :, 257:385], relr[:, :, :], relr[:, :, 127:128].to_broadcast([128, 7, 128]), ALU.not_equal)
            tt(mkr[:, :, 385:513], raw_d[:, :, :], raw_n[:, :, :], ALU.not_equal)
            v.tensor_scalar(lt[:, :, :], raw_d[:, :, :], float(LOOPS2), LN2, ALU.is_lt, ALU.mult)
            dve.drain()
            tt(mkr[:, :, 385:513], mkr[:, :, 385:513], lt[:, :, :], ALU.mult)
            v.tensor_scalar(mkr[:, :, 1:128], mkr[:, :, 1:128], -BIG, None, ALU.mult)
            v.tensor_scalar(mkr[:, :, 257:385], mkr[:, :, 257:385], -BIG, None, ALU.mult)
            dve.drain()
            dve.sem_inc(s_prep, 3)
            for c in range(21):
                which, c7 = divmod(c, 7)
                n = 128 if c7 < 6 else T - 6 * 128
                dst_v = (src_c, rel_c, ew_c)[which]
                dve.wait_ge(s_prep_t, c + 1)
                v.tensor_copy(dst_v[:, 128 * c7:128 * c7 + n], ot[c % 2][:, 0:n]).then_inc(s_prep_c, 1)
            dve.wait_ge(s_base, 32)
            dve.wait_ge(s_rowsdma, 16)
            tt(cneg_r[:, 1:T], base_r[:, 1:T], last_r[0:1, 0:T - 1], ALU.not_equal)
            tt(sneg_r[:, :], base_r[:, :], last_r[0:1, :], ALU.not_equal)
            v.memset(cneg_r[:, 0:1], 1.0)
            for k in range(2):
                v.memset(ag[k][:, :], 0.0)
            dve.drain()
            tt(sneg_r[:, :], sneg_r[:, :], cneg_r[:, :], ALU.add)
            dve.drain()
            v.tensor_scalar(cneg_r[:, :], cneg_r[:, :], -BIG, None, ALU.mult)
            v.tensor_scalar(sneg_r[:, :], sneg_r[:, :], -BIG, None, ALU.mult)
            barrier(dve)
            for L in range(5):
                p, H, PL = PASS[L], HEADS[L], PLANES[L]
                R = G * H
                if L == 0:
                    dve.sem_inc(p["added"], 2)

                rg = rings[L]

                def add_window(b, k):
                    base = dve.value_load(base_r[0:1, ds(b * G + k, 1)], min_val=0, max_val=N)
                    win = acc[:, 0:PL, ds(base, 128)]
                    dve.wait_ge(p["agg"], b * G + (k + 1 + G * AHEAD[L]))
                    dve.wait_ge(p["added"], b * G + (k + 2 + T * L))
                    tt(win, win, ag[k % 2][:, 0:128 * PL].rearrange("p (c j) -> p c j", c=PL), ALU.add)\
                        .then_inc(p["added"], 1)

                def one_hots(rel, g, weight):
                    for k in range(4 * g, 4 * g + 4):
                        if weight is None:
                            ins = v.tensor_scalar(ohc[:, g % 2, k % 4, :], iota[:, :], rel(k), None, ALU.is_equal)
                        else:
                            ins = v.tensor_scalar(ohc[:, g % 2, k % 4, :], iota[:, :], rel(k),
                                                  weight(k), ALU.is_equal, ALU.mult)
                    return ins

                if not H:
                    def hots(b, g):
                        wt = (lambda k: ew_c[:, ds(b * G + k, 1)]) if L == 0 else None
                        one_hots(lambda k: rel_c[:, ds(b * G + k, 1)], g, wt).then_inc(p["wready"], 1)
                    hots(0, 0)
                    with dve.Fori(0, NB // 4) as i:
                        for u in range(4):
                            b = i * 4 + u
                            for g in range(4):
                                if g < 3:
                                    hots(b, g + 1)
                                else:
                                    hots(b + 1, 0)
                                for k in range(4 * g, 4 * g + 4):
                                    add_window(b, k)
                else:
                    if L == 2:
                        dve.sem_inc(p["z"], 2)
                    if L == 1:
                        dve.sem_inc(p["prod"], 2)
                        dve.sem_inc(p["red"], 2)
                    if L == 2:
                        v.memset(w8[:, :, :, :], 1.0)
                    v.memset(fprev[:, :], -BIG)
                    v.memset(rows[:, :, :], -2.0 * BIG)

                    def keep_rel(b, rset):
                        v.tensor_copy(rel_s[:, rset, :], rel_c[:, ds(b * G, G)])

                    def hots_to_turn(b, rset, g):
                        wait(dve, p["oht"], b * 4 + (4 * past(L) + g - 1))
                        for k in range(4 * g, 4 * g + 4):
                            ins = v.tensor_scalar(ohb[:, g % 2, k % 4, :], iota_b[:, :],
                                                  rel_s[:, rset, k:k + 1], None, ALU.is_equal)
                        ins.then_inc(p["oh"], 1)

                    def scores_of(b, rset, use, par):
                        if L == 1:
                            for g in range(4):
                                hots_to_turn(b, rset, g)
                        sv = sc[:, par, 0:R].rearrange("p (h t) -> p t h", h=H)

                        def ready(k):
                            dve.wait_ge(s_ring[rset * 4 + k // 4], use * 64 + (64 + ring_base(L, rset * 4 + k // 4)))
                        if L == 1:
                            def reduce(r):
                                dve.wait_ge(p["prod"], b * 8 + (r + 3))
                                ins = v.tensor_reduce(
                                    sv[:, 2 * r:2 * r + 2, :],
                                    prod[:, r % 2, :, :].rearrange("p t (h d) -> p t h d", h=H), AX.X, ALU.add)
                                ins.then_inc(p["red"], 1)
                            for r in range(8):
                                if r % 2 == 0:
                                    ready(2 * r)
                                dve.wait_ge(p["qe"], b * 8 + (r + 3))
                                dve.wait_ge(p["red"], b * 8 + (r + 1))
                                tt(prod[:, r % 2, :, :], qe[r % 2][:, :].rearrange("p (t w) -> p t w", t=2),
                                   rg[:, rset * G + 2 * r:rset * G + 2 * r + 2, 0:256], ALU.mult)\
                                    .then_inc(p["prod"], 1)
                                if r:
                                    reduce(r - 1)
                            reduce(7)
                        else:
                            for k in range(0, G, 4):
                                ready(k)
                            dve.wait_ge(p["qeg"], b + (NB * (L - 2) + 1))
                            tt(sv, qe[par][:, 0:R].rearrange("p (t h) -> p t h", h=H),
                               rg[:, rset * G:rset * G + G, 256:256 + H], ALU.add).then_inc(p["z"], 1)
                            dve.drain()
                            v.scalar_tensor_tensor(sc[:, par, 0:R], sc[:, par, 0:R], 0.2, sc[:, par, 0:R],
                                                   ALU.mult, ALU.max)
                        dve.drain()
                        dve.sem_inc(p["s"], 1)

                    def ch1(b, par, ub):
                        dve.wait_ge(p[f"mk{par}"], ub * 16 + (16 + 8 * past(L)))
                        dve.wait_ge(p["st"], b + (past(L) + 1))
                        v.tensor_tensor_scan(out=fw[0:R, :], data0=mk[0:R, par, 0:128], data1=m0[0:R, 0:128],
                                             initial=-BIG, op0=ALU.add, op1=ALU.max)
                        dve.drain()
                        v.tensor_tensor_scan(out=mx[0:R, ::-1], data0=mk[0:R, par, 1:129][:, ::-1],
                                             data1=fw[0:R, ::-1], initial=-BIG, op0=ALU.add, op1=ALU.max)\
                            .then_inc(p["ch1"], 1)

                    def ch2(b, par, ub):
                        hv = lambda k: rows[0:1, k, 0:R].rearrange("p (h t) -> p h t", h=H)
                        nb = lambda r_, o, n: r_[0:1, ds(b * G + o, n)].unsqueeze(1).to_broadcast([1, H, n])
                        head = m1[0:1, 0:R].rearrange("p (h t) -> p h t", h=H)
                        tail = m1[0:1, 128:128 + R].rearrange("p (h t) -> p h t", h=H)
                        fp = fprev[0:1, 0:H].unsqueeze(2)
                        v.tensor_copy(hv(0)[:, :, 1:G], nb(sneg_r, 1, G - 1))
                        tt(hv(6)[:, :, 0:1], fp, nb(sneg_r, 0, 1), ALU.add)
                        dve.wait_ge(p["row"], b + (past(L) + 1))
                        v.tensor_copy(hv(1), tail)
                        tt(hv(2)[:, :, 0:G - 1], head[:, :, 1:G], nb(cneg_r, 1, G - 1), ALU.add)
                        tt(hv(5)[:, :, 0:1], fp, nb(cneg_r, 0, 1), ALU.add)
                        dve.drain()
                        tt(hv(1)[:, :, 0:1], hv(1)[:, :, 0:1], hv(6)[:, :, 0:1], ALU.max)
                        v.tensor_tensor_scan(out=rows[0:1, 3, 0:R][:, ::-1], data0=rows[0:1, 0, 1:R + 1][:, ::-1],
                                             data1=rows[0:1, 2, 0:R][:, ::-1], initial=-BIG,
                                             op0=ALU.add, op1=ALU.max)
                        dve.drain()
                        v.tensor_tensor_scan(out=rows[0:1, 4, 0:R], data0=rows[0:1, 0, 0:R],
                                             data1=rows[0:1, 1, 0:R], initial=-BIG, op0=ALU.add, op1=ALU.max)
                        dve.drain()
                        tt(rows[0:1, 4, 0:R], rows[0:1, 4, 0:R], rows[0:1, 3, 0:R], ALU.max)
                        dve.drain()
                        tt(hv(5)[:, :, 1:G], hv(4)[:, :, 0:G - 1], nb(cneg_r, 1, G - 1), ALU.add)
                        v.tensor_copy(fp, hv(4)[:, :, G - 1:G])
                        dve.drain()
                        dve.sem_inc(p["ch2"], 1)

                    def ch3(b, par, ub):
                        dve.wait_ge(p["col"], b + (past(L) + 1))
                        v.tensor_copy(cl[0:R, 0:2], m1[0:R, 256:258])
                        dve.drain()
                        v.scalar_tensor_tensor(m2[0:R, :], mk[0:R, par, 129:257], cl[0:R, 0:1], mx[0:R, :],
                                               ALU.add, ALU.max)
                        dve.drain()
                        v.scalar_tensor_tensor(m2[0:R, :], mk[0:R, par, 257:385], cl[0:R, 1:2], m2[0:R, :],
                                               ALU.add, ALU.max)
                        dve.drain()
                        tt(dd[0:R, :], m0[0:R, 0:128], m2[0:R, :], ALU.subtract)
                        tt(cl[0:R, 2:3], cl[0:R, 0:1], m2[0:R, 0:1], ALU.subtract)
                        dve.drain()
                        if L > 1:
                            tt(dd[0:R, :], dd[0:R, :], mk[0:R, par, 385:513], ALU.add)
                            dve.drain()
                        dve.sem_inc(p["ch3"], 1)

                    def weigh(rset, par, g):
                        rel = lambda k: rel_s[:, rset, k:k + 1]
                        if H == 1:
                            ins = one_hots(rel, g, lambda k: w8[:, par, k, 0:1])
                        else:
                            one_hots(rel, g, None)
                            o = 256 if L == 1 else 0
                            for k in range(4 * g, 4 * g + 4):
                                vv = rg[:, rset * G + k, o:o + 256].rearrange("p (h d) -> p h d", h=H)
                                wv = w8[:, par, k, 0:H].unsqueeze(2).to_broadcast([128, H, 256 // H])
                                ins = tt(vv, vv, wv, ALU.mult)
                        ins.then_inc(p["wready"], 1)
                    ahead = 1 if L == 1 else 2
                    for m in range(ahead):
                        keep_rel(m, m)
                    dve.drain()
                    if L > 1:
                        for g in range(4):
                            hots_to_turn(0, 0, g)

                    def batch(i, o, scores, sums):
                        b, rset, use, par, ub = batch_at(L, i, o)
                        c, cset, _, cp, _ = batch_at(L, i, o - 1)
                        if scores:
                            scores_of(b, rset, use, par)
                        if sums:
                            dve.wait_ge(p["w"], c + (past(L) + 3))
                            base = dve.value_load(base_r[0:1, ds(c * G, 1)], min_val=0, max_val=N)
                            colv = acc[:, 0:3, ds(base, 1)]
                            dve.wait_ge(p["added"], c * G + (2 + T * L))
                            tt(colv, colv, corr[:, cp, 0:3].unsqueeze(2), ALU.mult)
                            weigh(cset, cp, 0)
                            dve.drain()
                        for g in range(4):
                            if L > 1 and scores and (not isinstance(b, int) or b + 1 < NB):
                                hots_to_turn(b + 1, (rset + 1) % 4, g)
                            if sums:
                                if g < 3:
                                    weigh(cset, cp, g + 1)
                                for k in range(4 * g, 4 * g + 4):
                                    add_window(c, k)
                            if scores and g == 2 and (not isinstance(b, int) or b + ahead < NB):
                                keep_rel(b + ahead, (rset + ahead) % SETS[L])
                            if scores and g < 3:
                                (ch1, ch2, ch3)[g](b, par, ub)
                    softmax_batches(dve, L, batch)
                barrier(dve)
                q = NODE[L]
                if L == 0:
                    dve.wait_ge(q["wl"], 16 * 16)
                    for j in range(8):
                        kc, pp = j // 4, 32 * (j % 4)
                        for i8 in range(8):
                            c = OCT_IDX[i8][j]
                            v.tensor_scalar(wout[pp:pp + 32, kc, 32 * i8:32 * i8 + 32],
                                            wraw[pp:pp + 32, 6 + kc, 32 * c:32 * c + 32],
                                            float(OCT_SIGN[i8][j]), None, ALU.mult)
                    dve.drain()
                    dve.sem_inc(q["w"], 1)
                if L in (1, 2):
                    dve.wait_ge(q["wl"], 16 * {1: 5, 2: 6}[L])
                    Hn = HEADS[L + 1]
                    for kc in range(2):
                        for s_, av in ((0, as_b), (1, ad_b)):
                            tt(wtmp[:, :], wproj[:, kc, 0:256], av[:, :], ALU.mult)
                            dve.drain()
                            v.tensor_reduce(wproj[:, kc, 256 + Hn * s_:256 + Hn * s_ + Hn],
                                            wtmp[:, :].rearrange("p (h d) -> p h d", h=Hn), AX.X, ALU.add)
                            dve.drain()
                    dve.sem_inc(q["w"], 1)
                if L == 3:
                    dve.wait_ge(q["wl"], 32)
                    v.tensor_scalar(dcol[:, :], dcol[:, :], 1.0, None, ALU.add)
                    dve.drain()
                    v.tensor_scalar(rr[:, 0, 0:NT], dcol[:, :], 1.0, None, ALU.max).then_inc(s_sq, 1)
                    v.tensor_scalar(dcol[:, :], dcol[:, :], 0.0, None, ALU.is_gt)
                    dve.wait_ge(s_sqd, 2)
                    v.reciprocal(rr[:, 1, 0:NT], rr[:, 0, 0:NT])
                    dve.drain()
                    tt(dcol[:, :], dcol[:, :], rr[:, 1, 0:NT], ALU.mult)
                    dve.drain()
                    dve.sem_inc(q["w"], 1)
                if L in (0, 4):
                    if L == 4:
                        dve.wait_ge(q["wl"], 16 * 5)

                    def measure(c, par):
                        if L == 4:
                            dve.wait_ge(q["chd"], c + 1)
                        else:
                            dve.wait_ge(q["ch"], c + 3)
                        zv = qe[par][:, 0:2 * CH].rearrange("p (k n) -> p k n", k=2)
                        if L == 4:
                            dst_v = acc[:, 0:2, ds(c * CH, CH)]
                            tt(dst_v, zv, dinv_b[:, ds(c * CH, CH)].unsqueeze(1).to_broadcast([128, 2, CH]), ALU.mult)
                            dve.drain()
                            dve.sem_inc(q["ch"], 1)
                            for k in range(2):
                                v.tensor_scalar(acc[:, k, ds(c * CH, CH)], acc[:, k, ds(c * CH, CH)],
                                                cols[:, k, 2:3], None, ALU.add)
                            dve.drain()
                            for k in range(2):
                                v.bn_stats(stats[:, k, ds(c * 6, 6)], acc[:, k, ds(c * CH, CH)])
                        else:
                            for k in range(2):
                                v.bn_stats(stats[:, k, ds(c * 6, 6)], acc[:, k, ds(c * CH, CH)])
                    with dve.Fori(0, NCH // 2) as i:
                        measure(i * 2, 0)
                        measure(i * 2 + 1, 1)
                    measure(NCH - 1, 0)
                    dve.drain()
                    for k in range(2):
                        v.bn_aggr(bn[:, k, 0:2], stats[:, k, :])
                    dve.drain()
                    v.tensor_scalar(bn[:, :, 1], bn[:, :, 1], EPS, None, ALU.add).then_inc(s_sq, 1)
                    dve.wait_ge(s_sqd, 1 if L == 0 else 3)
                    v.reciprocal(bn[:, :, 1], bn[:, :, 1])
                    dve.drain()
                    for k in range(2):
                        tt(bn[:, k, 2:3], bn[:, k, 1:2], cols[:, k, 0:1], ALU.mult)
                    dve.drain()
                    for k in range(2):
                        tt(bn[:, k, 0:1], bn[:, k, 0:1], bn[:, k, 2:3], ALU.mult)
                    dve.drain()
                    for k in range(2):
                        tt(bn[:, k, 3:4], cols[:, k, 1:2], bn[:, k, 0:1], ALU.subtract)
                    dve.drain()
                    dve.sem_inc(q["w"], 1)
                if L in (1, 2, 3):
                    den = acc[0:H, 2, :] if L < 3 else acc[:, 2, :]
                    v.tensor_scalar(den, den, 0.5, None, ALU.max)
                    dve.drain()
                    v.reciprocal(den, den)
                    dve.drain()
                    dve.sem_inc(q["clr"], 1)

                def stages(i, off):
                    ok, n, par, use = tile_of(i, off, 0)
                    if ok and L in (1, 2, 3):
                        if L < 3:
                            dve.wait_ge(q["den"], n + 1)
                            dn = ag[par][:, 0:256].rearrange("p (k j) -> p k j", k=2)
                        else:
                            dn = acc[:, 2, ds(n * 128, 128)].unsqueeze(1).to_broadcast([128, 2, 128])
                        dve.wait_ge(q["y"], n + 1)
                        tt(pre[:, par, :].rearrange("p (k j) -> p k j", k=2), acc[:, 0:2, ds(n * 128, 128)], dn,
                           ALU.mult).then_inc(q["pre"], 1)
                    ok, n, par, use = tile_of(i, off, 1)
                    if ok:
                        dve.wait_ge(q["y"], n + 3)
                        wait(dve, q["xn"], n - 1)
                        if L in (1, 2, 3):
                            tt(rr[:, par, :], ot[par][:, 0:256], bo_b[:, :], ALU.add)
                            dve.drain()
                        if L != 2:
                            dve.wait_ge(q[f"xr{par}"], use * 16 + 16)
                            v.scalar_tensor_tensor(rr[:, par, :], xr[:, par, :], 2.0 if L == 4 else 1.0,
                                                   rr[:, par, :] if L in (1, 3) else ot[par][:, 0:256],
                                                   ALU.mult, ALU.add)
                            dve.drain()
                        v.bn_stats(lnst[:, par, 0:6], rr[:, par, :])
                        dve.drain()
                        v.bn_aggr(lnst[:, par, 6:8], lnst[:, par, 0:6])
                        dve.drain()
                        v.tensor_scalar(lnst[:, par, 8:9], lnst[:, par, 7:8], EPS, None, ALU.add)\
                            .then_inc(q["var"], 1)
                    ok, n, par, use = tile_of(i, off, 2)
                    if ok:
                        dve.wait_ge(q["std"], n + 1)
                        v.reciprocal(lnst[:, par, 10:11], lnst[:, par, 9:10])
                        if L != 2:
                            wait(dve, q[f"st{par}"], use * 16)
                        if L < 4:
                            wait(dve, q["xt"], n - 1)
                        dve.nop(nofuse=True)
                        dve.drain()
                        ins = v.tensor_scalar(xn[:, par, :], rr[:, par, :], lnst[:, par, 6:7], lnst[:, par, 10:11],
                                              ALU.subtract, ALU.mult)
                        if L == 2:
                            dve.drain()
                            tt(xn[:, par, :], xn[:, par, :], lg_b[:, :], ALU.mult)
                            dve.drain()
                            tt(xn[:, par, :], xn[:, par, :], lb_b[:, :], ALU.add)
                            dve.drain()
                            ins = v.tensor_scalar(xn[:, par, :], xn[:, par, :], 0.0, None, ALU.max)
                        if L == 3:
                            dve.drain()
                            wait(dve, q[f"ps{par}"], use * 16)
                            ins = v.tensor_scalar(xs[:, par, :], xn[:, par, :], dcol[:, ds(n, 1)], None, ALU.mult)
                        ins.then_inc(q["xn"], 1)
                if L == 3:
                    dve.wait_ge(s_deg, 32)
                dve.drain()
                pipeline(dve, stages)
                barrier(dve)


_INS = ["x", "src", "dst", "edge_weight", "L0_gnn_weight", "L0_gnn_gamma", "L0_gnn_beta",
        "L1_gnn_Wq", "L1_gnn_bq", "L1_gnn_Wk", "L1_gnn_bk", "L1_gnn_Wv", "L1_gnn_bv", "L1_gnn_Wo", "L1_gnn_bo",
        "L2_gnn_W1", "L2_gnn_a1_src", "L2_gnn_a1_dst", "L2_gnn_b1", "L2_gnn_ln_g", "L2_gnn_ln_b", "L2_gnn_W2",
        "L2_gnn_a2_src", "L2_gnn_a2_dst", "L2_gnn_b2", "L3_gnn_W", "L3_gnn_b", "L3_gnn_gamma", "L3_gnn_beta"]


def kernel(**inputs):
    import numpy as _np
    import concourse.bacc as _bacc
    from concourse.bass_utils import run_bass_kernel_spmd as _run

    nc = _bacc.Bacc("TRN2", target_bir_lowering=False, num_devices=1)
    arrays, args = {}, {}
    for name in _INS:
        arr = _np.ascontiguousarray(inputs[name])
        arrays[f"in_{name}"] = arr
        args[name] = nc.dram_tensor(f"in_{name}", arr.shape, mybir.dt.from_np(arr.dtype), kind="ExternalInput").ap()
    out = nc.dram_tensor("out_0", (N, D), F32, kind="ExternalOutput").ap()
    gnn_kernel(nc, args, out)
    r = _run(nc, [arrays], core_ids=[0])
    return r.results[0]["out_0"]
```

```python
import concourse.bass as bass
from concourse import mybir
from contextlib import ExitStack

F32 = mybir.dt.float32
I32 = mybir.dt.int32
BF16 = mybir.dt.bfloat16
ALU = mybir.AluOpType
ACT = mybir.ActivationFunctionType
AX = mybir.AxisListType

N, E, D = 6250, 106250, 256
G = 16
T = 832
NB = T // G
FULL, REST = divmod(E, 128)
NT = 50
NP = NT * 128
CH, NCH = 250, 25
SETS = [4, 2, 4, 4, 4]
AHEAD = [2, 2, 4, 4, 4]
SLOT = [260, 512, 260, 260, 260]
BIG = 1.0e30
EPS = 1e-5
LEAD = 3
H1, H2 = 8, 4
DEN = -(-NP // 512)
MKW = 513
LOOPS2 = 1250
LN2 = 0.6931471805599453
OCT_IDX = [[i ^ j for j in range(8)] for i in range(8)]
OCT_SIGN = [[1, 1, 1, 1, 1, 1, 1, 1], [1, -1, 1, -1, 1, -1, -1, 1], [1, -1, -1, 1, 1, 1, -1, -1],
            [1, 1, -1, -1, 1, -1, 1, -1], [1, -1, -1, -1, -1, 1, 1, 1], [1, 1, -1, 1, -1, -1, -1, 1],
            [1, 1, 1, -1, -1, 1, -1, -1], [1, -1, 1, 1, -1, -1, 1, -1]]
WIDTH = [256, 512, 260, 257, 256]
HEADS = [0, H1, H2, 1, 0]
PLANES = [2, 3, 3, 3, 2]
ds = bass.ds


def ring_base(L, k):
    return sum(64 * (NB // SETS[m]) for m in range(L) if k < 4 * SETS[m])


def made_before(L):
    return sum(T + LEAD * (HEADS[m] == 0) for m in range(L))


def past(L):
    return NB * (L - 1)


def wait(eng, sem, value):
    if isinstance(value, int) and value <= 0:
        return
    eng.wait_ge(sem, value)


def gate(eng, sem, value):
    wait(eng, sem, value)
    eng.nop(nofuse=True)


def gnn_kernel(nc, a, out):
    ctx = ExitStack()
    with ctx:
        def sb(name, shape, dt=F32):
            return ctx.enter_context(nc.sbuf_tensor(name, shape, dt))

        def sem(name):
            return ctx.enter_context(nc.semaphore(name))

        def dram(name, shape, dt=F32):
            return nc.dram_tensor(name, shape, dt).ap()

        x0 = dram("x0", (NP, D))
        x1 = dram("x1", (NP, D))
        x2 = dram("x2", (NP, D))
        x3 = dram("x3", (NP, D))
        kv_t = dram("kv_t", (NP, 512))
        q_t = dram("q_t", (NP, D))
        g1_t = dram("g1_t", (NP, 260))
        ed1_t = dram("ed1_t", (NP, 4))
        g2_t = dram("g2_t", (NP, 257))
        ed2_t = dram("ed2_t", (NP, 1))
        xs_t = dram("xs_t", (NP, D))
        deg_d = dram("deg_d", (NP,))
        dinv_d = dram("dinv_d", (NP,))
        mk1 = dram("mk1", (T, MKW))
        mk4 = dram("mk4", (NB, 4, G, MKW))
        mk8 = dram("mk8", (NB, 8, G, MKW))
        table = [a["x"], kv_t, g1_t, g2_t, xs_t]

        acc = sb("acc", [128, 3, NP])
        ring = sb("ring", [128, 64 * 260])
        rflat = ring[:, :]
        rings = [ring[:, 0:4 * SETS[L] * 4 * SLOT[L]].rearrange("p (s w) -> p s w", w=SLOT[L]) for L in range(5)]
        ohc = sb("ohc", [128, 8, 128])
        ohb = sb("ohb", [128, 2, 4, 128], BF16)
        oht = sb("oht", [128, 4, 4, 128])
        qw = sb("qw", [128, 8, 256])
        prod = sb("prod", [128, 2, 2, 256])
        src_c = sb("src_c", [128, T + G], I32)
        rel_c = sb("rel_c", [128, T + G])
        ew_c = sb("ew_c", [128, T + G])
        rel_s = sb("rel_s", [128, 4, G])
        base_r = sb("base_r", [1, T], I32)
        cneg_r = sb("cneg_r", [1, T])
        sneg_r = sb("sneg_r", [1, T])
        stage = sb("stage", [128, 4, G], I32)
        mk = sb("mk", [128, 2, MKW])
        sc = sb("sc", [128, 2, 128])
        fw = sb("fw", [128, 128])
        mx = sb("mx", [128, 128])
        m2 = dd = mx
        px = fw
        w8 = sb("w8", [128, 2, G, 3, 8])
        sel24 = sb("sel24", [128, 8])
        edw = sb("edw", [128, 2, G, 4])
        corr = sb("corr", [128, 2, 4])
        cl = sb("cl", [128, 4])
        ident = sb("ident", [128, 128])
        iota = sb("iota", [128, 128])
        ident_b = sb("ident_b", [128, 128], BF16)
        iota_b = sb("iota_b", [128, 128], BF16)
        ones = sb("ones", [1, 256])
        zeros = sb("zeros", [128, 1])
        selc8 = sb("selc8", [128, 384])
        selc4 = sb("selc4", [128, 384])
        seld8 = sb("seld8", [128, 256])
        seld4 = sb("seld4", [128, 256])
        degm = sb("degm", [1, 128])
        rows = sb("rows", [1, 7, 129])
        fprev = sb("fprev", [1, 8])
        bn = sb("bn", [128, 2, 4])
        lnst = sb("lnst", [128, 2, 12])
        cols = sb("cols", [128, 2, 4])
        dcol = sb("dcol", [128, NT])
        banks = [ctx.enter_context(nc.psum_tensor(f"bank{k}", [128, 512], F32)) for k in range(8)]
        ag, ot, qe, m0, m1 = banks[0:2], banks[2:4], banks[4:6], banks[6], banks[7]
        upper = lambda v_: v_.bitcast(BF16)[..., 1::2]
        selc = {H1: selc8, H2: selc4}
        seld = {H1: seld8, H2: seld4, 1: ones}

        at = [0]

        def view(*shape, dt=F32):
            size = 1
            for s in shape:
                size *= s
            v = rflat[:, at[0]:at[0] + size]
            at[0] += size
            assert at[0] <= 64 * 260
            if dt is not F32:
                v = v.bitcast(dt)
            if len(shape) == 2:
                v = v.rearrange("p (u v) -> p u v", u=shape[0])
            if len(shape) == 3:
                v = v.rearrange("p (u v w) -> p u v w", u=shape[0], v=shape[1])
            return v

        raw_i = view(7, 128, dt=I32)
        raw_f = view(7, 128)
        relr = view(7, 128)
        ewr = view(7, 128)
        mkr = view(7, MKW)
        last_r = view(T, dt=I32)
        raw_d = view(7, 128, dt=I32)
        zrow = view(256)
        raw_n = view(7, 128, dt=I32)
        lt = view(7, 128)
        at[0] = 0
        wraw = view(8, 256)
        wout = view(2, 256)
        pre = view(2, 256)
        xr = view(2, 256)
        xn = view(2, 256)
        rr = view(2, 256)
        stats = view(2, NCH * 6)
        shared = at[0]
        dinv_b = view(NP)
        at[0] = shared
        wproj = view(2, 768)
        xt = view(2, 256)
        po = view(2, 768)
        brow = view(768)
        bo_b = view(256)
        lg_b = view(256)
        lb_b = view(256)
        as_b = view(256)
        ad_b = view(256)
        wtmp = view(256)
        xs = view(2, 256)

        bar = sem("bar")
        s_ring = [sem(f"ring_ready{k}") for k in range(16)]
        s_const = sem("const_ready")
        s_prep_dma = sem("prep_loaded")
        s_base = sem("base_loaded")
        s_rowsdma = sem("lasts_loaded")
        s_prep = sem("prep_rows")
        s_prep_t = sem("prep_transposed")
        s_prep_c = sem("prep_copied")
        s_mkst = sem("masks_stored")
        s_x0 = sem("x0_stored")
        shared_sems = {k: sem(k) for k in ("staged", "added", "wready")}
        PASS = []
        for L in range(5):
            p = {"agg": sem(f"agg{L}"), **shared_sems}
            if L == 1:
                p.update({k: sem(f"{k}{L}") for k in (
                    "oh", "oht", "ohtc", "s", "st", "ch1", "row", "ch2", "col", "ch3", "px", "pb", "w",
                    "mk0", "mk1", "qe", "prod", "red", "qw0", "qw1", "qw2", "qw3")})
            if L == 2:
                p.update({k: sem(f"{k}{L}") for k in ("qeg", "z", "ed0", "ed1")})
            if L == 3:
                p["rows"] = sem("rows_weighted3")
            if L in (2, 3):
                p = {**PASS[L - 1], **p}
            PASS.append(p)
        NODE = []
        for P in range(5):
            names = ["wl", "w", "pre", "y", "var", "std", "xn"]
            names += ["wt", "wc"] if P in (0, 1, 4) else []
            names += ["xt", "xtc", "pj", "po", "ps0", "ps1"] if P < 3 else []
            names += ["xt", "xtc", "ps0", "ps1"] if P == 3 else []
            names += ["xr0", "xr1", "st0", "st1"] if P != 2 else []
            names += ["den", "clr"] if P in (1, 2, 3) else []
            names += ["ch", "chd"] if P in (0, 4) else []
            NODE.append({k: sem(f"n_{k}{P}") for k in names})
        s_deg = sem("deg_moved")
        s_sq = sem("to_square_root")
        s_sqd = sem("square_root_taken")

        block = ctx.enter_context(nc.Block())
        nbar = {}

        def barrier(eng):
            k = nbar.get(id(eng), 0) + 1
            nbar[id(eng)] = k
            eng.drain()
            eng.sem_inc(bar, 1)
            eng.wait_ge(bar, 5 * k)
            eng.nop(nofuse=True)

        def softmax_batches(eng, L, body):
            U = SETS[L]
            loops = (NB - 2) // U
            body(0, 0, True, False)
            with eng.Fori(0, loops) as i:
                for o in range(1, U + 1):
                    body(i, o, True, True)
            for b in range(loops * U + 1, NB):
                body(0, b, True, True)
            body(0, NB, False, True)

        def batch_at(L, i, o):
            U = SETS[L]
            return i * U + o, o % U, i + o // U, o % 2, i * (U // 2) + o // 2

        def pipeline(eng, body):
            for m in range(6):
                body(0, m)
            with eng.Fori(3, NT // 2 - 2) as i:
                body(i, 0)
                body(i, 1)
            for m in range(NT - 4, NT + 4):
                body(0, m)

        def tile_of(i, off, skew):
            o = off - skew
            if isinstance(i, int):
                n = 2 * i + o
                return (0 <= n < NT), n, n % 2, n // 2
            return True, i * 2 + o, o % 2, i + o // 2

        @block.sync
        def _(sp):
            sp.wait_ge(s_const, 1)
            sp.nop(nofuse=True)
            C6 = 6 * 128
            for dst_v, name in ((raw_i, "src"), (raw_d, "dst"), (ewr, "edge_weight")):
                v = a[name]
                sp.dma_start(dst_v[:, 0:6, :], v[0:C6 * 128].rearrange("(c p e) -> p c e", p=128, e=128))\
                    .then_inc(s_prep_dma, 16)
                sp.dma_start(dst_v[0:FULL - C6, 6, :], v[C6 * 128:FULL * 128].rearrange("(p e) -> p e", e=128))\
                    .then_inc(s_prep_dma, 16)
                sp.dma_start(dst_v[FULL - C6:FULL - C6 + 1, 6, 0:REST],
                             v[FULL * 128:E].rearrange("(p e) -> p e", p=1)).then_inc(s_prep_dma, 16)
            dn = a["dst"]
            sp.dma_start(raw_n[:, 0:6, :], dn[1:C6 * 128 + 1].rearrange("(c p e) -> p c e", p=128, e=128))\
                .then_inc(s_prep_dma, 16)
            sp.dma_start(raw_n[0:FULL - C6, 6, :], dn[C6 * 128 + 1:FULL * 128 + 1].rearrange("(p e) -> p e", e=128))\
                .then_inc(s_prep_dma, 16)
            sp.dma_start(raw_n[FULL - C6:FULL - C6 + 1, 6, 0:REST - 1],
                         dn[FULL * 128 + 1:E].rearrange("(p e) -> p e", p=1)).then_inc(s_prep_dma, 16)
            with nc.allow_non_contiguous_dma("one number of each tile"):
                dv = a["dst"][0:FULL * 128].rearrange("(o t e) -> o t e", o=1, e=128)
                sp.dma_start(base_r[0:1, 0:FULL].unsqueeze(2), dv[:, :, 0:1]).then_inc(s_base, 16)
                sp.dma_start(base_r[0:1, FULL:FULL + 1], a["dst"][FULL * 128:FULL * 128 + 1].unsqueeze(0))\
                    .then_inc(s_base, 16)
                sp.dma_start(last_r[0:1, 0:FULL].unsqueeze(2), dv[:, :, 127:128]).then_inc(s_rowsdma, 16)
            sp.dma_start(x0[0:N, :], a["x"][:, :]).then_inc(s_x0, 16)
            sp.dma_start(x0[N:N + 128, :], zrow[:, :]).then_inc(s_x0, 16)
            sp.dma_start(x0[N + 128:NP, :], zrow[0:NP - N - 128, :]).then_inc(s_x0, 16)
            sp.wait_ge(s_prep, 1)
            sp.nop(nofuse=True)
            sp.dma_start(mk1[0:C6, :].rearrange("(c p) w -> p c w", p=128), mkr[:, 0:6, :]).then_inc(s_mkst, 16)
            sp.dma_start(mk1[C6:T, :], mkr[0:T - C6, 6, :]).then_inc(s_mkst, 16)
            sp.wait_ge(s_mkst, 32)
            mkb = mk1.rearrange("(b t) w -> b (t w)", t=G)
            for dstm, H in ((mk4, H2), (mk8, H1)):
                for h in range(H):
                    sp.dma_start(dstm[:, h, :, :].rearrange("b t w -> b (t w)"), mkb).then_inc(s_mkst, 16)
            sp.wait_ge(s_mkst, 16 * (2 + H1 + H2))
            sp.wait_ge(s_x0, 48)
            barrier(sp)
            mk_of = {1: mk8, 2: mk4, 3: mk1}
            for L in range(5):
                p, H = PASS[L], HEADS[L]
                if H:
                    mrows = mk_of[L].rearrange("b h t w -> (b h t) w") if L < 3 else mk1

                    def windows(i, o, scores, sums):
                        if not scores:
                            return
                        b, _, _, par, _ = batch_at(L, i, o)
                        wait(sp, p["w"], b + (past(L) + 1))
                        sp.nop(nofuse=True)
                        sp.dma_start(mk[0:G * H, par, :], mrows[ds(b * (G * H), G * H), :])\
                            .then_inc(p[f"mk{par}"], 16)
                        for k in range(G):
                            base = sp.value_load(base_r[0:1, ds(b * G + k, 1)], min_val=0, max_val=N)
                            if L == 1:
                                if k % 2 == 0:
                                    wait(sp, p["qe"], b * 8 + (k // 2 - 1))
                                    sp.nop(nofuse=True)
                                sp.dma_start(qw[:, k % 8, :], q_t[ds(base, 128), :])\
                                    .then_inc(p[f"qw{k // 2 % 4}"], 16)
                            else:
                                edt = ed1_t if L == 2 else ed2_t
                                sp.dma_start(edw[:, par, k, 0:H], edt[ds(base, 128), :])\
                                    .then_inc(p[f"ed{par}"], 16)
                    softmax_batches(sp, L, windows)
                barrier(sp)
                q = NODE[L]
                col = lambda v: v.rearrange("(k p) -> p k", p=128)
                bc = lambda v, w: v.rearrange("(o w) -> o w", o=1).to_broadcast([128, w])

                def load(dst_v, src_v):
                    sp.dma_start(dst_v, src_v).then_inc(q["wl"], 16)

                def rowsof(v):
                    return v.rearrange("(k p) w -> p k w", p=128)
                with nc.allow_non_contiguous_dma("vectors as columns"):
                    if L == 0:
                        for j in range(8):
                            load(wraw[32 * (j % 4):32 * (j % 4) + 32, 6 + j // 4, :], a["L0_gnn_weight"][:, :])
                        load(cols[:, :, 0], col(a["L0_gnn_gamma"]))
                        load(cols[:, :, 1], col(a["L0_gnn_beta"]))
                        load(wraw[:, 0:2, :], rowsof(a["L1_gnn_Wk"]))
                        load(wraw[:, 2:4, :], rowsof(a["L1_gnn_Wv"]))
                        load(wraw[:, 4:6, :], rowsof(a["L1_gnn_Wq"]))
                        load(brow[0:1, 0:256], a["L1_gnn_bk"].unsqueeze(0))
                        load(brow[0:1, 256:512], a["L1_gnn_bv"].unsqueeze(0))
                        load(brow[0:1, 512:768], a["L1_gnn_bq"].unsqueeze(0))
                    if L == 1:
                        load(wraw[:, 0:2, :], rowsof(a["L1_gnn_Wo"]))
                        load(wproj[:, :, 0:256], rowsof(a["L2_gnn_W1"]))
                        load(bo_b[:, :], bc(a["L1_gnn_bo"], 256))
                        load(as_b[:, :], a["L2_gnn_a1_src"].rearrange("(o h) w -> o (h w)", o=1).to_broadcast([128, 256]))
                        load(ad_b[:, :], a["L2_gnn_a1_dst"].rearrange("(o h) w -> o (h w)", o=1).to_broadcast([128, 256]))
                    if L == 2:
                        load(wproj[:, :, 0:256], rowsof(a["L2_gnn_W2"]))
                        load(bo_b[:, :], bc(a["L2_gnn_b1"], 256))
                        load(lg_b[:, :], bc(a["L2_gnn_ln_g"], 256))
                        load(lb_b[:, :], bc(a["L2_gnn_ln_b"], 256))
                        load(as_b[:, :], a["L2_gnn_a2_src"].to_broadcast([128, 256]))
                        load(ad_b[:, :], a["L2_gnn_a2_dst"].to_broadcast([128, 256]))
                        sp.dma_start(deg_d.unsqueeze(0), acc[4:5, 2, :]).then_inc(s_deg, 16)
                        sp.wait_ge(s_deg, 16)
                    if L == 3:
                        load(bo_b[:, :], bc(a["L2_gnn_b2"], 256))
                        load(dcol[:, :], deg_d.rearrange("(n p) -> p n", p=128))
                    if L == 4:
                        load(wraw[:, 0:2, :], rowsof(a["L3_gnn_W"]))
                        load(cols[:, :, 0], col(a["L3_gnn_gamma"]))
                        load(cols[:, :, 1], col(a["L3_gnn_beta"]))
                        load(cols[:, :, 2], col(a["L3_gnn_b"]))
                        load(dinv_b[:, :], bc(dinv_d, NP))
                    if L == 3:
                        sp.wait_ge(q["w"], 1)
                        sp.dma_start(dinv_d.rearrange("(n p) -> p n", p=128), dcol[:, :]).then_inc(s_deg, 16)
                        sp.wait_ge(s_deg, 32)
                resid = [x0, x1, None, x2, x3][L]
                keep = [x1, x2, None, x3, None][L]

                def moves(i, off):
                    ok, n, par, use = tile_of(i, off, 0)
                    if ok and resid is not None:
                        wait(sp, q["var"], n - 1)
                        sp.nop(nofuse=True)
                        sp.dma_start(xr[:, par, :], resid[ds(n * 128, 128), :]).then_inc(q[f"xr{par}"], 16)
                    ok, n, par, use = tile_of(i, off, 2)
                    if ok and L != 2:
                        wait(sp, q["xn"], n + 1)
                        sp.nop(nofuse=True)
                        if keep is not None:
                            sp.dma_start(keep[ds(n * 128, 128), :], xn[:, par, :]).then_inc(q[f"st{par}"], 16)
                            if L == 3:
                                sp.dma_start(xs_t[ds(n * 128, 128), :], xs[:, par, :]).then_inc(q[f"ps{par}"], 16)
                        elif not isinstance(n, int) or 128 * (n + 1) <= N:
                            sp.dma_start(out[ds(n * 128, 128), :], xn[:, par, :]).then_inc(q[f"st{par}"], 16)
                        elif 128 * n < N:
                            sp.dma_start(out[128 * n:N, :], xn[0:N - 128 * n, par, :]).then_inc(q[f"st{par}"], 16)
                        else:
                            sp.nop().then_inc(q[f"st{par}"], 16)
                    ok, n, par, use = tile_of(i, off, 4)
                    if ok and L < 3:
                        wait(sp, q["po"], n + 1)
                        sp.nop(nofuse=True)
                        rws = ds(n * 128, 128)
                        if L == 0:
                            sp.dma_start(kv_t[rws, :], po[:, par, 0:512]).then_inc(q[f"ps{par}"], 16)
                            sp.dma_start(q_t[rws, :], po[:, par, 512:768]).then_inc(q[f"ps{par}"], 16)
                        if L == 1:
                            sp.dma_start(g1_t[rws, :], po[:, par, 0:260]).then_inc(q[f"ps{par}"], 16)
                            sp.dma_start(ed1_t[rws, :], po[:, par, 260:264]).then_inc(q[f"ps{par}"], 16)
                        if L == 2:
                            sp.dma_start(g2_t[rws, :], po[:, par, 0:257]).then_inc(q[f"ps{par}"], 16)
                            sp.dma_start(ed2_t[rws, :], po[:, par, 257:258]).then_inc(q[f"ps{par}"], 16)
                pipeline(sp, moves)
                for par in range(2):
                    if L != 2:
                        sp.wait_ge(q[f"st{par}"], 16 * (NT // 2))
                    if L < 4:
                        sp.wait_ge(q[f"ps{par}"], 16 * (NT // 2) * (2 if L < 3 else 1))
                barrier(sp)

        @block.gpsimd
        def _(pool):
            nc.gpsimd.memset(raw_i[:, :, :], 0)
            nc.gpsimd.memset(raw_d[:, :, :], N)
            nc.gpsimd.memset(raw_n[:, :, :], N)
            nc.gpsimd.memset(ewr[:, :, :], 0.0)
            nc.gpsimd.memset(base_r[:, :], N)
            nc.gpsimd.memset(last_r[0:1, :], N)
            nc.gpsimd.memset(zrow[:, :], 0.0)
            pool.drain()
            pool.sem_inc(s_const, 1)
            nc.gpsimd.memset(src_c[:, T:T + G], 0)
            nc.gpsimd.memset(rel_c[:, T:T + G], 0.0)
            nc.gpsimd.memset(ew_c[:, T:T + G], 0.0)
            nc.gpsimd.memset(ident[:, :], 0.0)
            nc.gpsimd.memset(ones[:, :], 1.0)
            nc.gpsimd.memset(zeros[:, :], 0.0)
            nc.gpsimd.memset(selc8[:, :], 0.0)
            nc.gpsimd.memset(selc4[:, :], 0.0)
            nc.gpsimd.memset(seld8[:, :], 0.0)
            nc.gpsimd.memset(seld4[:, :], 0.0)
            nc.gpsimd.memset(degm[:, :], 1.0)
            nc.gpsimd.memset(w8[:, :, :, :, :], 1.0)
            nc.gpsimd.memset(sel24[:, :], 0.0)
            nc.gpsimd.iota(iota[:, :], pattern=[[1, 128]], base=0, channel_multiplier=0,
                           allow_small_or_imprecise_dtypes=True)
            pool.drain()

            def ones_where(view_, pattern, base=0):
                nc.gpsimd.affine_select(out=view_, in_=view_, compare_op=ALU.not_equal, fill=1.0, base=base,
                                        pattern=pattern, channel_multiplier=1)
            ones_where(ident[:, :], [[-1, 128]])
            ones_where(selc8[:, 0:256].rearrange("p (g f) -> p g f", g=8), [[-G, 8], [0, 32]])
            ones_where(selc8[:, 256:384].rearrange("p (s h) -> p s h", h=8), [[0, 16], [-G, 8]])
            ones_where(selc4[:, 0:256].rearrange("p (g f) -> p g f", g=4), [[-G, 4], [0, 64]])
            ones_where(selc4[:, 256:384].rearrange("p (s h) -> p s h", h=8), [[0, 16], [-G, 8]])
            ones_where(seld8[:, :].rearrange("p (g f) -> p g f", g=8), [[-1, 8], [0, 32]])
            ones_where(seld4[:, :].rearrange("p (g f) -> p g f", g=4), [[-1, 4], [0, 64]])
            nc.gpsimd.memset(degm[:, :].rearrange("p (s h) -> p s h", h=8)[:, :, 0:4], 0.0)
            for part in range(3):
                pool.drain()
                ones_where(sel24[:, :], [[-1, 8]], base=-8 * part)
            pool.drain()
            nc.gpsimd.tensor_copy(ident_b[:, :], ident[:, :])
            nc.gpsimd.tensor_copy(iota_b[:, :], iota[:, :])
            nc.gpsimd.memset(acc[:, :, :], 0.0)
            pool.drain()
            pool.sem_inc(s_const, 1)
            barrier(pool)
            for L in range(5):
                p, W = PASS[L], WIDTH[L]
                nc.gpsimd.tensor_copy(stage[:, 0, :], src_c[:, 0:G]).then_inc(p["staged"], 1)
                with pool.Fori(0, NB // 4) as i:
                    for s in range(4):
                        if AHEAD[L] > 2:
                            for f in range(4):
                                f += (s + 1) % 4 * 4
                                pool.wait_ge(s_ring[f], i * 64 + ((s + 1) // 4 * 64 + ring_base(L, f)))
                            pool.nop(nofuse=True)
                        nc.gpsimd.tensor_copy(stage[:, (s + 1) % 4, :], src_c[:, ds(i * (4 * G) + (s + 1) * G, G)])\
                            .then_inc(p["staged"], 1)
                        for g in range(4):
                            pool.wait_ge(p["agg"], i * (4 * G) + (s * G + 4 * g + 4))
                            if g == 0:
                                pool.wait_ge(p["staged"], i * 4 + (s + 1 + (NB + 1) * L))
                            pool.nop(nofuse=True)
                            for j in range(4):
                                slot = (s % SETS[L]) * G + 4 * g + j
                                nc.gpsimd.indirect_dma_start(
                                    out=rings[L][:, slot, 0:W], out_offset=None, in_=table[L][:, :],
                                    in_offset=bass.IndirectOffsetOnAxis(
                                        ap=stage[:, s, 4 * g + j:4 * g + j + 1], axis=0))\
                                    .then_inc(s_ring[slot // 4], 16)
                barrier(pool)
                q = NODE[L]
                if L < 3:
                    def clear(i, off):
                        ok, n, par, use = tile_of(i, off, 1)
                        if ok:
                            wait(pool, q["pre"], n + 1)
                            nc.gpsimd.tensor_copy(acc[:, :, ds(n * 128, 128)],
                                                  zeros[:, :].unsqueeze(2).to_broadcast([128, 3, 128]))
                    if L == 2:
                        pool.wait_ge(s_deg, 16)
                    pipeline(pool, clear)
                barrier(pool)

        @block.scalar
        def _(act):
            barrier(act)
            for L in range(5):
                p, H = PASS[L], HEADS[L]
                R = G * H
                if H:
                    if L == 1:
                        act.sem_inc(p["ohtc"], 2)
                        act.sem_inc(p["w"], 2)

                    def turned(b):
                        for g in range(4):
                            wait(act, p["oht"], b * 4 + (4 * past(L) + g + 1))
                            if L == 1:
                                wait(act, p["qe"], b * 8 + (2 * g - 4))
                            elif g == 0:
                                wait(act, p["qeg"], b + NB * (L - 2))
                            act.activation(oht[:, g, :, :],
                                           ot[g % 2][:, 0:256].bitcast(BF16).rearrange("p (k j) -> p k j", k=4),
                                           ACT.Copy).then_inc(p["ohtc"], 1)
                    turned(0)

                    def chain(i, o, scores, sums):
                        if not scores:
                            return
                        b, rset, _, par, _ = batch_at(L, i, o)
                        feed = not isinstance(b, int) or b + 1 < NB
                        if L > 1 and feed:
                            turned(b + 1)
                        wait(act, p["ch3"], b + (past(L) + 1))
                        act.activation(px[0:R, :], dd[0:R, :], ACT.Exp)
                        act.activation(cl[0:R, 3:4], cl[0:R, 2:3], ACT.Exp).then_inc(p["px"], 1)
                        wait(act, p["pb"], b + (past(L) + 1))
                        act.activation(w8[:, par, :, 0, 0:H],
                                       m0[:, 128:128 + R].rearrange("p (h t) -> p t h", h=H), ACT.Copy)
                        act.activation(corr[:, par, 0:3], m1[:, 264:267], ACT.Copy).then_inc(p["w"], 1)
                        if L == 1 and feed:
                            turned(b + 1)
                        if L == 3:
                            act.drain()
                            for k in range(G):
                                row = rings[L][:, rset * G + k, 0:256]
                                ins = act.activation(row, row, ACT.Copy, scale=w8[:, par, k, 0, 0:1])
                                if k % 4 == 3:
                                    ins.then_inc(p["rows"], 1)
                    softmax_batches(act, L, chain)
                barrier(act)
                q = NODE[L]
                if L in (0, 4):
                    act.sem_inc(q["ch"], 2)
                if L < 4:
                    act.sem_inc(q["xtc"], 2)
                if L in (0, 1, 4):
                    for m in range({0: 3, 1: 1, 4: 1}[L]):
                        act.wait_ge(q["wt"], m + 1)
                        dst_v = {0: wproj[:, :, 256 * m:256 * m + 256], 1: wout, 4: wout}[L]
                        scale = float(1.0 / (32.0 ** 0.5)) if (L == 0 and m == 2) else 1.0
                        act.activation(dst_v, ot[m % 2][:, :].rearrange("p (k f) -> p k f", k=2), ACT.Copy,
                                       scale=scale).then_inc(q["wc"], 1)
                    if L == 0:
                        act.wait_ge(q["wl"], 16 * 16)
                        act.activation(brow[0:1, 512:768], brow[0:1, 512:768], ACT.Copy,
                                       scale=float(1.0 / (32.0 ** 0.5))).then_inc(q["wc"], 1)
                if L in (0, 4):
                    if L == 0:
                        def keep_chunk(c, par):
                            act.wait_ge(q["chd"], c + 1)
                            act.activation(acc[:, 0:2, ds(c * CH, CH)],
                                           qe[par][:, 0:2 * CH].rearrange("p (k n) -> p k n", k=2), ACT.Copy)\
                                .then_inc(q["ch"], 1)
                        with act.Fori(0, NCH // 2) as i:
                            keep_chunk(i * 2, 0)
                            keep_chunk(i * 2 + 1, 1)
                        keep_chunk(NCH - 1, 0)
                    for m in {0: (1,), 4: (3,)}[L]:
                        act.wait_ge(s_sq, m)
                        act.activation(bn[:, :, 1], bn[:, :, 1], ACT.Sqrt).then_inc(s_sqd, 1)
                    act.wait_ge(q["w"], 1 if L == 4 else 2)
                if L == 0:
                    act.drain()
                    for k in range(2):
                        act.activation(acc[:, k, 0:N], acc[:, k, 0:N], ACT.Tanh,
                                       bias=bn[:, k, 3:4], scale=bn[:, k, 2:3])
                if L == 3:
                    act.wait_ge(s_sq, 2)
                    act.activation(rr[:, 0, 0:NT], rr[:, 0, 0:NT], ACT.Sqrt).then_inc(s_sqd, 1)
                act.drain()

                def stages(i, off):
                    ok, n, par, use = tile_of(i, off, 3)
                    if ok and L == 3:
                        wait(act, q["xt"], n + 1)
                        act.activation(acc[:, 0:2, ds(n * 128, 128)],
                                       (m0, m1)[par][:, 0:256].rearrange("p (k j) -> p k j", k=2), ACT.Copy)\
                            .then_inc(q["xtc"], 1)
                    if ok and L < 3:
                        wait(act, q["xt"], n + 1)
                        wait(act, q["pj"], n + 1)
                        act.activation(xt[:, par, :], (m0, m1)[par][:, 0:256], ACT.Copy)\
                            .then_inc(q["xtc"], 1)
                    ok, n, par, use = tile_of(i, off, 0)
                    if ok and L in (0, 4):
                        wait(act, q["y"], n + 1)
                        for k in range(2):
                            if L == 0:
                                ins = act.activation(pre[:, par, 128 * k:128 * k + 128],
                                                     acc[:, k, ds(n * 128, 128)], ACT.Copy)
                            else:
                                ins = act.activation(pre[:, par, 128 * k:128 * k + 128],
                                                     acc[:, k, ds(n * 128, 128)], ACT.Relu,
                                                     bias=bn[:, k, 3:4], scale=bn[:, k, 2:3])
                        ins.then_inc(q["pre"], 1)
                    ok, n, par, use = tile_of(i, off, 4)
                    if ok and L < 3:
                        wait(act, q["pj"], n + 3)
                        wait(act, q[f"ps{par}"], use * 32)
                        w1 = [512, 264, 258][L]
                        ins = act.activation(po[:, par, 0:w1], qe[par][:, 0:w1], ACT.Copy)
                        if L == 0:
                            ins = act.activation(po[:, par, 512:768], ag[par][:, 0:256], ACT.Copy)
                        ins.then_inc(q["po"], 1)
                    ok, n, par, use = tile_of(i, off, 1)
                    if ok:
                        act.wait_ge(q["var"], n + 1)
                        act.activation(lnst[:, par, 9:10], lnst[:, par, 8:9], ACT.Sqrt).then_inc(q["std"], 1)
                pipeline(act, stages)
                barrier(act)

        @block.tensor
        def _(pe):
            mm = nc.tensor.matmul
            tr = nc.tensor.transpose
            pe.wait_ge(s_const, 2)
            for c in range(21):
                which, c7 = divmod(c, 7)
                n = 128 if c7 < 6 else T - 6 * 128
                rows_v = (raw_f, relr, ewr)[which]
                if c7 == 0:
                    pe.wait_ge(s_prep, (2, 3, 3)[which])
                if c >= 2:
                    pe.wait_ge(s_prep_c, c - 1)
                tr(ot[c % 2][:, 0:n], rows_v[0:n, c7, :], ident[0:n, 0:n]).then_inc(s_prep_t, 1)
            barrier(pe)
            for L in range(5):
                p, H, PL = PASS[L], HEADS[L], PLANES[L]
                R = G * H
                pe.sem_inc(p["agg"], G * AHEAD[L])
                if L == 1:
                    pe.sem_inc(p["qe"], 2)
                rg = rings[L]
                vo = 256 if L == 1 else 0

                def add_tile(b, rset, k, use):
                    pe.wait_ge(p["wready"], b * G + (k + 1 + made_before(L)))
                    if L == 3 and k % 4 == 0:
                        pe.wait_ge(p["rows"], b * 4 + (k // 4 + 1))
                    slot = rset * G + k
                    one_hot = ohc[:, k % 8, :]
                    if not H and k % 4 == 0:
                        pe.wait_ge(s_ring[slot // 4], use * 64 + (64 + ring_base(L, slot // 4)))
                    pe.wait_ge(p["added"], b * G + (k + 1 + T * L))
                    for c in range(2):
                        ins = mm(ag[k % 2][:, 128 * c:128 * c + 128], rg[:, slot, vo + 128 * c:vo + 128 * c + 128],
                                 one_hot, start=True, stop=True)
                    if H:
                        ins = mm(ag[k % 2][0:24, 256:384],
                                 upper(w8[:, rset % 2, k, :, :].rearrange("p s h -> p (s h)")), upper(one_hot),
                                 start=True, stop=True)
                    ins.then_inc(p["agg"], 1)

                if not H:
                    with pe.Fori(0, NB // 4) as i:
                        for rset in range(4):
                            for k in range(G):
                                add_tile(i * 4 + rset, rset, k, i)
                else:
                    def turn(b, g):
                        pe.wait_ge(p["oh"], b * 4 + (4 * past(L) + g + 1))
                        pe.wait_ge(p["ohtc"], b * 4 + (4 * past(L) + g + 1))
                        for j in range(4):
                            ins = tr(ot[g % 2][:, 64 * j:64 * j + 64].bitcast(BF16), ohb[:, g % 2, j, :],
                                     ident_b[:, :])
                        ins.then_inc(p["oht"], 1)

                    def dest_scores(b, par, ub, g):
                        if g == 0:
                            gate(pe, p["ohtc"], b * 4 + (4 * past(L) + 6))
                            pe.wait_ge(p[f"ed{par}"], ub * 256 + (256 + 128 * past(L - 1)))
                            gate(pe, p["z"], b + (past(L - 1) + 1))
                        for k in range(4 * g, 4 * g + 4):
                            ins = mm(qe[par][:, k * H:k * H + H], oht[:, k // 4, k % 4, :],
                                     edw[:, par, k, 0:H], start=True, stop=True)
                        if g == 3:
                            ins.then_inc(p["qeg"], 1)

                    def dest_rows(b, r):
                        if r % 2 == 0:
                            gate(pe, p["ohtc"], b * 4 + (4 * past(L) + r // 2 + 3))
                        pe.wait_ge(p["prod"], b * 8 + r + 1)
                        pe.wait_ge(p[f"qw{r % 4}"], b * 64 + 32 * (r // 4) + 32)
                        for j in range(2):
                            k = 2 * r + j
                            ins = mm(qe[r % 2][:, 256 * j:256 * j + 256], oht[:, k // 4, k % 4, :],
                                     qw[:, k % 8, :], start=True, stop=True)
                        ins.then_inc(p["qe"], 1)
                    for g in range(4):
                        turn(0, g)
                    if L > 1:
                        for g in range(4):
                            dest_scores(0, 0, 0, g)
                    turns = (11, 13, 16, 16) if L == 1 else (3, 5, 7, 9)
                    at_row, at_col, at_px = (11, 13, 15) if L == 1 else (5, 9, 13)

                    def batch(i, o, scores, sums):
                        b, _, _, par, _ = batch_at(L, i, o)
                        c, cset, cu, _, _ = batch_at(L, i, o - 1)
                        nb, _, _, npar, nub = batch_at(L, i, o + 1)
                        feed = scores and (not isinstance(b, int) or b + 1 < NB)

                        def turn_scores():
                            gate(pe, p["w"], b + (past(L) + 2))
                            gate(pe, p["s"], b + (past(L) + 1))
                            tr(m0[0:R, 0:128], sc[:, par, 0:R], ident[:, :]).then_inc(p["st"], 1)
                        if scores and L == 1:
                            dest_rows(b, 0)
                            dest_rows(b, 1)
                        if scores and L > 1:
                            turn_scores()
                        for k in range(G):
                            if sums:
                                add_tile(c, cset, k, None)
                            if scores and L == 1 and k + 2 < 8:
                                dest_rows(b, k + 2)
                            if scores and L == 1 and k == 9:
                                turn_scores()
                            if feed and k in turns:
                                turn(nb, turns.index(k))
                            if feed and L > 1 and k in (10, 11, 12, 14):
                                dest_scores(nb, npar, nub, (10, 11, 12, 14).index(k))
                            if scores and k == at_row:
                                gate(pe, p["ch1"], b + (past(L) + 1))
                                mm(m1[0:1, 0:R], mx[0:R, 0:1], ident[0:R, 0:R], start=True, stop=True)
                                mm(m1[0:1, 128:128 + R], mx[0:R, 127:128], ident[0:R, 0:R], start=True, stop=True)\
                                    .then_inc(p["row"], 1)
                            if scores and k == at_col:
                                gate(pe, p["ch2"], b + (past(L) + 1))
                                mm(m1[0:R, 256:257], rows[0:1, 5, 0:R], ones[0:1, 0:1], start=True, stop=True)
                                mm(m1[0:R, 257:258], rows[0:1, 4, 0:R], ones[0:1, 0:1], start=True, stop=True)\
                                    .then_inc(p["col"], 1)
                            if scores and k == at_px:
                                gate(pe, p["px"], b + (past(L) + 1))
                                tr(m0[:, 128:128 + R], px[0:R, :], ident[0:R, 0:R])
                                for f in range(3):
                                    if H == 1:
                                        ins = mm(m1[:, 264 + f:265 + f], ones[0:1, 0:128], cl[0:1, 3:4],
                                                 start=True, stop=True)
                                    else:
                                        add = H == H2 and f == 2
                                        ins = mm(m1[:, 264 + f:265 + f], selc[H][0:R, 128 * f:128 * f + 128],
                                                 cl[0:R, 3:4], start=True, stop=not add)
                                        if add:
                                            ins = mm(m1[:, 264 + f:265 + f], degm[0:1, :], ones[0:1, 0:1],
                                                     start=False, stop=True)
                                ins.then_inc(p["pb"], 1)
                        if feed and L == 1:
                            turn(nb, 2)
                            turn(nb, 3)
                    softmax_batches(pe, L, batch)
                barrier(pe)
                q = NODE[L]
                if L in (0, 1, 4):
                    pe.wait_ge(q["wl"], 16 * {0: 16, 1: 5, 4: 5}[L])
                    for m in range({0: 3, 1: 1, 4: 1}[L]):
                        if m >= 2:
                            pe.wait_ge(q["wc"], m - 1)
                        for kc in range(2):
                            for oc in range(2):
                                ins = tr(ot[m % 2][:, 256 * kc + 128 * oc:256 * kc + 128 * oc + 128],
                                         wraw[:, 2 * m + oc, 128 * kc:128 * kc + 128], ident[:, :])
                        ins.then_inc(q["wt"], 1)
                    pe.wait_ge(q["wc"], {0: 4, 1: 1, 4: 1}[L])
                if L in (0, 4):
                    if L == 0:
                        pe.wait_ge(q["w"], 1)

                    def project(c, par):
                        pe.wait_ge(q["ch"], c + 1)
                        for oc in range(2):
                            for kc in range(2):
                                ins = mm(qe[par][:, CH * oc:CH * oc + CH], wout[:, kc, 128 * oc:128 * oc + 128],
                                         acc[:, kc, ds(c * CH, CH)], start=kc == 0, stop=kc == 1)
                        ins.then_inc(q["chd"], 1)
                    with pe.Fori(0, NCH // 2) as i:
                        project(i * 2, 0)
                        project(i * 2 + 1, 1)
                    project(NCH - 1, 0)
                pe.sem_inc(q["y"], 2)
                if L < 3:
                    pe.sem_inc(q["pj"], 2)

                if L in (1, 2, 3):
                    for m in range(DEN):
                        wait(pe, q["clr"], m - 1)
                        n = min(512, NP - 512 * m)
                        mm(qe[m % 2][0:8, 0:n], sel24[0:24, :], acc[0:24, 2, 512 * m:512 * m + n],
                           start=True, stop=True).then_inc(q["den"], 1)

                def stages(i, off):
                    ok, n, par, use = tile_of(i, off, 0)
                    if ok and L in (1, 2, 3):
                        if isinstance(n, int) and n == 0:
                            pe.wait_ge(q["clr"], DEN + 1)
                        wait(pe, q["pre"], n - 1)
                        pe.nop(nofuse=True)
                        for c in range(2):
                            ins = mm(ag[par][:, 128 * c:128 * c + 128], seld[H][0:H, 128 * c:128 * c + 128],
                                     acc[0:H, 2, ds(n * 128, 128)], start=True, stop=True)
                        ins.then_inc(q["den"], 1)
                    ok, n, par, use = tile_of(i, off, 3)
                    if ok and L < 4:
                        pe.wait_ge(q["xn"], n + 1)
                        pe.wait_ge(q["xtc"], n + 1)
                        for c in range(2):
                            ins = tr((m0, m1)[par][:, 128 * c:128 * c + 128],
                                     (xs if L == 3 else xn)[:, par, 128 * c:128 * c + 128], ident[:, :])
                        ins.then_inc(q["xt"], 1)
                    ok, n, par, use = tile_of(i, off, 1)
                    if ok:
                        pe.wait_ge(q["pre"], n + 1)
                        wait(pe, q["var"], n - 1)
                        if L == 1:
                            for c in range(2):
                                ins = mm(ot[par][:, 0:256], pre[:, par, 128 * c:128 * c + 128], wout[:, c, :],
                                         start=c == 0, stop=c == 1)
                        else:
                            for c in range(2):
                                ins = tr(ot[par][:, 128 * c:128 * c + 128], pre[:, par, 128 * c:128 * c + 128],
                                         ident[:, :])
                        ins.then_inc(q["y"], 1)
                    ok, n, par, use = tile_of(i, off, 3)
                    if ok and L < 3:
                        pe.wait_ge(q["xtc"], n + 3)
                        wait(pe, q["po"], n - 1)
                        if L:
                            pe.wait_ge(q["w"], 1)
                        w1 = [512, 264, 258][L]
                        xv = xt[:, par, :]
                        for c in range(2):
                            ins = mm(qe[par][:, 0:w1], xv[:, 128 * c:128 * c + 128], wproj[:, c, 0:w1],
                                     start=c == 0, stop=(c == 1 and L > 0))
                        if L == 0:
                            mm(qe[par][:, 0:512], ones[0:1, 0:128], brow[0:1, 0:512], start=False, stop=True)
                            for c in range(2):
                                mm(ag[par][:, 0:256], xv[:, 128 * c:128 * c + 128],
                                   wproj[:, c, 512:768], start=c == 0, stop=False)
                            ins = mm(ag[par][:, 0:256], ones[0:1, 0:128], brow[0:1, 512:768],
                                     start=False, stop=True)
                        ins.then_inc(q["pj"], 1)
                pipeline(pe, stages)
                barrier(pe)

        @block.vector
        def _(dve):
            v = nc.vector
            tt = v.tensor_tensor
            dve.wait_ge(s_prep_dma, 12 * 16)
            v.tensor_copy(raw_f[:, :, :], raw_i[:, :, :])
            v.tensor_copy(relr[:, :, :], raw_d[:, :, :])
            dve.drain()
            tt(relr[:, :, :], relr[:, :, :], raw_d[:, :, 0:1].to_broadcast([128, 7, 128]), ALU.subtract)
            v.memset(mkr[:, :, 0:1], 0.0)
            v.memset(mkr[:, :, 128:129], 0.0)
            dve.drain()
            tt(mkr[:, :, 1:128], relr[:, :, 1:128], relr[:, :, 0:127], ALU.not_equal)
            v.tensor_scalar(mkr[:, :, 129:257], relr[:, :, :], 0.0, -BIG, ALU.not_equal, ALU.mult)
            tt(mkr[:, :, 257:385], relr[:, :, :], relr[:, :, 127:128].to_broadcast([128, 7, 128]), ALU.not_equal)
            tt(mkr[:, :, 385:513], raw_d[:, :, :], raw_n[:, :, :], ALU.not_equal)
            v.tensor_scalar(lt[:, :, :], raw_d[:, :, :], float(LOOPS2), LN2, ALU.is_lt, ALU.mult)
            dve.drain()
            tt(mkr[:, :, 385:513], mkr[:, :, 385:513], lt[:, :, :], ALU.mult)
            v.tensor_scalar(mkr[:, :, 1:128], mkr[:, :, 1:128], -BIG, None, ALU.mult)
            v.tensor_scalar(mkr[:, :, 257:385], mkr[:, :, 257:385], -BIG, None, ALU.mult)
            dve.drain()
            dve.sem_inc(s_prep, 3)
            for c in range(21):
                which, c7 = divmod(c, 7)
                n = 128 if c7 < 6 else T - 6 * 128
                dst_v = (src_c, rel_c, ew_c)[which]
                dve.wait_ge(s_prep_t, c + 1)
                v.tensor_copy(dst_v[:, 128 * c7:128 * c7 + n], ot[c % 2][:, 0:n]).then_inc(s_prep_c, 1)
            dve.wait_ge(s_base, 32)
            dve.wait_ge(s_rowsdma, 16)
            tt(cneg_r[:, 1:T], base_r[:, 1:T], last_r[0:1, 0:T - 1], ALU.not_equal)
            tt(sneg_r[:, :], base_r[:, :], last_r[0:1, :], ALU.not_equal)
            v.memset(cneg_r[:, 0:1], 1.0)
            for k in range(2):
                v.memset(ag[k][:, :], 0.0)
            dve.drain()
            tt(sneg_r[:, :], sneg_r[:, :], cneg_r[:, :], ALU.add)
            dve.drain()
            v.tensor_scalar(cneg_r[:, :], cneg_r[:, :], -BIG, None, ALU.mult)
            v.tensor_scalar(sneg_r[:, :], sneg_r[:, :], -BIG, None, ALU.mult)
            barrier(dve)
            for L in range(5):
                p, H, PL = PASS[L], HEADS[L], PLANES[L]
                R = G * H
                if L == 0:
                    dve.sem_inc(p["added"], 2)

                rg = rings[L]

                def add_window(b, k):
                    base = dve.value_load(base_r[0:1, ds(b * G + k, 1)], min_val=0, max_val=N)
                    win = acc[:, 0:PL, ds(base, 128)]
                    dve.wait_ge(p["agg"], b * G + (k + 1 + G * AHEAD[L]))
                    dve.wait_ge(p["added"], b * G + (k + 2 + T * L))
                    tt(win, win, ag[k % 2][:, 0:128 * PL].rearrange("p (c j) -> p c j", c=PL), ALU.add)\
                        .then_inc(p["added"], 1)

                def one_hot(rel, k, weight):
                    if weight is None:
                        return v.tensor_scalar(ohc[:, k % 8, :], iota[:, :], rel, None, ALU.is_equal)
                    return v.tensor_scalar(ohc[:, k % 8, :], iota[:, :], rel, weight, ALU.is_equal, ALU.mult)

                if not H:
                    def hot(b, k):
                        wt = ew_c[:, ds(b * G + k, 1)] if L == 0 else None
                        one_hot(rel_c[:, ds(b * G + k, 1)], k, wt).then_inc(p["wready"], 1)
                    for k in range(LEAD):
                        hot(0, k)
                    with dve.Fori(0, NB // 4) as i:
                        for u in range(4):
                            for k in range(G):
                                hot(i * 4 + u, k + LEAD)
                                add_window(i * 4 + u, k)
                else:
                    if L == 2:
                        dve.sem_inc(p["z"], 2)
                    if L == 1:
                        dve.sem_inc(p["prod"], 2)
                        dve.sem_inc(p["red"], 2)
                    if L == 2:
                        v.memset(w8[:, :, :, 0, :], 1.0)
                    v.memset(fprev[:, :], -BIG)
                    v.memset(rows[:, :, :], -2.0 * BIG)

                    def keep_rel(b, to):
                        v.tensor_copy(rel_s[:, to, :], rel_c[:, ds(b * G, G)])

                    def hot_to_turn(b, par, k):
                        if k % 4 == 0:
                            wait(dve, p["oht"], b * 4 + (4 * past(L) + k // 4 - 1))
                        ins = v.tensor_scalar(ohb[:, k // 4 % 2, k % 4, :], iota_b[:, :],
                                              rel_s[:, 2 + par, k:k + 1], None, ALU.is_equal)
                        if k % 4 == 3:
                            ins.then_inc(p["oh"], 1)

                    def ready(rset, use, k):
                        dve.wait_ge(s_ring[rset * 4 + k // 4], use * 64 + (64 + ring_base(L, rset * 4 + k // 4)))

                    def reduce(b, par, r):
                        dve.wait_ge(p["prod"], b * 8 + (r + 3))
                        v.tensor_reduce(sc[:, par, 0:R].rearrange("p (h t) -> p t h", h=H)[:, 2 * r:2 * r + 2, :],
                                        prod[:, r % 2, :, :].rearrange("p t (h d) -> p t h d", h=H), AX.X, ALU.add)\
                            .then_inc(p["red"], 1)

                    def products(b, rset, use, par, r):
                        if r % 2 == 0:
                            ready(rset, use, 2 * r)
                        dve.wait_ge(p["qe"], b * 8 + (r + 3))
                        dve.wait_ge(p["red"], b * 8 + (r + 1))
                        tt(prod[:, r % 2, :, :], qe[r % 2][:, :].rearrange("p (t w) -> p t w", t=2),
                           rg[:, rset * G + 2 * r:rset * G + 2 * r + 2, 0:256], ALU.mult).then_inc(p["prod"], 1)
                        if r:
                            reduce(b, par, r - 1)

                    def scores_of(b, rset, use, par):
                        for k in range(0, G, 4):
                            ready(rset, use, k)
                        dve.wait_ge(p["qeg"], b + (NB * (L - 2) + 1))
                        tt(sc[:, par, 0:R].rearrange("p (h t) -> p t h", h=H),
                           qe[par][:, 0:R].rearrange("p (t h) -> p t h", h=H),
                           rg[:, rset * G:rset * G + G, 256:256 + H], ALU.add).then_inc(p["z"], 1)
                        dve.drain()
                        v.scalar_tensor_tensor(sc[:, par, 0:R], sc[:, par, 0:R], 0.2, sc[:, par, 0:R],
                                               ALU.mult, ALU.max)
                        dve.drain()
                        dve.sem_inc(p["s"], 1)

                    def ch1(b, par, ub):
                        dve.wait_ge(p[f"mk{par}"], ub * 16 + (16 + 8 * past(L)))
                        dve.wait_ge(p["st"], b + (past(L) + 1))
                        v.tensor_tensor_scan(out=fw[0:R, :], data0=mk[0:R, par, 0:128], data1=m0[0:R, 0:128],
                                             initial=-BIG, op0=ALU.add, op1=ALU.max)
                        dve.drain()
                        v.tensor_tensor_scan(out=mx[0:R, ::-1], data0=mk[0:R, par, 1:129][:, ::-1],
                                             data1=fw[0:R, ::-1], initial=-BIG, op0=ALU.add, op1=ALU.max)\
                            .then_inc(p["ch1"], 1)

                    def ch2(b, par, ub):
                        hv = lambda k: rows[0:1, k, 0:R].rearrange("p (h t) -> p h t", h=H)
                        nb = lambda r_, o, n: r_[0:1, ds(b * G + o, n)].unsqueeze(1).to_broadcast([1, H, n])
                        head = m1[0:1, 0:R].rearrange("p (h t) -> p h t", h=H)
                        tail = m1[0:1, 128:128 + R].rearrange("p (h t) -> p h t", h=H)
                        fp = fprev[0:1, 0:H].unsqueeze(2)
                        v.tensor_copy(hv(0)[:, :, 1:G], nb(sneg_r, 1, G - 1))
                        tt(hv(6)[:, :, 0:1], fp, nb(sneg_r, 0, 1), ALU.add)
                        dve.wait_ge(p["row"], b + (past(L) + 1))
                        v.tensor_copy(hv(1), tail)
                        tt(hv(2)[:, :, 0:G - 1], head[:, :, 1:G], nb(cneg_r, 1, G - 1), ALU.add)
                        tt(hv(5)[:, :, 0:1], fp, nb(cneg_r, 0, 1), ALU.add)
                        dve.drain()
                        tt(hv(1)[:, :, 0:1], hv(1)[:, :, 0:1], hv(6)[:, :, 0:1], ALU.max)
                        v.tensor_tensor_scan(out=rows[0:1, 3, 0:R][:, ::-1], data0=rows[0:1, 0, 1:R + 1][:, ::-1],
                                             data1=rows[0:1, 2, 0:R][:, ::-1], initial=-BIG,
                                             op0=ALU.add, op1=ALU.max)
                        dve.drain()
                        v.tensor_tensor_scan(out=rows[0:1, 4, 0:R], data0=rows[0:1, 0, 0:R],
                                             data1=rows[0:1, 1, 0:R], initial=-BIG, op0=ALU.add, op1=ALU.max)
                        dve.drain()
                        tt(rows[0:1, 4, 0:R], rows[0:1, 4, 0:R], rows[0:1, 3, 0:R], ALU.max)
                        dve.drain()
                        tt(hv(5)[:, :, 1:G], hv(4)[:, :, 0:G - 1], nb(cneg_r, 1, G - 1), ALU.add)
                        v.tensor_copy(fp, hv(4)[:, :, G - 1:G])
                        dve.drain()
                        dve.sem_inc(p["ch2"], 1)

                    def ch3(b, par, ub):
                        dve.wait_ge(p["col"], b + (past(L) + 1))
                        v.tensor_copy(cl[0:R, 0:2], m1[0:R, 256:258])
                        dve.drain()
                        v.scalar_tensor_tensor(m2[0:R, :], mk[0:R, par, 129:257], cl[0:R, 0:1], mx[0:R, :],
                                               ALU.add, ALU.max)
                        dve.drain()
                        v.scalar_tensor_tensor(m2[0:R, :], mk[0:R, par, 257:385], cl[0:R, 1:2], m2[0:R, :],
                                               ALU.add, ALU.max)
                        dve.drain()
                        tt(cl[0:R, 2:3], cl[0:R, 0:1], m2[0:R, 0:1], ALU.subtract)
                        dve.drain()
                        tt(dd[0:R, :], m0[0:R, 0:128], m2[0:R, :], ALU.subtract)
                        dve.drain()
                        if L > 1:
                            tt(dd[0:R, :], dd[0:R, :], mk[0:R, par, 385:513], ALU.add)
                            dve.drain()
                        dve.sem_inc(p["ch3"], 1)

                    def weigh(rset, par, k):
                        ins = one_hot(rel_s[:, par, k:k + 1], k, None)
                        if H > 1:
                            o = 256 if L == 1 else 0
                            vv = rg[:, rset * G + k, o:o + 256].rearrange("p (h d) -> p h d", h=H)
                            wv = w8[:, par, k, 0, 0:H].unsqueeze(2).to_broadcast([128, H, 256 // H])
                            ins = tt(vv, vv, wv, ALU.mult)
                        ins.then_inc(p["wready"], 1)

                    steps = (10, 12, 14) if L == 1 else (3, 7, 11)
                    keep_rel(0, 2)
                    keep_rel(1, 3)
                    dve.drain()
                    for k in range(G):
                        hot_to_turn(0, 0, k)

                    def batch(i, o, scores, sums):
                        b, rset, use, par, ub = batch_at(L, i, o)
                        c, cset, _, cp, _ = batch_at(L, i, o - 1)
                        feed = scores and (not isinstance(b, int) or b + 1 < NB)
                        if sums:
                            base = dve.value_load(base_r[0:1, ds(c * G, 1)], min_val=0, max_val=N)
                        if scores and L > 1:
                            scores_of(b, rset, use, par)
                        if sums:
                            dve.wait_ge(p["w"], c + (past(L) + 3))
                            colv = acc[:, 0:3, ds(base, 1)]
                            dve.wait_ge(p["added"], c * G + (2 + T * L))
                            tt(colv, colv, corr[:, cp, 0:3].unsqueeze(2), ALU.mult)
                            part = lambda s: w8[:, cp, :, s, :]
                            tt(part(1), part(0), upper(part(0)), ALU.subtract)
                            dve.drain()
                            tt(part(2), part(1), upper(part(1)), ALU.subtract)
                            for k in range(LEAD):
                                weigh(cset, cp, k)
                        for k in range(G):
                            if scores and L == 1 and k < 8:
                                products(b, rset, use, par, k)
                            if scores and L == 1 and k == 8:
                                reduce(b, par, 7)
                                dve.drain()
                                dve.sem_inc(p["s"], 1)
                            t0 = 2 * k - (16 if L == 1 else 0)
                            if feed and 0 <= t0 < G:
                                hot_to_turn(b + 1, (o + 1) % 2, t0)
                                hot_to_turn(b + 1, (o + 1) % 2, t0 + 1)
                            if sums:
                                if k + LEAD < G:
                                    weigh(cset, cp, k + LEAD)
                                add_window(c, k)
                            if scores and k == 10:
                                keep_rel(b, par)
                                if not isinstance(b, int) or b + 2 < NB:
                                    keep_rel(b + 2, 2 + par)
                            if scores and k in steps:
                                (ch1, ch2, ch3)[steps.index(k)](b, par, ub)
                    softmax_batches(dve, L, batch)
                barrier(dve)
                q = NODE[L]
                if L == 0:
                    dve.wait_ge(q["wl"], 16 * 16)
                    for j in range(8):
                        kc, pp = j // 4, 32 * (j % 4)
                        for i8 in range(8):
                            c = OCT_IDX[i8][j]
                            v.tensor_scalar(wout[pp:pp + 32, kc, 32 * i8:32 * i8 + 32],
                                            wraw[pp:pp + 32, 6 + kc, 32 * c:32 * c + 32],
                                            float(OCT_SIGN[i8][j]), None, ALU.mult)
                    dve.drain()
                    dve.sem_inc(q["w"], 1)
                if L in (1, 2):
                    dve.wait_ge(q["wl"], 16 * {1: 5, 2: 6}[L])
                    Hn = HEADS[L + 1]
                    for kc in range(2):
                        for s_, av in ((0, as_b), (1, ad_b)):
                            tt(wtmp[:, :], wproj[:, kc, 0:256], av[:, :], ALU.mult)
                            dve.drain()
                            v.tensor_reduce(wproj[:, kc, 256 + Hn * s_:256 + Hn * s_ + Hn],
                                            wtmp[:, :].rearrange("p (h d) -> p h d", h=Hn), AX.X, ALU.add)
                            dve.drain()
                    dve.sem_inc(q["w"], 1)
                if L == 3:
                    dve.wait_ge(q["wl"], 32)
                    v.tensor_scalar(dcol[:, :], dcol[:, :], 1.0, None, ALU.add)
                    dve.drain()
                    v.tensor_scalar(rr[:, 0, 0:NT], dcol[:, :], 1.0, None, ALU.max).then_inc(s_sq, 1)
                    v.tensor_scalar(dcol[:, :], dcol[:, :], 0.0, None, ALU.is_gt)
                    dve.wait_ge(s_sqd, 2)
                    v.reciprocal(rr[:, 1, 0:NT], rr[:, 0, 0:NT])
                    dve.drain()
                    tt(dcol[:, :], dcol[:, :], rr[:, 1, 0:NT], ALU.mult)
                    dve.drain()
                    dve.sem_inc(q["w"], 1)
                if L in (0, 4):
                    if L == 4:
                        dve.wait_ge(q["wl"], 16 * 5)

                    def measure(c, par):
                        if L == 4:
                            dve.wait_ge(q["chd"], c + 1)
                        else:
                            dve.wait_ge(q["ch"], c + 3)
                        zv = qe[par][:, 0:2 * CH].rearrange("p (k n) -> p k n", k=2)
                        if L == 4:
                            dst_v = acc[:, 0:2, ds(c * CH, CH)]
                            tt(dst_v, zv, dinv_b[:, ds(c * CH, CH)].unsqueeze(1).to_broadcast([128, 2, CH]), ALU.mult)
                            dve.drain()
                            dve.sem_inc(q["ch"], 1)
                            for k in range(2):
                                v.tensor_scalar(acc[:, k, ds(c * CH, CH)], acc[:, k, ds(c * CH, CH)],
                                                cols[:, k, 2:3], None, ALU.add)
                            dve.drain()
                            for k in range(2):
                                v.bn_stats(stats[:, k, ds(c * 6, 6)], acc[:, k, ds(c * CH, CH)])
                        else:
                            for k in range(2):
                                v.bn_stats(stats[:, k, ds(c * 6, 6)], acc[:, k, ds(c * CH, CH)])
                    with dve.Fori(0, NCH // 2) as i:
                        measure(i * 2, 0)
                        measure(i * 2 + 1, 1)
                    measure(NCH - 1, 0)
                    dve.drain()
                    for k in range(2):
                        v.bn_aggr(bn[:, k, 0:2], stats[:, k, :])
                    dve.drain()
                    v.tensor_scalar(bn[:, :, 1], bn[:, :, 1], EPS, None, ALU.add).then_inc(s_sq, 1)
                    dve.wait_ge(s_sqd, 1 if L == 0 else 3)
                    v.reciprocal(bn[:, :, 1], bn[:, :, 1])
                    dve.drain()
                    for k in range(2):
                        tt(bn[:, k, 2:3], bn[:, k, 1:2], cols[:, k, 0:1], ALU.mult)
                    dve.drain()
                    for k in range(2):
                        tt(bn[:, k, 0:1], bn[:, k, 0:1], bn[:, k, 2:3], ALU.mult)
                    dve.drain()
                    for k in range(2):
                        tt(bn[:, k, 3:4], cols[:, k, 1:2], bn[:, k, 0:1], ALU.subtract)
                    dve.drain()
                    dve.sem_inc(q["w"], 1)
                if L in (1, 2, 3):
                    den = acc[0:H, 2, :]
                    for m in range(DEN):
                        dve.wait_ge(q["den"], m + 1)
                        n = min(512, NP - 512 * m)
                        v.tensor_scalar(den[:, 512 * m:512 * m + n], qe[m % 2][0:H, 0:n], 0.5, None, ALU.max)\
                            .then_inc(q["clr"], 1)
                    dve.drain()
                    v.reciprocal(den, den)
                    dve.drain()
                    dve.sem_inc(q["clr"], 1)

                def stages(i, off):
                    ok, n, par, use = tile_of(i, off, 0)
                    if ok and L in (1, 2, 3):
                        dve.wait_ge(q["den"], n + (DEN + 1))
                        dn = ag[par][:, 0:256].rearrange("p (k j) -> p k j", k=2)
                        dve.wait_ge(q["y"], n + 1)
                        tt(pre[:, par, :].rearrange("p (k j) -> p k j", k=2), acc[:, 0:2, ds(n * 128, 128)], dn,
                           ALU.mult).then_inc(q["pre"], 1)
                    ok, n, par, use = tile_of(i, off, 1)
                    if ok:
                        dve.wait_ge(q["y"], n + 3)
                        wait(dve, q["xn"], n - 1)
                        if L in (1, 2, 3):
                            tt(rr[:, par, :], ot[par][:, 0:256], bo_b[:, :], ALU.add)
                            dve.drain()
                        if L != 2:
                            dve.wait_ge(q[f"xr{par}"], use * 16 + 16)
                            v.scalar_tensor_tensor(rr[:, par, :], xr[:, par, :], 2.0 if L == 4 else 1.0,
                                                   rr[:, par, :] if L in (1, 3) else ot[par][:, 0:256],
                                                   ALU.mult, ALU.add)
                            dve.drain()
                        v.bn_stats(lnst[:, par, 0:6], rr[:, par, :])
                        dve.drain()
                        v.bn_aggr(lnst[:, par, 6:8], lnst[:, par, 0:6])
                        dve.drain()
                        v.tensor_scalar(lnst[:, par, 8:9], lnst[:, par, 7:8], EPS, None, ALU.add)\
                            .then_inc(q["var"], 1)
                    ok, n, par, use = tile_of(i, off, 2)
                    if ok:
                        dve.wait_ge(q["std"], n + 1)
                        v.reciprocal(lnst[:, par, 10:11], lnst[:, par, 9:10])
                        if L != 2:
                            wait(dve, q[f"st{par}"], use * 16)
                        if L < 4:
                            wait(dve, q["xt"], n - 1)
                        dve.nop(nofuse=True)
                        dve.drain()
                        ins = v.tensor_scalar(xn[:, par, :], rr[:, par, :], lnst[:, par, 6:7], lnst[:, par, 10:11],
                                              ALU.subtract, ALU.mult)
                        if L == 2:
                            dve.drain()
                            tt(xn[:, par, :], xn[:, par, :], lg_b[:, :], ALU.mult)
                            dve.drain()
                            tt(xn[:, par, :], xn[:, par, :], lb_b[:, :], ALU.add)
                            dve.drain()
                            ins = v.tensor_scalar(xn[:, par, :], xn[:, par, :], 0.0, None, ALU.max)
                        if L == 3:
                            dve.drain()
                            wait(dve, q[f"ps{par}"], use * 16)
                            ins = v.tensor_scalar(xs[:, par, :], xn[:, par, :], dcol[:, ds(n, 1)], None, ALU.mult)
                        ins.then_inc(q["xn"], 1)
                if L == 3:
                    dve.wait_ge(s_deg, 32)
                dve.drain()
                pipeline(dve, stages)
                barrier(dve)


_INS = ["x", "src", "dst", "edge_weight", "L0_gnn_weight", "L0_gnn_gamma", "L0_gnn_beta",
        "L1_gnn_Wq", "L1_gnn_bq", "L1_gnn_Wk", "L1_gnn_bk", "L1_gnn_Wv", "L1_gnn_bv", "L1_gnn_Wo", "L1_gnn_bo",
        "L2_gnn_W1", "L2_gnn_a1_src", "L2_gnn_a1_dst", "L2_gnn_b1", "L2_gnn_ln_g", "L2_gnn_ln_b", "L2_gnn_W2",
        "L2_gnn_a2_src", "L2_gnn_a2_dst", "L2_gnn_b2", "L3_gnn_W", "L3_gnn_b", "L3_gnn_gamma", "L3_gnn_beta"]


def kernel(**inputs):
    import numpy as _np
    import concourse.bacc as _bacc
    from concourse.bass_utils import run_bass_kernel_spmd as _run

    nc = _bacc.Bacc("TRN2", target_bir_lowering=False, num_devices=1)
    arrays, args = {}, {}
    for name in _INS:
        arr = _np.ascontiguousarray(inputs[name])
        arrays[f"in_{name}"] = arr
        args[name] = nc.dram_tensor(f"in_{name}", arr.shape, mybir.dt.from_np(arr.dtype), kind="ExternalInput").ap()
    out = nc.dram_tensor("out_0", (N, D), F32, kind="ExternalOutput").ap()
    gnn_kernel(nc, args, out)
    r = _run(nc, [arrays], core_ids=[0])
    return r.results[0]["out_0"]
```
